# Optimizing a Trainium2 kernel written in Bass

```python
import numpy as np
import jax
import jax.numpy as jnp

def _softmax(x, axis=-1):
    return jax.nn.softmax(x, axis=axis)

def _gelu(x):
    return jax.nn.gelu(x, approximate=True)

def _silu(x):
    return jax.nn.silu(x)

def _sigmoid(x):
    return jax.nn.sigmoid(x)

def _layernorm(x, axis=-1, eps=1e-05):
    m = jnp.mean(x, axis=axis, keepdims=True)
    v = jnp.var(x, axis=axis, keepdims=True)
    return (x - m) / jnp.sqrt(v + eps)

def _scatter_add(tgt, idx, src, axis=0):
    return tgt.at[idx].add(src)

def _segment_sum(src, seg, n):
    return jax.ops.segment_sum(src, seg, n)
kernel_name = 'mk_cond_seq_d4_seqx_r8_c0a093'

def setup_inputs(seed: int=0):
    np.random.seed(seed)
    _w = jnp.asarray

    def _rec_inputs():
        import jax
        import jax.numpy as jnp
        _rk = jax.random.key(seed)
        x = -0.0002928 + 1 * jax.random.normal(jax.random.fold_in(_rk, 1), (8, 256, 128), jnp.float32)
        _lenS = 256 - jax.random.randint(jax.random.fold_in(_rk, 7), (8,), 0, max(1, 256 // 4) + 1, jnp.int32)
        _lenS2 = 256 - jax.random.randint(jax.random.fold_in(_rk, 8), (8,), 0, max(1, 256 // 4) + 1, jnp.int32)
        itok_B_6_14 = jax.random.randint(jax.random.fold_in(_rk, 11), (8,), 6, 15, jnp.int32)
        condB_theta = jax.random.uniform(jax.random.fold_in(_rk, 12), (8,), jnp.float32, 0.0, 0.983423)
        condB_phi = jax.random.uniform(jax.random.fold_in(_rk, 13), (8,), jnp.float32, 0.0, 0.961312)
        itok_B_0_7 = jax.random.randint(jax.random.fold_in(_rk, 14), (8,), 0, 8, jnp.int32)
        condB_gatescore = jax.random.uniform(jax.random.fold_in(_rk, 15), (8,), jnp.float32, 0.0, 0.581427)
        return (x, itok_B_6_14, condB_theta, condB_phi, itok_B_0_7, condB_gatescore)
    x, itok_B_6_14, condB_theta, condB_phi, itok_B_0_7, condB_gatescore = _rec_inputs()

    def _L0_cond_setup():
        import jax, jax.numpy as jnp
        import numpy as np
        D = 128
        E = 8
        FF = 512
        TOPK = 2
        S = 32
        SE = 64
        SH = 128
        B, T = (2, 256)

        def _forward(x, subject_ids, ln_g, ln_b, subj_emb, hyp_w1, hyp_b1, hyp_w2, hyp_b2, sty_w1, sty_b1, sty_w2, sty_b2, router_w, exp_w1, exp_b1, exp_w2, exp_b2):
            mu = x.mean(-1, keepdims=True)
            var = x.var(-1, keepdims=True)
            h = (x - mu) * jax.lax.rsqrt(var + 1e-05) * ln_g + ln_b
            m_t = h.mean(1, keepdims=True)
            v_t = h.var(1, keepdims=True)
            h_norm = (h - m_t) * jax.lax.rsqrt(v_t + 1e-08)
            se = subj_emb[subject_ids]
            hyp = jax.nn.relu(se @ hyp_w1 + hyp_b1) @ hyp_w2 + hyp_b2
            sty = jax.nn.relu(hyp @ sty_w1 + sty_b1) @ sty_w2 + sty_b2
            gamma, beta = jnp.split(sty, 2, axis=-1)
            gamma = jax.nn.softplus(gamma) + 1e-08
            h = h_norm * gamma[:, None, :] + beta[:, None, :]
            h_flat = h.reshape(-1, D)
            probs = jax.nn.softmax(h_flat @ router_w, axis=-1)
            gates, idx = jax.lax.top_k(probs, TOPK)
            gates = gates / gates.sum(-1, keepdims=True)
            N = h_flat.shape[0]
            combine = jnp.zeros((N, E), h_flat.dtype).at[jnp.arange(N)[:, None], idx].add(gates)
            hid = jax.nn.relu(jnp.einsum('nd,edf->nef', h_flat, exp_w1) + exp_b1)
            eout = jnp.einsum('nef,efd->ned', hid, exp_w2) + exp_b2
            y = jnp.einsum('ned,ne->nd', eout, combine)
            return x + y.reshape(x.shape)
        key = jax.random.key(seed)
        ks = jax.random.split(key, 16)
        n = lambda k, sh, s=0.02: jax.random.normal(k, sh, dtype=jnp.float32) * s
        return {'x': jax.random.normal(ks[0], (B, T, D), dtype=jnp.float32), 'subject_ids': jax.random.randint(ks[1], (B,), 0, S), 'ln_g': jnp.ones((D,), jnp.float32), 'ln_b': jnp.zeros((D,), jnp.float32), 'subj_emb': n(ks[2], (S, SE)), 'hyp_w1': n(ks[3], (SE, SH), 1.0 / np.sqrt(SE)), 'hyp_b1': jnp.zeros((SH,), jnp.float32), 'hyp_w2': n(ks[4], (SH, SH), 1.0 / np.sqrt(SH)), 'hyp_b2': jnp.zeros((SH,), jnp.float32), 'sty_w1': n(ks[5], (SH, SH // 2), 1.0 / np.sqrt(SH)), 'sty_b1': jnp.zeros((SH // 2,), jnp.float32), 'sty_w2': n(ks[6], (SH // 2, 2 * D), 1.0 / np.sqrt(SH // 2)), 'sty_b2': jnp.zeros((2 * D,), jnp.float32), 'router_w': n(ks[7], (D, E), 1.0 / np.sqrt(D)), 'exp_w1': n(ks[8], (E, D, FF), 1.0 / np.sqrt(D)), 'exp_b1': jnp.zeros((E, FF), jnp.float32), 'exp_w2': n(ks[9], (E, FF, D), 1.0 / np.sqrt(FF)), 'exp_b2': jnp.zeros((E, D), jnp.float32)}
    _L0_cond_all = _L0_cond_setup()
    _L0_cond_in = {k: v for k, v in _L0_cond_all.items() if k in ('ln_g', 'ln_b', 'subj_emb', 'hyp_w1', 'hyp_b1', 'hyp_w2', 'hyp_b2', 'sty_w1', 'sty_b1', 'sty_w2', 'sty_b2', 'router_w', 'exp_w1', 'exp_b1', 'exp_w2', 'exp_b2')}
    del _L0_cond_all

    def _L1_cond_setup():
        import jax, jax.numpy as jnp
        import numpy as np
        key = jax.random.key(seed)
        k1, k2, k3 = jax.random.split(key, 3)
        B, N, D = (16, 512, 128)
        embeddings = jax.random.normal(k1, (B, N, D), dtype=jnp.float32)
        theta = jax.random.uniform(k2, (B,), dtype=jnp.float32)
        phi = jax.random.uniform(k3, (B,), dtype=jnp.float32)
        return {'embeddings': embeddings, 'theta': theta, 'phi': phi}
    _L1_cond_all = _L1_cond_setup()
    _L1_cond_in = {k: v for k, v in _L1_cond_all.items() if k in ()}
    del _L1_cond_all

    def _L2_cond_setup():
        import jax, jax.numpy as jnp
        import numpy as np
        E, H, I = (8, 128, 512)
        B, S = (4, 128)
        LN_EPS = 1e-12
        key = jax.random.key(seed)
        ks = jax.random.split(key, 8)
        x = jax.random.normal(ks[0], (B, S, H), dtype=jnp.float32)
        expert_idx = jax.random.randint(ks[1], (B,), 0, E, dtype=jnp.int64)
        Wi = jax.random.normal(ks[2], (E, H, I), dtype=jnp.float32) * 0.02
        bi = jnp.zeros((E, I), dtype=jnp.float32)
        Wo = jax.random.normal(ks[3], (E, I, H), dtype=jnp.float32) * 0.02
        bo = jnp.zeros((E, H), dtype=jnp.float32)
        gamma = jnp.ones((E, H), dtype=jnp.float32)
        beta = jnp.zeros((E, H), dtype=jnp.float32)
        return {'input_tensor': x, 'expert_idx': expert_idx, 'Wi': Wi, 'bi': bi, 'Wo': Wo, 'bo': bo, 'gamma': gamma, 'beta': beta}
    _L2_cond_all = _L2_cond_setup()
    _L2_cond_in = {k: v for k, v in _L2_cond_all.items() if k in ('Wi', 'bi', 'Wo', 'bo', 'gamma', 'beta')}
    del _L2_cond_all

    def _L3_cond_setup():
        import jax, jax.numpy as jnp
        import numpy as np
        D_MODEL = 128
        N_HEADS = 16
        D_HEAD = D_MODEL // N_HEADS
        D_FF = 512
        EPS = 1e-05

        def layernorm(x, gamma, beta):
            mu = jnp.mean(x, axis=-1, keepdims=True)
            var = jnp.var(x, axis=-1, keepdims=True)
            return (x - mu) * jax.lax.rsqrt(var + EPS) * gamma + beta
        key = jax.random.key(seed)
        ks = jax.random.split(key, 16)
        B, T = (4, 256)
        s = 1.0 / np.sqrt(D_MODEL)
        sf = 1.0 / np.sqrt(D_FF)
        return {'x': jax.random.normal(ks[0], (B, T, D_MODEL), jnp.float32), 'gate_score': jax.random.uniform(ks[1], (B,), jnp.float32), 'Wq': jax.random.normal(ks[2], (D_MODEL, D_MODEL), jnp.float32) * s, 'bq': jnp.zeros((D_MODEL,), jnp.float32), 'Wk': jax.random.normal(ks[3], (D_MODEL, D_MODEL), jnp.float32) * s, 'bk': jnp.zeros((D_MODEL,), jnp.float32), 'Wv': jax.random.normal(ks[4], (D_MODEL, D_MODEL), jnp.float32) * s, 'bv': jnp.zeros((D_MODEL,), jnp.float32), 'Wo': jax.random.normal(ks[5], (D_MODEL, D_MODEL), jnp.float32) * s, 'bo': jnp.zeros((D_MODEL,), jnp.float32), 'W1': jax.random.normal(ks[6], (D_MODEL, D_FF), jnp.float32) * s, 'b1': jnp.zeros((D_FF,), jnp.float32), 'W2': jax.random.normal(ks[7], (D_FF, D_MODEL), jnp.float32) * sf, 'b2': jnp.zeros((D_MODEL,), jnp.float32), 'gamma1': jnp.ones((D_MODEL,), jnp.float32), 'beta1': jnp.zeros((D_MODEL,), jnp.float32), 'gamma2': jnp.ones((D_MODEL,), jnp.float32), 'beta2': jnp.zeros((D_MODEL,), jnp.float32)}
    _L3_cond_all = _L3_cond_setup()
    _L3_cond_in = {k: v for k, v in _L3_cond_all.items() if k in ('Wq', 'bq', 'Wk', 'bk', 'Wv', 'bv', 'Wo', 'bo', 'W1', 'b1', 'W2', 'b2', 'gamma1', 'beta1', 'gamma2', 'beta2')}
    del _L3_cond_all
    return {'x': x, 'itok_B_6_14': itok_B_6_14, 'condB_theta': condB_theta, 'condB_phi': condB_phi, 'itok_B_0_7': itok_B_0_7, 'condB_gatescore': condB_gatescore, 'L0_cond_ln_g': _L0_cond_in['ln_g'], 'L0_cond_ln_b': _L0_cond_in['ln_b'], 'L0_cond_subj_emb': _L0_cond_in['subj_emb'], 'L0_cond_hyp_w1': _L0_cond_in['hyp_w1'], 'L0_cond_hyp_b1': _L0_cond_in['hyp_b1'], 'L0_cond_hyp_w2': _L0_cond_in['hyp_w2'], 'L0_cond_hyp_b2': _L0_cond_in['hyp_b2'], 'L0_cond_sty_w1': _L0_cond_in['sty_w1'], 'L0_cond_sty_b1': _L0_cond_in['sty_b1'], 'L0_cond_sty_w2': _L0_cond_in['sty_w2'], 'L0_cond_sty_b2': _L0_cond_in['sty_b2'], 'L0_cond_router_w': _L0_cond_in['router_w'], 'L0_cond_exp_w1': _L0_cond_in['exp_w1'], 'L0_cond_exp_b1': _L0_cond_in['exp_b1'], 'L0_cond_exp_w2': _L0_cond_in['exp_w2'], 'L0_cond_exp_b2': _L0_cond_in['exp_b2'], 'L2_cond_Wi': _L2_cond_in['Wi'], 'L2_cond_bi': _L2_cond_in['bi'], 'L2_cond_Wo': _L2_cond_in['Wo'], 'L2_cond_bo': _L2_cond_in['bo'], 'L2_cond_gamma': _L2_cond_in['gamma'], 'L2_cond_beta': _L2_cond_in['beta'], 'L3_cond_Wq': _L3_cond_in['Wq'], 'L3_cond_bq': _L3_cond_in['bq'], 'L3_cond_Wk': _L3_cond_in['Wk'], 'L3_cond_bk': _L3_cond_in['bk'], 'L3_cond_Wv': _L3_cond_in['Wv'], 'L3_cond_bv': _L3_cond_in['bv'], 'L3_cond_Wo': _L3_cond_in['Wo'], 'L3_cond_bo': _L3_cond_in['bo'], 'L3_cond_W1': _L3_cond_in['W1'], 'L3_cond_b1': _L3_cond_in['b1'], 'L3_cond_W2': _L3_cond_in['W2'], 'L3_cond_b2': _L3_cond_in['b2'], 'L3_cond_gamma1': _L3_cond_in['gamma1'], 'L3_cond_beta1': _L3_cond_in['beta1'], 'L3_cond_gamma2': _L3_cond_in['gamma2'], 'L3_cond_beta2': _L3_cond_in['beta2']}

def reference(x, itok_B_6_14, condB_theta, condB_phi, itok_B_0_7, condB_gatescore, L0_cond_ln_g, L0_cond_ln_b, L0_cond_subj_emb, L0_cond_hyp_w1, L0_cond_hyp_b1, L0_cond_hyp_w2, L0_cond_hyp_b2, L0_cond_sty_w1, L0_cond_sty_b1, L0_cond_sty_w2, L0_cond_sty_b2, L0_cond_router_w, L0_cond_exp_w1, L0_cond_exp_b1, L0_cond_exp_w2, L0_cond_exp_b2, L2_cond_Wi, L2_cond_bi, L2_cond_Wo, L2_cond_bo, L2_cond_gamma, L2_cond_beta, L3_cond_Wq, L3_cond_bq, L3_cond_Wk, L3_cond_bk, L3_cond_Wv, L3_cond_bv, L3_cond_Wo, L3_cond_bo, L3_cond_W1, L3_cond_b1, L3_cond_W2, L3_cond_b2, L3_cond_gamma1, L3_cond_beta1, L3_cond_gamma2, L3_cond_beta2):
    import jax
    import jax.numpy as jnp

    def _L0_cond_ref(x, subject_ids, ln_g, ln_b, subj_emb, hyp_w1, hyp_b1, hyp_w2, hyp_b2, sty_w1, sty_b1, sty_w2, sty_b2, router_w, exp_w1, exp_b1, exp_w2, exp_b2):
        import jax, jax.numpy as jnp
        import numpy as np
        D = 128
        E = 8
        FF = 512
        TOPK = 2
        S = 32
        SE = 64
        SH = 128
        B, T = (2, 256)

        def _forward(x, subject_ids, ln_g, ln_b, subj_emb, hyp_w1, hyp_b1, hyp_w2, hyp_b2, sty_w1, sty_b1, sty_w2, sty_b2, router_w, exp_w1, exp_b1, exp_w2, exp_b2):
            mu = x.mean(-1, keepdims=True)
            var = x.var(-1, keepdims=True)
            h = (x - mu) * jax.lax.rsqrt(var + 1e-05) * ln_g + ln_b
            m_t = h.mean(1, keepdims=True)
            v_t = h.var(1, keepdims=True)
            h_norm = (h - m_t) * jax.lax.rsqrt(v_t + 1e-08)
            se = subj_emb[subject_ids]
            hyp = jax.nn.relu(se @ hyp_w1 + hyp_b1) @ hyp_w2 + hyp_b2
            sty = jax.nn.relu(hyp @ sty_w1 + sty_b1) @ sty_w2 + sty_b2
            gamma, beta = jnp.split(sty, 2, axis=-1)
            gamma = jax.nn.softplus(gamma) + 1e-08
            h = h_norm * gamma[:, None, :] + beta[:, None, :]
            h_flat = h.reshape(-1, D)
            probs = jax.nn.softmax(h_flat @ router_w, axis=-1)
            gates, idx = jax.lax.top_k(probs, TOPK)
            gates = gates / gates.sum(-1, keepdims=True)
            N = h_flat.shape[0]
            combine = jnp.zeros((N, E), h_flat.dtype).at[jnp.arange(N)[:, None], idx].add(gates)
            hid = jax.nn.relu(jnp.einsum('nd,edf->nef', h_flat, exp_w1) + exp_b1)
            eout = jnp.einsum('nef,efd->ned', hid, exp_w2) + exp_b2
            y = jnp.einsum('ned,ne->nd', eout, combine)
            return x + y.reshape(x.shape)
        return _forward(x, subject_ids, ln_g, ln_b, subj_emb, hyp_w1, hyp_b1, hyp_w2, hyp_b2, sty_w1, sty_b1, sty_w2, sty_b2, router_w, exp_w1, exp_b1, exp_w2, exp_b2)

    def _L1_cond_ref(embeddings, theta, phi):
        import jax, jax.numpy as jnp
        import numpy as np
        B, N, D = embeddings.shape
        e = embeddings.reshape(B, N, D // 4, 4)
        ct = jnp.cos(theta)[:, None, None]
        st = jnp.sin(theta)[:, None, None]
        cp = jnp.cos(phi)[:, None, None]
        sp = jnp.sin(phi)[:, None, None]
        x0, x1, x2, x3 = (e[..., 0], e[..., 1], e[..., 2], e[..., 3])
        out = jnp.stack([x0 * ct + x1 * st, -x0 * st + x1 * ct, x2 * cp + x3 * sp, -x2 * sp + x3 * cp], axis=-1)
        return out.reshape(B, N, D)

    def _L2_cond_ref(input_tensor, expert_idx, Wi, bi, Wo, bo, gamma, beta):
        import jax, jax.numpy as jnp
        import numpy as np
        E, H, I = (8, 128, 512)
        B, S = (4, 128)
        LN_EPS = 1e-12
        Wi_b = Wi[expert_idx]
        bi_b = bi[expert_idx]
        Wo_b = Wo[expert_idx]
        bo_b = bo[expert_idx]
        g_b = gamma[expert_idx]
        be_b = beta[expert_idx]
        h = jax.nn.gelu(jnp.einsum('bsh,bhi->bsi', input_tensor, Wi_b) + bi_b[:, None, :], approximate=False)
        o = jnp.einsum('bsi,bih->bsh', h, Wo_b) + bo_b[:, None, :]
        r = o + input_tensor
        mu = jnp.mean(r, axis=-1, keepdims=True)
        var = jnp.mean(jnp.square(r - mu), axis=-1, keepdims=True)
        y = (r - mu) * jax.lax.rsqrt(var + LN_EPS)
        return y * g_b[:, None, :] + be_b[:, None, :]

    def _L3_cond_ref(x, gate_score, Wq, bq, Wk, bk, Wv, bv, Wo, bo, W1, b1, W2, b2, gamma1, beta1, gamma2, beta2):
        import jax, jax.numpy as jnp
        import numpy as np
        D_MODEL = 128
        N_HEADS = 16
        D_HEAD = D_MODEL // N_HEADS
        D_FF = 512
        EPS = 1e-05

        def layernorm(x, gamma, beta):
            mu = jnp.mean(x, axis=-1, keepdims=True)
            var = jnp.var(x, axis=-1, keepdims=True)
            return (x - mu) * jax.lax.rsqrt(var + EPS) * gamma + beta
        B, T, C = x.shape
        h = layernorm(x, gamma1, beta1)
        Q = (h @ Wq + bq).reshape(B, T, N_HEADS, D_HEAD).transpose(0, 2, 1, 3)
        K = (h @ Wk + bk).reshape(B, T, N_HEADS, D_HEAD).transpose(0, 2, 1, 3)
        V = (h @ Wv + bv).reshape(B, T, N_HEADS, D_HEAD).transpose(0, 2, 1, 3)
        scores = jnp.einsum('bhqd,bhkd->bhqk', Q, K) / np.sqrt(D_HEAD)
        causal = jnp.tril(jnp.ones((T, T), dtype=bool))
        scores = jnp.where(causal, scores, -jnp.inf)
        attn = jax.nn.softmax(scores, axis=-1)
        ctx = jnp.einsum('bhqk,bhkd->bhqd', attn, V)
        ctx = ctx.transpose(0, 2, 1, 3).reshape(B, T, C)
        attn_out = ctx @ Wo + bo
        x1 = x + attn_out
        h2 = layernorm(x1, gamma2, beta2)
        ff = jax.nn.gelu(h2 @ W1 + b1, approximate=False) @ W2 + b2
        x2 = x1 + ff
        g = gate_score[:, None, None]
        return x + g * (x2 - x)
    x = _L0_cond_ref(x, itok_B_6_14, L0_cond_ln_g, L0_cond_ln_b, L0_cond_subj_emb, L0_cond_hyp_w1, L0_cond_hyp_b1, L0_cond_hyp_w2, L0_cond_hyp_b2, L0_cond_sty_w1, L0_cond_sty_b1, L0_cond_sty_w2, L0_cond_sty_b2, L0_cond_router_w, L0_cond_exp_w1, L0_cond_exp_b1, L0_cond_exp_w2, L0_cond_exp_b2)
    x = _L1_cond_ref(x, condB_theta, condB_phi)
    x = _L2_cond_ref(x, itok_B_0_7, L2_cond_Wi, L2_cond_bi, L2_cond_Wo, L2_cond_bo, L2_cond_gamma, L2_cond_beta)
    x = _L3_cond_ref(x, condB_gatescore, L3_cond_Wq, L3_cond_bq, L3_cond_Wk, L3_cond_bk, L3_cond_Wv, L3_cond_bv, L3_cond_Wo, L3_cond_bo, L3_cond_W1, L3_cond_b1, L3_cond_W2, L3_cond_b2, L3_cond_gamma1, L3_cond_beta1, L3_cond_gamma2, L3_cond_beta2)
    return x

_drawn_inputs = setup_inputs


def setup_inputs(seed=0):
    import zlib

    import numpy as np

    out = dict(_drawn_inputs(seed))
    spreads = {'L0_cond_ln_g': (1.0, 0.6),
     'L0_cond_ln_b': (0.0, 0.8),
     'L0_cond_hyp_b1': (0.0, 0.1),
     'L0_cond_hyp_b2': (0.0, 0.1),
     'L0_cond_sty_b1': (0.0, 0.1),
     'L0_cond_sty_b2': (0.0, 0.1),
     'L0_cond_exp_b1': (0.0, 0.1),
     'L0_cond_exp_b2': (0.0, 0.1),
     'L2_cond_bi': (0.0, 0.339),
     'L2_cond_bo': (0.0, 0.1),
     'L2_cond_gamma': (1.0, 0.2),
     'L2_cond_beta': (0.0, 0.1),
     'L3_cond_bq': (0.0, 0.8),
     'L3_cond_bk': (0.0, 0.8),
     'L3_cond_bv': (0.0, 0.1),
     'L3_cond_bo': (0.0, 0.1),
     'L3_cond_b1': (0.0, 0.369),
     'L3_cond_b2': (0.0, 0.1),
     'L3_cond_gamma1': (1.0, 0.2),
     'L3_cond_beta1': (0.0, 0.1),
     'L3_cond_gamma2': (1.0, 0.2),
     'L3_cond_beta2': (0.0, 0.343)}
    factors = {}
    for name, (base, spread) in spreads.items():
        noise = np.random.default_rng([zlib.crc32(name.encode()), seed]).standard_normal(out[name].shape)
        drawn = base * np.exp(spread * noise) if base else spread * noise
        out[name] = jnp.asarray(drawn.astype(out[name].dtype))
    for name, factor in factors.items():
        out[name] = (out[name] * factor).astype(out[name].dtype)
    return out
```

```python
from contextlib import ExitStack

import concourse.bass as bass
from concourse import mybir

F32 = mybir.dt.float32
F32R = mybir.dt.float32r
BF16 = mybir.dt.bfloat16
I32 = mybir.dt.int32
ALU = mybir.AluOpType
ACT = mybir.ActivationFunctionType
AX_X = mybir.AxisListType.X

P = 128
D = 128
SEQS, T = 8, 256
TILES = SEQS * T // P
BLOCKS, BT = 4, 512
BTILES = BT // P
E, FF = 8, 512
FC = FF // P
CHUNKS = E * FC
HEADS, DH = 16, 8
SLOT = 32
GROUP = P // SLOT
PAIRS = HEADS // 2
LAG = 4
SUBJECTS, SE = 32, 64
MASKED = -1e30
PI = 3.141592653589793

ROWS = ["b1"] * (E * FC) + ["b2"] * E + ["ln_g", "ln_b"] + ["ffn_b1"] * FC + \
       ["hyp_b1", "hyp_b2", "sty_b2", "sty_b2", "gamma1", "beta1", "gamma2", "beta2"]
COL = {name: ROWS.index(name) for name in ROWS}
NROWS = len(ROWS)


class Chain:

    def __init__(self, eng, sem, name, wait):
        self.wait = wait
        self.eng, self.sem, self.name, self.base, self.n = eng, sem, name, 0, 0

    def step(self, ins):
        ins.then_inc(self.sem, 1)
        self.n += 1

    def settle(self):
        self.wait(self.eng, self.sem, self.base + self.n)

    def link(self, ins):
        self.step(ins)
        self.settle()

    def enter(self, base):
        self.base, self.n = base, 0


NORM = {"stats": 1, "rstd": 2, "normed": 4, "nT": 6, "hT": 7, "tstats": 8, "tscale": 9, "h2": 11, "logits": 13,
        "shift": 14, "exp": 15, "gates": 17, "gT_ps": 22, "gT": 23}
COND_DVE = 5
STEPS_OF_TWO = {"pool": 10, "dve": 76}
OUT_CREDIT = 1


def conditioned_stack(nc, x, ids, angles, rows, sty_b1, subj, hyp_w, sty_w1, sty_w2, router, moe_w, mlp_w,
                      mlp_rows, mlp_bi, att_w, att_rows, out):
    with ExitStack() as ctx:
        def sb(name, shape, dt=F32):
            return ctx.enter_context(nc.sbuf_tensor(name, shape, dt))

        def sem(name):
            return ctx.enter_context(nc.semaphore(name))

        psA = ctx.enter_context(nc.psum_tensor("psA", [P, 2, 512], F32))
        psB = ctx.enter_context(nc.psum_tensor("psB", [P, 2, 512], F32))
        psC = ctx.enter_context(nc.psum_tensor("psC", [P, 2, 512], F32))
        psD = ctx.enter_context(nc.psum_tensor("psD", [P, 2, 512], F32))

        ident = sb("ident", [P, P])
        ident16 = sb("ident16", [P, P], BF16)
        mask_qk = sb("mask_qk", [P, 2 * P], BF16)
        mask_kq = sb("mask_kq", [P, 2 * P], BF16)
        pick = sb("pick", [3 * E, E, P], BF16)
        before = sb("before", [P, E, E])
        neghalf = sb("neghalf", [P, 8])
        rowno = sb("rowno", [P, 1])
        rowno_i = sb("rowno_i", [P, 1], I32)

        X = sb("X", [P, TILES, D])
        idrow = sb("idrow", [1, 16], I32)
        idall = sb("idall", [SUBJECTS, 16], I32)
        idf = sb("idf", [SUBJECTS, 16])
        ang = sb("ang", [P, 24])
        prow = sb("prow", [NROWS, P])
        pcol = sb("pcol", [P, NROWS])
        styb1 = sb("styb1", [SE, 1])
        subj_sb = sb("subj_sb", [SUBJECTS, SE])
        hyp1_sb = sb("hyp1_sb", [SE, P])
        hyp2_sb = sb("hyp2_sb", [P, P])
        sty1_sb = sb("sty1_sb", [P, SE])
        sty2_sb = sb("sty2_sb", [SE, 2 * D])
        router_sb = sb("router_sb", [D, E])
        bi_rows = sb("bi_rows", [E, FF])
        arow = sb("arow", [P, 640])
        watt = sb("watt", [P, 512])
        raw = sb("raw", [P, E, 1024])

        onehot = sb("onehot", [SUBJECTS, 8])
        onehot_x = sb("onehot_x", [E, 8])
        cond_a = sb("cond_a", [P, 8])
        cond_b = sb("cond_b", [P, 8])
        cond_c = sb("cond_c", [P, 8])
        cond_d = sb("cond_d", [P, 8])
        gam = sb("gam", [P, 8])
        bet = sb("bet", [P, 8])
        sp_t = sb("sp_t", [P, 6, 8])
        trig = sb("trig", [P, 6, 16])
        rot_c = sb("rot_c", [P, SEQS, 4])
        rot_s = sb("rot_s", [P, SEQS, 4])
        bi_col = sb("bi_col", [P, FC, SEQS])

        wh = sb("wh", [P, E, 1024], F32R)
        wl = sb("wl", [P, E, 1024], F32R)
        stats = sb("stats", [P, BTILES, 6])
        mv = sb("mv", [P, BTILES, 2])
        rstd = sb("rstd", [P, BTILES])
        nwork = sb("nwork", [P, 3 * BT])
        normed = nwork[:, 0:BT].rearrange("p (t d) -> p t d", t=BTILES)
        hT, h2 = nwork[:, BT:2 * BT], nwork[:, 2 * BT:3 * BT]
        tstats = sb("tstats", [P, 2, 6])
        tmv = sb("tmv", [P, 2, 2])
        tscale = sb("tscale", [P, 2])
        tshift = sb("tshift", [P, 2])
        tvar = sb("tvar", [P, 2])
        hh = sb("hh", [P, BLOCKS, BT], F32R)
        hl = sb("hl", [P, BLOCKS, BT], F32R)
        lmax = sb("lmax", [P, BTILES])
        probs = sb("probs", [P, BTILES, E])
        psums = sb("psums", [P, BTILES])
        above = sb("above", [P, BTILES, E, E])
        equal = sb("equal", [P, BTILES, E, E])
        rank = sb("rank", [P, BTILES, E])
        gates = sb("gates", [P, BTILES, E])
        gparts = sb("gparts", [P, BTILES, 3 * E], BF16)
        gT = sb("gT", [3 * E, BLOCKS, BT], BF16)
        hidh = sb("hidh", [P, 4, BT], F32R)
        hidl = sb("hidl", [P, 4, BT], F32R)
        work = sb("work", [P, 4096])
        hid = work[:, 0:2048].rearrange("p (n t) -> p n t", n=4)
        gb = work[:, 2048:3072].rearrange("p (n t) -> p n t", n=2)
        part = work[:, 3072:4096].rearrange("p (n t) -> p n t", n=2)
        ysum = sb("ysum", [P, BT])
        rot_t = sb("rot_t", [P, 2, 2, D])

        rawf = raw[:, :, :].rearrange("p e c -> p (e c)")
        wmlp = [rawf[:, 1024 * i:1024 * (i + 1)] for i in range(2)]
        ghid = rawf[:, 2048:3072].rearrange("p (f t) -> p f t", f=FC)
        fhid = rawf[:, 3072:4096].rearrange("p (f t) -> p f t", f=FC)
        vm = [v.rearrange("p (j h c) -> p j h c", j=2, h=HEADS) for v in (rawf[:, 4096:8192], work[:, :])]
        whf = wh[:, :, :].rearrange("p e c -> p (e c)")
        stack = [whf[:, 2048 * i:2048 * (i + 1)].rearrange("p (j q h c) -> p j q h c", j=2, q=2, h=HEADS)
                 for i in range(2)]
        qT = [whf[:, 4096 + 1024 * i:5120 + 1024 * i].rearrange("p (g t) -> p g t", g=GROUP) for i in range(2)]
        kT = [whf[:, 6144 + 1024 * i:7168 + 1024 * i].rearrange("p (g t) -> p g t", g=GROUP) for i in range(2)]
        wffn = sb("wffn", [P, 1024])
        mrow = [sb(f"mrow{i}", [P, 384]) for i in range(2)]
        pr_n = sb("pr_n", [P, 2, D])
        pr_t = sb("pr_t", [P, T])
        pr_b = sb("pr_b", [P, 2, D])
        pr_r = sb("pr_r", [P, 2, D])
        pr_st = sb("pr_st", [P, 2, 6])
        pr_mv = sb("pr_mv", [P, 2, 2])
        pr_rs = sb("pr_rs", [P, 2])
        qk = sb("qk", [P, 2, 2, HEADS, DH])
        qmT = sb("qmT", [P, 2, T], F32R)
        rmax = sb("rmax", [P, 2, HEADS])
        prob = nwork[:, :].rearrange("p (n i c) -> p n i c", n=2, i=2)
        rden = sb("rden", [64, 512])
        ctxT = sb("ctxT", [P, T])
        po_b = sb("po_b", [P, 2, D])
        po_x = sb("po_x", [P, 2, D])
        po_n = sb("po_n", [P, 2, D])
        po_t = sb("po_t", [P, T])
        po_d = sb("po_d", [P, 2, D])
        po_st = sb("po_st", [P, 2, 6])
        po_mv = sb("po_mv", [P, 2, 2])
        po_rs = sb("po_rs", [P, 2])

        ids_in, params_in, cond_in, att_in, x_in0, x_in = map(sem, ["ids_in", "params_in", "cond_in", "att_in", "x_in0", "x_in"])
        moe_in = [sem(f"moe_in{e}") for e in range(E)]
        mlp_in = [sem("mlp_in0"), sem("mlp_in1")]
        const_ready, dve_step, pool_step, act_step = map(sem, ["const_ready", "dve_step", "pool_step", "act_step"])
        cond_dve, cond_pe, cond_act = map(sem, ["cond_dve", "cond_pe", "cond_act"])
        whigh, wsplit = sem("whigh"), sem("wsplit")
        (stat_ready, rstd_ready, normed_ready, nT_ps, hT_ready, tstat_ready, tscale_ready, h2_ready, hsplit, logits_ps,
         shifted, exps, gparts_ready, gT_ps, gT_ready, gb_ps, gb_ready, hid_ps, hid_ready, hid_split, y_ps, part_ready,
         y_sum, yT_ps, x1_ready, rotated) = map(sem, [
             "stat_ready", "rstd_ready", "normed_ready", "nT_ps", "hT_ready", "tstat_ready", "tscale_ready", "h2_ready",
             "hsplit", "logits_ps", "shifted", "exps", "gparts_ready", "gT_ps", "gT_ready", "gb_ps", "gb_ready",
             "hid_ps", "hid_ready", "hid_split", "y_ps", "part_ready", "y_sum", "yT_ps", "x1_ready", "rotated"])
        (xT_ps, xT_ready, xbo_ready, ghid_ps, ghid_ready, mlp_ps, mstat, mrstd, mnorm, x3_ready, astat, arstd, anorm,
         aT_ps, aT_ready, qkv_ps, qkv_ready, stack_ready, kT_ps, kT_ready, qT_ps, qT_ready) = map(sem, [
             "xT_ps", "xT_ready", "xbo_ready", "ghid_ps", "ghid_ready", "mlp_ps", "mstat", "mrstd", "mnorm", "x3_ready",
             "astat", "arstd", "anorm", "aT_ps", "aT_ready", "qkv_ps", "qkv_ready", "stack_ready", "kT_ps", "kT_ready",
             "qT_ps", "qT_ready"])
        (s_ps, max_ready, m_ready, qmT_ps, qmT_ready, t_ps, prob_ready, pv_ps, ctx_ready, wo_ps, xb4_ready, fstat, frstd,
         fnorm, fT_ps, fT_ready, fhid_ps, fhid_ready, ffn_ps, diff_ready, out_ready, out_done) = map(sem, [
             "s_ps", "max_ready", "m_ready", "qmT_ps", "qmT_ready", "t_ps", "prob_ready", "pv_ps", "ctx_ready", "wo_ps",
             "xb4_ready", "fstat", "frstd", "fnorm", "fT_ps", "fT_ready", "fhid_ps", "fhid_ready", "ffn_ps",
             "diff_ready", "out_ready", "out_done"])

        values_clear, stack_clear, trig_ready, xcopy_ready = map(
            sem, ["values_clear", "stack_clear", "trig_ready", "xcopy_ready"])
        started = sem("started")
        out_credit = sb("out_credit", [P, 1])

        scale = float(DH) ** -0.5
        x_tiles = x.rearrange("s (j p) d -> p (s j) d", p=P)
        out_tiles = out.rearrange("s (j p) d -> p (s j) d", p=P)

        def col(name, i=0):
            return pcol[:, COL[name] + i:COL[name] + i + 1]

        def mlp_count(n, par):
            return 16 * (n + 2 - par)

        def diagonal(cols):
            (step, count), (one, _) = cols.ap
            return bass.AP(cols.tensor, cols.offset, [(step, count), ((P + DH) * one, 8), (one, DH)])

        def sequences(eng, chain, pre_at, post_at, pre, post, attention=None, told=False):
            def body(s, par, first, last):
                for slot in range(3 * PAIRS):
                    if attention is not None:
                        attention(s, par, slot // 3, slot % 3, first, last)
                    if not last and not (isinstance(s, int) and s == SEQS - 1):
                        for at, step in pre_at:
                            if at == slot:
                                pre(s + 1, 1 - par, step)
                    if not first:
                        for at, step in post_at:
                            if at == slot:
                                if told:
                                    post(s - 1, not (isinstance(s, int) and s >= SEQS - 1), step)
                                else:
                                    post(s - 1, step)

            for _, step in pre_at:
                pre(0, 0, step)
            body(0, 0, True, False)
            start = chain.n + chain.base if chain else 0
            per = STEPS_OF_TWO[chain.name] if chain else 0
            with eng.Fori(0, 3) as i:
                if chain:
                    chain.enter(start + per * i)
                body(2 * i + 1, 1, False, False)
                body(2 * i + 2, 0, False, False)
                if chain:
                    assert chain.n == per, (chain.name, chain.n)
            if chain:
                chain.enter(start + 3 * per)
            body(SEQS - 1, 1, False, False)
            body(SEQS, 0, False, True)

        def need(eng, sem, value):
            if not isinstance(value, int) or value > 0:
                eng.wait_ge(sem, value)

        def apart(eng, sem, value):
            if not isinstance(value, int):
                value = eng.to_reg(value)
                eng.wait_ge(started, 1)
            if not isinstance(value, int) or value > 0:
                eng.wait_ge(sem, value)

        block = ctx.enter_context(nc.Block())

        @block.sync
        def _(sp):
            sp.dma_start(X[:, 0:BTILES, :], x_tiles[:, 0:BTILES, :]).then_inc(x_in0, 16)
            sp.dma_start(prow[:, :], rows).then_inc(params_in, 16)
            sp.dma_start(idall[:, :], ids.partition_broadcast(SUBJECTS).rearrange("p a n -> p (a n)")).then_inc(ids_in, 16)
            sp.dma_start(idrow[:, :], ids).then_inc(ids_in, 16)
            for dst, src in ((subj_sb[:, :], subj), (bi_rows[:, :], mlp_bi), (hyp1_sb[:, :], hyp_w[0:SE, :]),
                             (hyp2_sb[:, :], hyp_w[SE:SE + P, :]), (sty1_sb[:, :], sty_w1), (sty2_sb[:, :], sty_w2),
                             (styb1[:, :], sty_b1), (router_sb[:, :], router),
                             (ang[:, :], angles.partition_broadcast(P).rearrange("p a n -> p (a n)"))):
                sp.dma_start(dst, src).then_inc(cond_in, 16)
            for e in range(E):
                sp.dma_start(raw[:, e, :], moe_w[e]).then_inc(moe_in[e], 16)
            for g in range(1, BLOCKS):
                sp.dma_start(X[:, g * BTILES:(g + 1) * BTILES, :],
                             x_tiles[:, g * BTILES:(g + 1) * BTILES, :]).then_inc(x_in, 16)
            sp.dma_start(watt[:, :], att_w[:, 0:512]).then_inc(att_in, 16)
            sp.dma_start(wffn[:, :], att_w[:, 512:1536]).then_inc(att_in, 16)
            sp.dma_start(arow[:, :], att_rows.partition_broadcast(P).rearrange("p a n -> p (a n)")).then_inc(att_in, 16)
            sp.wait_ge(ids_in, 32)
            sp.wait_ge(wsplit, E)

            def load_mlp(s, par):
                need(sp, mlp_ps, s - 1)
                need(sp, x3_ready, s - 1)
                e = sp.value_load(idrow[0:1, bass.ds(s + 8, 1)], min_val=0, max_val=E - 1)
                sp.dma_start(wmlp[par], mlp_w[bass.ds(e, 1)].rearrange("a p c -> p (a c)")).then_inc(mlp_in[par], 16)
                sp.dma_start(mrow[par][:, :], mlp_rows[bass.ds(e, 1), :].partition_broadcast(P)
                             .rearrange("p a n -> p (a n)")).then_inc(mlp_in[par], 16)

            def store(s):
                sp.wait_ge(out_ready, s + 1 + OUT_CREDIT)
                sp.dma_start(out_tiles[:, bass.ds(2 * s, 2), :], X[:, bass.ds(2 * s, 2), :]).then_inc(out_done, 16)

            for s in range(3):
                load_mlp(s, s % 2)
            with sp.Fori(0, 2) as i:
                store(2 * i)
                load_mlp(2 * i + 3, 1)
                store(2 * i + 1)
                load_mlp(2 * i + 4, 0)
            store(4)
            load_mlp(7, 1)
            for s in range(5, SEQS):
                store(s)
            sp.wait_ge(out_done, 16 * SEQS)

        @block.gpsimd
        def _(pool):
            g_ = nc.gpsimd
            chain = Chain(pool, pool_step, "pool", apart)
            g_.memset(ident[:, :], 0.0).then_inc(started, 1)
            chain.step(g_.memset(ident16[:, :], 0.0))
            chain.step(g_.memset(mask_qk[:, :], 0.0))
            chain.step(g_.memset(mask_kq[:, :], 0.0))
            chain.step(g_.memset(pick[:, :, :], 0.0))
            chain.step(g_.memset(before[:, :, :], 1.0))
            chain.step(g_.memset(neghalf[:, :], -0.5))
            chain.step(g_.iota(rowno_i[:, :], pattern=[[0, 1]], base=0, channel_multiplier=1))
            chain.settle()
            chain.step(g_.tensor_copy(rowno[:, :], rowno_i[:, :]))
            for m in (ident, ident16):
                chain.step(g_.affine_select(out=m[:, :], in_=m[:, :], compare_op=ALU.not_equal, fill=1.0, base=0,
                                            pattern=[[-1, P]], channel_multiplier=1))
            chain.step(g_.affine_select(out=mask_qk[:, :].rearrange("p (b k) -> p b k", b=2),
                                        in_=mask_qk[:, :].rearrange("p (b k) -> p b k", b=2), compare_op=ALU.is_ge,
                                        fill=MASKED, base=0, pattern=[[0, 2], [-1, P]], channel_multiplier=1))
            chain.step(g_.affine_select(out=mask_kq[:, :].rearrange("p (b q) -> p b q", b=2),
                                        in_=mask_kq[:, :].rearrange("p (b q) -> p b q", b=2), compare_op=ALU.is_ge,
                                        fill=MASKED, base=0, pattern=[[0, 2], [1, P]], channel_multiplier=-1))
            chain.step(g_.affine_select(out=before[:, :, :], in_=before[:, :, :], compare_op=ALU.is_gt, fill=0.0,
                                        base=0, pattern=[[1, E], [-1, E]], channel_multiplier=0))
            for k in range(3):
                chain.link(g_.affine_select(out=pick[:, :, :], in_=pick[:, :, :], compare_op=ALU.not_equal, fill=1.0,
                                            base=-E * k, pattern=[[-1, E], [0, P]], channel_multiplier=1))
            chain.link(g_.tensor_copy(rden[:, 0:1], rowno[0:64, :]))
            g_.tensor_copy(rden[:, 1:2], rowno[0:64, :]).then_inc(const_ready, 1)

            def inverse_root(var, eps, out_ap, tmp, done):
                chain.link(g_.tensor_scalar(tmp, var, eps, None, ALU.add))
                ins = g_.tensor_tensor(out_ap, tmp, neghalf[:, 0:var.shape[1]], ALU.pow)
                return ins.then_inc(done, 1) if done is not None else chain.link(ins)

            def norm_rstd(a):
                apart(pool, stat_ready, a + 1)
                inverse_root(mv[:, :, 1], 1e-5, rstd[:, :], rstd[:, :], rstd_ready)

            def norm_tscale(a):
                apart(pool, tstat_ready, a + 1)
                inverse_root(tmv[:, :, 1], 1e-8, tvar[:, :], tvar[:, :], None)
                chain.link(g_.tensor_tensor(tscale[:, :], tvar[:, :], gam[:, bass.ds(2 * a, 2)], ALU.mult))
                chain.link(g_.tensor_tensor(tvar[:, :], tmv[:, :, 0], tscale[:, :], ALU.mult))
                g_.tensor_tensor(tshift[:, :], bet[:, bass.ds(2 * a, 2)], tvar[:, :], ALU.subtract)\
                    .then_inc(tscale_ready, 1)

            def expert_sum(g, e):
                apart(pool, part_ready, 8 * g + e + 1)
                if e == 1:
                    apart(pool, yT_ps, g)
                    g_.tensor_tensor(ysum[:, :], part[:, 0], part[:, 1], ALU.add).then_inc(y_sum, 1)
                elif e > 1:
                    apart(pool, y_sum, 7 * g + e - 1)
                    g_.tensor_tensor(ysum[:, :], ysum[:, :], part[:, e % 2], ALU.add).then_inc(y_sum, 1)

            def rotate(g):
                apart(pool, x1_ready, g + 1)
                for j in range(2):
                    s = 2 * g + j
                    xs = X[:, bass.ds(2 * s, 2), :].rearrange("p j (q c) -> p (j q) c", c=4)
                    t = rot_t[:, j].rearrange("p j (q c) -> p (j q) c", c=4)
                    cs = rot_c[:, bass.ds(s, 1), :].to_broadcast([P, 64, 4])
                    ss = rot_s[:, bass.ds(s, 1), :].to_broadcast([P, 64, 4])
                    chain.step(g_.tensor_tensor(t[:, :, 0:4:2], xs[:, :, 1:4:2], ss[:, :, 0:4:2], ALU.mult))
                    chain.link(g_.tensor_tensor(t[:, :, 1:4:2], xs[:, :, 0:4:2], ss[:, :, 1:4:2], ALU.mult))
                    chain.link(g_.tensor_tensor(xs, xs, cs, ALU.mult))
                    if j == 0:
                        chain.step(g_.tensor_tensor(xs, xs, t, ALU.add))
                    else:
                        g_.tensor_tensor(xs, xs, t, ALU.add).then_inc(rotated, 1)

            pool.wait_ge(cond_dve, COND_DVE)
            norm_rstd(0)
            norm_tscale(0)

            def moe(g, ahead):
                for n in range(CHUNKS):
                    if n % FC == 1 and n > 1:
                        expert_sum(g, n // FC - 1)
                    if ahead and n == NORM["rstd"]:
                        norm_rstd(g + 1)
                    if ahead and n == NORM["tscale"]:
                        norm_tscale(g + 1)
                expert_sum(g, E - 1)
                rotate(g)

            pro = chain.n
            moe(0, True)
            per = chain.n - pro
            with pool.Fori(1, BLOCKS - 1) as g:
                chain.enter(pro + per * g)
                moe(g, True)
                assert chain.n == per
            chain.enter(pro + per * (BLOCKS - 1))
            moe(BLOCKS - 1, False)

            def clear_values(i):
                chain.link(g_.memset(vm[i], 0.0))
                for q in range(2):
                    v = vm[i].rearrange("p j (q h) c -> p j q h c", q=2)[:, :, q]
                    for h in range(8):
                        ins = g_.memset(v[:, :, h, 64 + DH * h:64 + DH * (h + 1)], 1.0)
                        if (q, h) != (1, 7):
                            chain.step(ins)
                        else:
                            ins.then_inc(values_clear, 1)

            clear_values(0)
            clear_values(1)
            for i in range(2):
                chain.step(g_.memset(stack[i][:, :, :, :, 24:32].bitcast(F32), 0.0))
                chain.settle()
                ins = g_.memset(stack[i][:, :, 1, :, 24:26].bitcast(F32), -1.0)
                ins.then_inc(stack_clear, 1)

            def pre(n, par, step):
                if step == "xbo":
                    pool.wait_ge(rotated, BLOCKS)
                    apart(pool, mlp_in[par], mlp_count(n, par))
                    g_.tensor_tensor(pr_b[:, :, :], X[:, bass.ds(2 * n, 2), :],
                                     mrow[par][:, 0:D].unsqueeze(1).to_broadcast([P, 2, D]), ALU.add)\
                        .then_inc(xbo_ready, 1)
                elif step == "mrstd":
                    apart(pool, mstat, n + 1)
                    inverse_root(pr_mv[:, :, 1], 1e-12, pr_rs[:, :], pr_rs[:, :], mrstd)
                elif step == "affine":
                    apart(pool, mnorm, n + 1)
                    chain.link(g_.tensor_tensor(pr_n[:, :, :], pr_n[:, :, :],
                                                mrow[par][:, D:2 * D].unsqueeze(1).to_broadcast([P, 2, D]), ALU.mult))
                    g_.tensor_tensor(X[:, bass.ds(2 * n, 2), :], pr_n[:, :, :],
                                     mrow[par][:, 2 * D:3 * D].unsqueeze(1).to_broadcast([P, 2, D]), ALU.add)\
                        .then_inc(x3_ready, 1)
                elif step == "arstd":
                    apart(pool, astat, n + 1)
                    inverse_root(pr_mv[:, :, 1], 1e-5, pr_rs[:, :], pr_rs[:, :], arstd)

            def post(m, step):
                if step == "xb4":
                    g_.tensor_tensor(po_b[:, :, :], X[:, bass.ds(2 * m, 2), :],
                                     arow[:, 384:512].unsqueeze(1).to_broadcast([P, 2, D]), ALU.add)\
                        .then_inc(xb4_ready, 1)
                elif step == "frstd":
                    apart(pool, fstat, m + 1)
                    inverse_root(po_mv[:, :, 1], 1e-5, po_rs[:, :], po_rs[:, :], frstd)
                elif step == "diff":
                    chain.link(g_.tensor_tensor(po_d[:, :, :], po_x[:, :, :],
                                                arow[:, 512:640].unsqueeze(1).to_broadcast([P, 2, D]), ALU.add))
                    g_.tensor_tensor(po_d[:, :, :], po_d[:, :, :], X[:, bass.ds(2 * m, 2), :], ALU.subtract)\
                        .then_inc(diff_ready, 1)

            PRE = [(0, "xbo"), (7, "mrstd"), (8, "affine"), (9, "arstd")]
            POST = [(10, "xb4"), (14, "frstd"), (15, "diff")]
            sequences(pool, chain, PRE, POST, pre, post)

        @block.tensor
        def _(pe):
            mm, tr = nc.tensor.matmul, nc.tensor.transpose

            pe.wait_ge(const_ready, 1)
            pe.wait_ge(params_in, 16)
            tr(psD[:, 0, 0:NROWS], prow[:, :], ident[0:NROWS, 0:NROWS]).then_inc(cond_pe, 1)
            pe.wait_ge(cond_in, 16 * 9)
            pe.wait_ge(cond_dve, 1)
            mm(psD[0:SE, 1, 0:8], subj_sb[:, :], onehot[:, :], start=True, stop=True)
            for f in range(FC):
                last = mm(psD[:, 1, 64 + 8 * f:72 + 8 * f], bi_rows[:, f * P:(f + 1) * P], onehot_x[:, :],
                          start=True, stop=True)
            last.then_inc(cond_pe, 1)
            pe.wait_ge(cond_dve, 2)
            mm(psD[:, 1, 128:136], hyp1_sb[:, :], cond_a[0:SE, :], start=True, stop=True).then_inc(cond_pe, 1)
            pe.wait_ge(cond_act, 1)
            mm(psD[:, 1, 136:144], hyp2_sb[:, :], cond_b[:, :], start=True, stop=True).then_inc(cond_pe, 1)
            pe.wait_ge(cond_act, 2)
            mm(psD[0:SE, 1, 144:152], sty1_sb[:, :], cond_c[:, :], start=True, stop=True).then_inc(cond_pe, 1)
            pe.wait_ge(cond_act, 3)
            mm(psD[:, 1, 152:160], sty2_sb[:, 0:D], cond_d[0:SE, :], start=True, stop=True)
            mm(psD[:, 1, 160:168], sty2_sb[:, D:2 * D], cond_d[0:SE, :], start=True, stop=True).then_inc(cond_pe, 1)

            def norm_nT(a):
                pe.wait_ge(normed_ready, a + 1)
                need(pe, hT_ready, a)
                for t in range(BTILES):
                    last = tr(psC[:, 1, t * P:(t + 1) * P], normed[:, t, :], ident[:, :])
                last.then_inc(nT_ps, 1)

            def norm_logits(a):
                pe.wait_ge(h2_ready, a + 1)
                for t in range(BTILES):
                    last = mm(psD[:, 0, t * E:(t + 1) * E], h2[:, t * P:(t + 1) * P], router_sb[:, :],
                              start=True, stop=True)
                last.then_inc(logits_ps, 1)

            def norm_gT(a):
                pe.wait_ge(gparts_ready, a + 1)
                for t in range(BTILES):
                    last = tr(psD[0:3 * E, 0, 64 * t:64 * (t + 1)].bitcast(BF16), gparts[:, t, :], ident16[:, :])
                last.then_inc(gT_ps, 1)

            norm_nT(0)
            norm_logits(0)
            norm_gT(0)

            def three(out_ap, wcols, h_hi, h_lo, start, stop):
                mm(out_ap, wh[:, wcols[0], wcols[1]:wcols[1] + P], h_hi, start=start, stop=False)
                mm(out_ap, wh[:, wcols[0], wcols[1]:wcols[1] + P], h_lo, start=False, stop=False)
                return mm(out_ap, wl[:, wcols[0], wcols[1]:wcols[1] + P], h_hi, start=False, stop=stop)

            def up(g, n):
                e, f = divmod(n, FC)
                if f == 0:
                    pe.wait_ge(wsplit, e + 1)
                    if e == 0:
                        pe.wait_ge(gT_ready, g + 1)
                        pe.wait_ge(hsplit, g + 1)
                    apart(pe, gb_ready, 8 * g + e)
                    mm(psC[:, 0, :], pick[:, e, :], gT[:, g, :], start=True, stop=True).then_inc(gb_ps, 1)
                need(pe, hid_ready, CHUNKS * g + n - 1)
                three(psA[:, n % 2, :], (e, f * P), hh[:, g, :], hl[:, g, :], True, True).then_inc(hid_ps, 1)

            def down(g, n):
                e, f = divmod(n, FC)
                pe.wait_ge(hid_split, CHUNKS * g + n + 1)
                if f == 0:
                    need(pe, part_ready, 8 * g + e - 1)
                three(psB[:, e % 2, :], (e, FF + f * P), hidh[:, n % 4, :], hidl[:, n % 4, :], f == 0, f == FC - 1)\
                    .then_inc(y_ps, 1)

            def moe(g, ahead):
                for n in range(CHUNKS):
                    up(g, n)
                    if n >= 2:
                        down(g, n - 2)
                    if ahead and n == NORM["nT"]:
                        norm_nT(g + 1)
                    if ahead and n == NORM["logits"]:
                        norm_logits(g + 1)
                    if ahead and n == NORM["gT_ps"]:
                        norm_gT(g + 1)
                down(g, CHUNKS - 2)
                down(g, CHUNKS - 1)
                pe.wait_ge(y_sum, 7 * g + 7)
                for t in range(BTILES):
                    last = tr(psC[:, 1, t * P:(t + 1) * P], ysum[:, t * P:(t + 1) * P], ident[:, :])
                last.then_inc(yT_ps, 1)

            moe(0, True)
            with pe.Fori(1, BLOCKS - 1) as g:
                moe(g, True)
            moe(BLOCKS - 1, False)

            def pre(n, par, step):
                if step == "xT":
                    pe.wait_ge(xcopy_ready, n + 1)
                    need(pe, qT_ready, 2 * n)
                    for j in range(2):
                        last = tr(psD[:, 0, j * P:(j + 1) * P], pr_n[:, j, :], ident[:, :])
                    last.then_inc(xT_ps, 1)
                elif step in ("mlp1a", "mlp1b"):
                    b = 1 if step == "mlp1a" else 0
                    if b == 1:
                        pe.wait_ge(xT_ready, n + 1)
                        pe.wait_ge(mlp_in[par], mlp_count(n, par))
                        need(pe, out_ready, n - 2 + OUT_CREDIT)
                    for k in range(2):
                        f = 2 * (1 - b) + k
                        last = mm(psD[:, b, k * T:(k + 1) * T], wmlp[par][:, f * P:(f + 1) * P], pr_t[:, :],
                                  start=True, stop=True)
                    last.then_inc(ghid_ps, 1)
                elif step == "mlp2":
                    pe.wait_ge(ghid_ready, 2 * (n + 1))
                    for j in range(2):
                        for f in range(FC):
                            last = mm(psD[:, 1, j * P:(j + 1) * P], ghid[:, f, j * P:(j + 1) * P],
                                      wmlp[par][:, FF + f * P:FF + (f + 1) * P], start=f == 0, stop=f == FC - 1)
                    last.then_inc(mlp_ps, 1)
                elif step == "aT":
                    pe.wait_ge(anorm, n + 1)
                    for j in range(2):
                        last = tr(psD[:, 0, j * P:(j + 1) * P], pr_r[:, j, :], ident[:, :])
                    last.then_inc(aT_ps, 1)
                elif step == "qkv":
                    pe.wait_ge(aT_ready, n + 1)
                    if isinstance(n, int) and n == 0:
                        pe.wait_ge(att_in, 48)
                    need(pe, fstat, n - 1)
                    for j in range(2):
                        last = mm(psD[:, 1 - j, 0:3 * D], pr_t[:, j * P:(j + 1) * P], watt[:, 0:3 * D],
                                  start=True, stop=True)
                    last.then_inc(qkv_ps, 1)
                elif step in ("kT", "qT"):
                    pe.wait_ge(stack_ready, n + 1)
                    need(pe, fT_ready if step == "kT" else fhid_ready, n - 1 if step == "kT" else 2 * (n - 1))
                    if step == "qT":
                        pe.wait_ge(kT_ready, 2 * (n + 1))
                    qk_ = 1 if step == "kT" else 0
                    for b in (1, 0):
                        for k in range(2):
                            gr = 2 * (1 - b) + k
                            for j in range(2):
                                src = stack[par][:, j, qk_, GROUP * gr:GROUP * (gr + 1), :].bitcast(F32)
                                last = tr(psD[:, b, k * T + j * P:k * T + (j + 1) * P],
                                          src.rearrange("p h c -> p (h c)"), ident[:, :])
                        last.then_inc(kT_ps if step == "kT" else qT_ps, 1)

            def post(m, with_pre, step):
                if step == "wo":
                    pe.wait_ge(ctx_ready, m + 1)
                    if with_pre:
                        pe.wait_ge(mstat, m + 3)
                    else:
                        pe.wait_ge(out_ready, m + OUT_CREDIT)
                    for j in range(2):
                        last = mm(psD[:, 1, j * P:(j + 1) * P], ctxT[:, j * P:(j + 1) * P], watt[:, 3 * D:4 * D],
                                  start=True, stop=True)
                    last.then_inc(wo_ps, 1)
                elif step == "fT":
                    pe.wait_ge(fnorm, m + 1)
                    if with_pre:
                        pe.wait_ge(qkv_ready, m + 3)
                    for j in range(2):
                        last = tr(psD[:, 1, j * P:(j + 1) * P], po_n[:, j, :], ident[:, :])
                    last.then_inc(fT_ps, 1)
                elif step == "ffn1":
                    pe.wait_ge(fT_ready, m + 1)
                    if with_pre:
                        pe.wait_ge(kT_ready, 2 * (m + 3))
                    for b in (1, 0):
                        for k in range(2):
                            f = 2 * (1 - b) + k
                            last = mm(psD[:, b, k * T:(k + 1) * T], wffn[:, f * P:(f + 1) * P], po_t[:, :],
                                      start=True, stop=True)
                        last.then_inc(fhid_ps, 1)
                elif step == "ffn2":
                    pe.wait_ge(fhid_ready, 2 * (m + 1))
                    if with_pre:
                        pe.wait_ge(qT_ready, 2 * (m + 3))
                    for j in range(2):
                        for f in range(FC):
                            last = mm(psD[:, 1, j * P:(j + 1) * P], fhid[:, f, j * P:(j + 1) * P],
                                      wffn[:, FF + f * P:FF + (f + 1) * P], start=f == 0, stop=f == FC - 1)
                    last.then_inc(ffn_ps, 1)

            def scores(s, par, k):
                if k == 0:
                    pe.wait_ge(qT_ready, 2 * (s + 1))
                need(pe, max_ready, 8 * s + k)
                for i in range(2):
                    gr, r = divmod(2 * k + i, GROUP)
                    rows_ = slice(SLOT * r, SLOT * r + 24)
                    mm(psA[:, i, P:3 * P], ident16[:, :], mask_qk[:, :], start=True, stop=False, skip_group_check=True)
                    mm(psA[:, i, 0:2 * P], qT[par][rows_, gr, P:2 * P], kT[par][rows_, gr, :],
                       start=False, stop=False, skip_group_check=True)
                    last = mm(psA[:, i, 2 * P:4 * P], qT[par][rows_, gr, 0:P], kT[par][rows_, gr, :],
                              start=False, stop=True, skip_group_check=True)
                last.then_inc(s_ps, 1)

            def queries_with_max(s, par, gr):
                pe.wait_ge(m_ready, 4 * s + gr + 1)
                need(pe, qmT_ready, 4 * s + gr)
                for j in range(2):
                    src = stack[par][:, j, 0, GROUP * gr:GROUP * (gr + 1), :].bitcast(F32)
                    last = tr(psC[:, 1, j * P:(j + 1) * P], src.rearrange("p h c -> p (h c)"), ident[:, :])
                last.then_inc(qmT_ps, 1)

            def scores_t(s, par, k):
                pe.wait_ge(qmT_ready, 4 * s + k // 2 + 1)
                need(pe, prob_ready, 8 * s + k)
                for i in range(2):
                    gr, r = divmod(2 * k + i, GROUP)
                    rows_ = slice(SLOT * r, SLOT * r + 26)
                    mm(psB[:, i, P:3 * P], ident16[:, :], mask_kq[:, :], start=True, stop=False, skip_group_check=True)
                    mm(psB[:, i, 0:2 * P], kT[par][rows_, gr, P:2 * P], qmT[rows_, gr % 2, :],
                       start=False, stop=False, skip_group_check=True)
                    last = mm(psB[:, i, 2 * P:4 * P], kT[par][rows_, gr, 0:P], qmT[rows_, gr % 2, :],
                              start=False, stop=True, skip_group_check=True)
                last.then_inc(t_ps, 1)

            def context(s, par, k):
                if k == 0:
                    need(pe, ctx_ready, s)
                pe.wait_ge(prob_ready, 8 * s + k + 1)
                for i in range(2):
                    h = 2 * k + i
                    c = T * (h // 8)
                    mm(psC[:, 0, c:c + T], vm[par][:, 0, h, :], prob[:, k % 2, i, P:3 * P],
                       start=h % 8 == 0, stop=False, skip_group_check=True)
                    last = mm(psC[:, 0, c + P:c + T], vm[par][:, 1, h, :], prob[:, k % 2, i, 0:P],
                              start=False, stop=h % 8 == 7, skip_group_check=True)
                last.then_inc(pv_ps, 1)

            def attention(s, par, k, part_, first, last):
                if part_ == 0:
                    if not last:
                        scores(s, par, k)
                    if k % 2 == 0:
                        if k >= 2 and not last:
                            queries_with_max(s, par, k // 2 - 1)
                        elif k == 0 and not first:
                            queries_with_max(s - 1, 1 - par, 3)
                elif part_ == 1:
                    if k >= 3 and not last:
                        scores_t(s, par, k - 3)
                    elif k < 3 and not first:
                        scores_t(s - 1, 1 - par, k + 5)
                else:
                    if k >= 4 and not last:
                        context(s, par, k - 4)
                    elif k < 4 and not first:
                        context(s - 1, 1 - par, k + 4)

            PRE = [(1, "xT"), (3, "mlp1a"), (4, "mlp1b"), (6, "mlp2"), (11, "aT"), (13, "qkv"), (17, "kT"), (20, "qT")]
            POST = [(12, "wo"), (16, "fT"), (18, "ffn1"), (22, "ffn2")]
            sequences(pe, None, PRE, POST, pre, post, attention, True)

        @block.scalar
        def _(act):
            a_ = nc.scalar.activation
            chain = Chain(act, act_step, "act", need)
            act.wait_ge(cond_dve, 3)
            chain.step(a_(trig[:, 4, :], trig[:, 2, :], ACT.Sin))
            a_(trig[:, 5, :], trig[:, 3, :], ACT.Sin).then_inc(trig_ready, 1)
            act.wait_ge(cond_pe, 3)
            a_(cond_b[:, :], psD[:, 1, 128:136], ACT.Relu, bias=col("hyp_b1")).then_inc(cond_act, 1)
            act.wait_ge(cond_pe, 4)
            a_(cond_c[:, :], psD[:, 1, 136:144], ACT.Identity, bias=col("hyp_b2")).then_inc(cond_act, 1)
            act.wait_ge(cond_pe, 5)
            a_(cond_d[0:SE, :], psD[0:SE, 1, 144:152], ACT.Relu, bias=styb1[:, :]).then_inc(cond_act, 1)
            act.wait_ge(cond_dve, 4)
            chain.link(a_(sp_t[:, 2, :], sp_t[:, 1, :], ACT.Exp, scale=-1.0))
            a_(sp_t[:, 3, :], sp_t[:, 2, :], ACT.Ln, bias=1.0).then_inc(cond_act, 1)

            def norm_hT(a):
                act.wait_ge(nT_ps, a + 1)
                a_(hT[:, :], psC[:, 1, :], ACT.Identity, bias=col("ln_b"), scale=col("ln_g")).then_inc(hT_ready, 1)

            def norm_exp(a):
                act.wait_ge(shifted, a + 1)
                a_(probs[:, :, :], probs[:, :, :], ACT.Exp).then_inc(exps, 1)

            def norm_gT(a):
                act.wait_ge(gT_ps, a + 1)
                a_(gT[:, a, :], psD[0:3 * E, 0, 0:256].bitcast(BF16), ACT.Copy).then_inc(gT_ready, 1)

            norm_hT(0)
            for e in range(E):
                act.wait_ge(moe_in[e], 16)
                a_(wh[:, e, :], raw[:, e, :], ACT.Copy).then_inc(whigh, 1)
                if e == 0:
                    norm_exp(0)
                if e == 1:
                    norm_gT(0)

            def moe(g, ahead):
                for n in range(CHUNKS):
                    e, f = divmod(n, FC)
                    if f == 0:
                        act.wait_ge(gb_ps, 8 * g + e + 1)
                        need(act, part_ready, 8 * g + e - 1)
                        a_(gb[:, e % 2, :], psC[:, 0, :], ACT.Copy).then_inc(gb_ready, 1)
                    act.wait_ge(hid_ps, CHUNKS * g + n + 1)
                    need(act, hid_split, CHUNKS * g + n - 3)
                    a_(hid[:, n % 4, :], psA[:, n % 2, :], ACT.Relu, bias=col("b1", n)).then_inc(hid_ready, 1)
                    if ahead and n == NORM["hT"]:
                        norm_hT(g + 1)
                    if ahead and n == NORM["exp"]:
                        norm_exp(g + 1)
                    if ahead and n == NORM["gT"]:
                        norm_gT(g + 1)

            moe(0, True)
            with act.Fori(1, BLOCKS - 1) as g:
                moe(g, True)
            moe(BLOCKS - 1, False)

            def pre(n, par, step):
                if step == "xT":
                    act.wait_ge(xT_ps, n + 1)
                    a_(pr_t[:, :], psD[:, 0, 0:T], ACT.Copy).then_inc(xT_ready, 1)
                elif step in ("gelu_a", "gelu_b"):
                    b = 1 if step == "gelu_a" else 0
                    act.wait_ge(ghid_ps, 2 * n + 2 - b)
                    for k in range(2):
                        f = 2 * (1 - b) + k
                        ins = a_(ghid[:, f, :], psD[:, b, k * T:(k + 1) * T], ACT.Gelu,
                                 bias=bi_col[:, f, bass.ds(n, 1)])
                    ins.then_inc(ghid_ready, 1)
                elif step == "aT":
                    act.wait_ge(aT_ps, n + 1)
                    a_(pr_t[:, :], psD[:, 0, 0:T], ACT.Identity, bias=col("beta1"), scale=col("gamma1"))\
                        .then_inc(aT_ready, 1)
                elif step in ("kT", "qT"):
                    for b in (1, 0):
                        act.wait_ge(kT_ps if step == "kT" else qT_ps, 2 * n + 2 - b)
                        dst = (kT if step == "kT" else qT)[par][:, 2 * (1 - b):2 * (2 - b), :]
                        a_(dst, psD[:, b, :].rearrange("p (g t) -> p g t", g=2), ACT.Copy)\
                            .then_inc(kT_ready if step == "kT" else qT_ready, 1)

            def post(m, with_pre, step):
                if step == "fT":
                    act.wait_ge(fT_ps, m + 1)
                    a_(po_t[:, :], psD[:, 1, 0:T], ACT.Identity, bias=col("beta2"), scale=col("gamma2"))\
                        .then_inc(fT_ready, 1)
                elif step == "gelu":
                    for b in (1, 0):
                        act.wait_ge(fhid_ps, 2 * m + 2 - b)
                        for k in range(2):
                            f = 2 * (1 - b) + k
                            ins = a_(fhid[:, f, :], psD[:, b, k * T:(k + 1) * T], ACT.Gelu, bias=col("ffn_b1", f))
                        ins.then_inc(fhid_ready, 1)

            def exp_t(s, k):
                act.wait_ge(t_ps, 8 * s + k + 1)
                need(act, pv_ps, 8 * s + k - 1)
                a_(prob[:, k % 2], psB[:, :, P:4 * P], ACT.Exp, scale=scale).then_inc(prob_ready, 1)

            def queries(s, gr):
                act.wait_ge(qmT_ps, 4 * s + gr + 1)
                need(act, t_ps, 8 * s + 2 * gr - 2)
                a_(qmT[:, gr % 2, :], psC[:, 1, 0:T], ACT.Copy).then_inc(qmT_ready, 1)

            def attention(s, par, k, part_, first, last):
                if part_ == 0 and k % 2 == 0:
                    if k >= 2 and not last:
                        queries(s, k // 2 - 1)
                    elif k == 0 and not first:
                        queries(s - 1, 3)
                elif part_ == 1:
                    if k >= 3 and not last:
                        exp_t(s, k - 3)
                    elif k < 3 and not first:
                        exp_t(s - 1, k + 5)

            PRE = [(2, "xT"), (4, "gelu_a"), (5, "gelu_b"), (12, "aT"), (18, "kT"), (21, "qT")]
            POST = [(17, "fT"), (19, "gelu")]
            sequences(act, None, PRE, POST, pre, post, attention, True)

        @block.vector
        def _(dve):
            v_ = nc.vector
            chain = Chain(dve, dve_step, "dve", need)

            def layer_stats(src, st, out_mv, count, done):
                for t in range(count):
                    chain.step(v_.bn_stats(st[:, t, :], src(t)))
                apart(dve, chain.sem, chain.base + chain.n)
                for t in range(count):
                    ins = v_.bn_aggr(out_mv[:, t, :], st[:, t, :])
                    if t < count - 1:
                        chain.step(ins)
                ins.then_inc(done, 1)

            def layer_norm(src, mv_, rs, dst, count, done):
                for t in range(count):
                    ins = v_.tensor_scalar(dst(t), src(t), mv_[:, t, 0:1], rs[:, t:t + 1], ALU.subtract, ALU.mult)
                    if t < count - 1:
                        chain.step(ins)
                ins.then_inc(done, 1)

            def norm_stats(a):
                if isinstance(a, int) and a == 0:
                    dve.wait_ge(x_in0, 16)
                else:
                    dve.wait_ge(x_in, 48)
                layer_stats(lambda t: X[:, BTILES * a + t, :], stats, mv, BTILES, stat_ready)

            def norm_normed(a):
                dve.wait_ge(rstd_ready, a + 1)
                need(dve, nT_ps, a)
                layer_norm(lambda t: X[:, BTILES * a + t, :], mv, rstd, lambda t: normed[:, t, :], BTILES, normed_ready)

            def norm_tstats(a):
                dve.wait_ge(hT_ready, a + 1)
                layer_stats(lambda j: hT[:, j * T:(j + 1) * T], tstats, tmv, 2, tstat_ready)

            def norm_h2(a):
                dve.wait_ge(tscale_ready, a + 1)
                need(dve, logits_ps, a)
                for j in range(2):
                    ins = v_.tensor_scalar(h2[:, j * T:(j + 1) * T], hT[:, j * T:(j + 1) * T], tscale[:, j:j + 1],
                                           tshift[:, j:j + 1], ALU.mult, ALU.add)
                    if j == 0:
                        chain.step(ins)
                ins.then_inc(h2_ready, 1)
                dve.wait_ge(h2_ready, a + 1)
                chain.link(v_.tensor_copy(hh[:, a, :], h2[:, :]))
                v_.tensor_tensor(hl[:, a, :], h2[:, :], hh[:, a, :].bitcast(F32), ALU.subtract).then_inc(hsplit, 1)

            def norm_shift(a):
                dve.wait_ge(logits_ps, a + 1)
                lg = psD[:, 0, 0:BTILES * E].rearrange("p (t e) -> p t e", t=BTILES)
                chain.link(v_.tensor_reduce(lmax[:, :], lg, AX_X, ALU.max))
                v_.tensor_tensor(probs[:, :, :], lg, lmax[:, :].unsqueeze(2).to_broadcast([P, BTILES, E]),
                                 ALU.subtract).then_inc(shifted, 1)

            def norm_gates(a):
                wide = [P, BTILES, E]
                dve.wait_ge(exps, a + 1)
                chain.link(v_.tensor_reduce(psums[:, :], probs[:, :, :], AX_X, ALU.add))
                chain.link(v_.reciprocal(psums[:, :], psums[:, :]))
                chain.link(v_.tensor_tensor(probs[:, :, :], probs[:, :, :], psums[:, :].unsqueeze(2).to_broadcast(wide),
                                            ALU.mult))
                pj = probs[:, :, :].unsqueeze(2).to_broadcast([P, BTILES, E, E])
                pe_ = probs[:, :, :].unsqueeze(3).to_broadcast([P, BTILES, E, E])
                chain.step(v_.tensor_tensor(above[:, :, :, :], pj, pe_, ALU.is_gt))
                chain.link(v_.tensor_tensor(equal[:, :, :, :], pj, pe_, ALU.is_equal))
                chain.link(v_.tensor_tensor(equal[:, :, :, :], equal[:, :, :, :],
                                            before[:, :, :].unsqueeze(1).to_broadcast([P, BTILES, E, E]), ALU.mult))
                chain.link(v_.tensor_tensor(above[:, :, :, :], above[:, :, :, :], equal[:, :, :, :], ALU.add))
                chain.link(v_.tensor_reduce(rank[:, :, :], above[:, :, :, :], AX_X, ALU.add))
                chain.link(v_.scalar_tensor_tensor(out=gates[:, :, :], in0=rank[:, :, :], scalar=2.0, in1=probs[:, :, :],
                                                   op0=ALU.is_lt, op1=ALU.mult))
                chain.link(v_.tensor_reduce(psums[:, :], gates[:, :, :], AX_X, ALU.add))
                chain.link(v_.reciprocal(psums[:, :], psums[:, :]))
                chain.link(v_.tensor_tensor(gates[:, :, :], gates[:, :, :], psums[:, :].unsqueeze(2).to_broadcast(wide),
                                            ALU.mult))
                for k in range(3):
                    ins = v_.tensor_copy(gparts[:, :, k * E:(k + 1) * E], gates[:, :, :])
                    if k < 2:
                        chain.link(ins)
                        chain.link(v_.tensor_tensor(gates[:, :, :], gates[:, :, :], gparts[:, :, k * E:(k + 1) * E],
                                                    ALU.subtract))
                ins.then_inc(gparts_ready, 1)

            dve.wait_ge(const_ready, 1)
            dve.wait_ge(ids_in, 32)
            chain.link(v_.tensor_copy(idf[:, :], idall[:, :]))
            chain.step(v_.tensor_scalar(onehot[:, :], idf[:, 0:8], rowno[0:SUBJECTS, :], None, ALU.is_equal))
            v_.tensor_scalar(onehot_x[:, :], idf[0:E, 8:16], rowno[0:E, :], None, ALU.is_equal).then_inc(cond_dve, 1)
            v_.memset(out_credit[:, :], 0.0).then_inc(out_ready, OUT_CREDIT)
            norm_stats(0)
            dve.wait_ge(cond_pe, 1)
            chain.step(v_.tensor_copy(pcol[:, :], psD[:, 0, 0:NROWS]))
            dve.wait_ge(cond_pe, 2)
            chain.step(v_.tensor_copy(bi_col[:, :, :], psD[:, 1, 64:96].rearrange("p (f s) -> p f s", f=FC)))
            v_.tensor_copy(cond_a[0:SE, :], psD[0:SE, 1, 0:8]).then_inc(cond_dve, 1)
            dve.wait_ge(cond_in, 16 * 9)
            magic = 12582912.0
            chain.link(v_.tensor_scalar(trig[:, 0, :], ang[:, 0:16], 1.0 / (2 * PI), magic, ALU.mult, ALU.add))
            chain.link(v_.tensor_scalar(trig[:, 0, :], trig[:, 0, :], magic, None, ALU.subtract))
            chain.link(v_.scalar_tensor_tensor(out=trig[:, 1, :], in0=trig[:, 0, :], scalar=-6.28125, in1=ang[:, 0:16],
                                               op0=ALU.mult, op1=ALU.add))
            chain.link(v_.scalar_tensor_tensor(out=trig[:, 1, :], in0=trig[:, 0, :], scalar=-(2 * PI - 6.28125),
                                               in1=trig[:, 1, :], op0=ALU.mult, op1=ALU.add))
            chain.link(v_.tensor_scalar(trig[:, 2, :], trig[:, 1, :], 3.1415925, -3.1415925, ALU.min, ALU.max))
            chain.link(v_.tensor_scalar(trig[:, 0, :], trig[:, 1, :], PI / 2, -2 * PI, ALU.is_gt, ALU.mult))
            chain.link(v_.tensor_tensor(trig[:, 3, :], trig[:, 1, :], trig[:, 0, :], ALU.add))
            chain.link(v_.tensor_scalar(trig[:, 3, :], trig[:, 3, :], PI / 2, 3.1415925, ALU.add, ALU.min))
            v_.tensor_scalar(trig[:, 3, :], trig[:, 3, :], -3.1415925, None, ALU.max).then_inc(cond_dve, 1)
            dve.wait_ge(trig_ready, 1)
            for k in range(2):
                sin_, cos_ = trig[:, 4, 8 * k:8 * k + 8], trig[:, 5, 8 * k:8 * k + 8]
                chain.step(v_.tensor_copy(rot_s[:, :, 2 * k], sin_))
                chain.step(v_.tensor_scalar(rot_s[:, :, 2 * k + 1], sin_, -1.0, None, ALU.mult))
                chain.step(v_.tensor_copy(rot_c[:, :, 2 * k], cos_))
                chain.step(v_.tensor_copy(rot_c[:, :, 2 * k + 1], cos_))
            dve.wait_ge(cond_pe, 6)
            chain.settle()
            chain.step(v_.tensor_scalar(bet[:, :], psD[:, 1, 160:168], col("sty_b2", 1), None, ALU.add))
            chain.link(v_.tensor_scalar(sp_t[:, 0, :], psD[:, 1, 152:160], col("sty_b2"), None, ALU.add))
            chain.link(v_.tensor_scalar(sp_t[:, 1, :], sp_t[:, 0, :], -1.0, None, ALU.mult))
            v_.tensor_tensor(sp_t[:, 1, :], sp_t[:, 0, :], sp_t[:, 1, :], ALU.max).then_inc(cond_dve, 1)
            dve.wait_ge(cond_act, 4)
            u, lw, w1, q = (sp_t[:, i, :] for i in (2, 3, 4, 5))
            chain.link(v_.tensor_scalar(w1, u, 1.0, -1.0, ALU.add, ALU.add))
            chain.link(v_.tensor_scalar(q, w1, 1e-30, None, ALU.max))
            chain.link(v_.reciprocal(q, q))
            chain.link(v_.tensor_tensor(q, q, u, ALU.mult))
            chain.link(v_.tensor_tensor(q, q, lw, ALU.mult))
            chain.link(v_.scalar_tensor_tensor(out=w1, in0=w1, scalar=0.0, in1=u, op0=ALU.is_equal, op1=ALU.mult))
            chain.link(v_.tensor_tensor(q, q, w1, ALU.add))
            chain.link(v_.scalar_tensor_tensor(out=q, in0=sp_t[:, 0, :], scalar=0.0, in1=q, op0=ALU.max, op1=ALU.add))
            v_.tensor_scalar(gam[:, :], q, 1e-8, None, ALU.add).then_inc(cond_dve, 1)
            norm_normed(0)
            norm_tstats(0)
            norm_h2(0)

            def split_weights(e):
                dve.wait_ge(whigh, e + 1)
                v_.tensor_tensor(wl[:, e, :], raw[:, e, :], wh[:, e, :].bitcast(F32), ALU.subtract).then_inc(wsplit, 1)

            split_weights(0)
            norm_shift(0)
            norm_gates(0)
            for e in range(1, E):
                split_weights(e)

            def split_hidden(g, n):
                dve.wait_ge(hid_ready, CHUNKS * g + n + 1)
                need(dve, y_ps, CHUNKS * g + n - 3)
                chain.link(v_.tensor_copy(hidh[:, n % 4, :], hid[:, n % 4, :]))
                v_.tensor_tensor(hidl[:, n % 4, :], hid[:, n % 4, :], hidh[:, n % 4, :].bitcast(F32), ALU.subtract)\
                    .then_inc(hid_split, 1)

            def gated(g, e):
                dve.wait_ge(y_ps, CHUNKS * g + FC * (e + 1))
                dve.wait_ge(gb_ready, 8 * g + e + 1)
                need(dve, y_sum, 7 * g + (max(e - 2, 1) if e >= 2 else e - 1))
                v_.scalar_tensor_tensor(out=part[:, e % 2, :], in0=psB[:, e % 2, :], scalar=col("b2", e),
                                        in1=gb[:, e % 2, :], op0=ALU.add, op1=ALU.mult).then_inc(part_ready, 1)

            def moe(g, ahead):
                for n in range(CHUNKS):
                    split_hidden(g, n)
                    if n % FC == 1 and n > 1:
                        gated(g, n // FC - 1)
                    if ahead:
                        for name, fn in (("stats", norm_stats), ("normed", norm_normed), ("tstats", norm_tstats),
                                         ("h2", norm_h2), ("shift", norm_shift), ("gates", norm_gates)):
                            if n == NORM[name]:
                                fn(g + 1)
                gated(g, E - 1)
                dve.wait_ge(yT_ps, g + 1)
                xs = X[:, bass.ds(BTILES * g, BTILES), :]
                v_.tensor_tensor(xs, psC[:, 1, :].rearrange("p (t d) -> p t d", t=BTILES), xs, ALU.add)\
                    .then_inc(x1_ready, 1)

            pro = chain.n
            moe(0, True)
            per = chain.n - pro
            with dve.Fori(1, BLOCKS - 1) as g:
                chain.enter(pro + per * g)
                moe(g, True)
                assert chain.n == per
            chain.enter(pro + per * (BLOCKS - 1))
            moe(BLOCKS - 1, False)

            def pre(n, par, step):
                if step == "xcopy":
                    dve.wait_ge(rotated, BLOCKS)
                    need(dve, x3_ready, n)
                    v_.tensor_copy(pr_n[:, :, :], X[:, bass.ds(2 * n, 2), :]).then_inc(xcopy_ready, 1)
                elif step == "stats":
                    dve.wait_ge(mlp_ps, n + 1)
                    dve.wait_ge(xbo_ready, n + 1)
                    chain.link(v_.tensor_tensor(pr_r[:, :, :], psD[:, 1, 0:T].rearrange("p (j d) -> p j d", j=2),
                                                pr_b[:, :, :], ALU.add))
                    layer_stats(lambda j: pr_r[:, j, :], pr_st, pr_mv, 2, mstat)
                elif step == "norm":
                    dve.wait_ge(mrstd, n + 1)
                    layer_norm(lambda j: pr_r[:, j, :], pr_mv, pr_rs, lambda j: pr_n[:, j, :], 2, mnorm)
                elif step == "astats":
                    apart(dve, x3_ready, n + 1)
                    layer_stats(lambda j: X[:, 2 * n + j, :], pr_st, pr_mv, 2, astat)
                elif step == "anorm":
                    dve.wait_ge(arstd, n + 1)
                    layer_norm(lambda j: X[:, 2 * n + j, :], pr_mv, pr_rs, lambda j: pr_r[:, j, :], 2, anorm)
                elif step == "qkv":
                    dve.wait_ge(qkv_ps, n + 1)
                    dve.wait_ge(values_clear, par + 1)
                    if isinstance(n, int) and n == 0:
                        dve.wait_ge(att_in, 48)
                    need(dve, pv_ps, 8 * (n - 1))
                    for j in range(2):
                        ps = psD[:, 1 - j, :]
                        chain.step(v_.tensor_tensor(qk[:, j].rearrange("p q h d -> p (q h d)"), ps[:, 0:2 * D],
                                                    arow[:, 0:2 * D], ALU.add))
                        for q in range(2):
                            c = 2 * D + 64 * q
                            base = vm[par][:, j, 8 * q:8 * (q + 1), :].rearrange("p h c -> p (h c)")
                            diag = diagonal(base)
                            ins = v_.tensor_tensor(diag, ps[:, c:c + 64].rearrange("p (h d) -> p h d", h=8),
                                                   arow[:, c:c + 64].rearrange("p (h d) -> p h d", h=8), ALU.add)
                            if (j, q) != (1, 1):
                                chain.step(ins)
                    ins.then_inc(qkv_ready, 1)
                elif step == "stack":
                    dve.wait_ge(qkv_ready, n + 1)
                    dve.wait_ge(stack_clear, 2)
                    need(dve, qmT_ps, 4 * (n - 1))
                    st = stack[par]
                    hi = st[:, :, :, :, 0:DH].rearrange("p j q h c -> p (j q h) c")
                    chain.link(v_.tensor_copy(hi, qk[:, :, :, :, :].rearrange("p j q h d -> p (j q h) d")))
                    for q, lo, dup in ((0, DH, 2 * DH), (1, 2 * DH, DH)):
                        h_ = st[:, :, q, :, 0:DH].bitcast(F32)
                        chain.step(v_.tensor_tensor(st[:, :, q, :, lo:lo + DH], qk[:, :, q], h_, ALU.subtract))
                        ins = v_.tensor_copy(st[:, :, q, :, dup:dup + DH], h_)
                        if q == 0:
                            chain.step(ins)
                    ins.then_inc(stack_ready, 1)

            def post(m, with_pre, step):
                if step == "ctx":
                    dve.wait_ge(pv_ps, 8 * (m + 1))
                    chain.link(v_.reciprocal(rden[:, :], psC[64:128, 0, :]))
                    chain.step(v_.tensor_tensor(ctxT[0:64, :], psC[0:64, 0, 0:T], rden[:, 0:T], ALU.mult))
                    v_.tensor_tensor(ctxT[64:128, :], psC[0:64, 0, T:2 * T], rden[:, T:2 * T], ALU.mult)\
                        .then_inc(ctx_ready, 1)
                elif step == "x4":
                    dve.wait_ge(wo_ps, m + 1)
                    dve.wait_ge(xb4_ready, m + 1)
                    chain.link(v_.tensor_tensor(po_x[:, :, :], psD[:, 1, 0:T].rearrange("p (j d) -> p j d", j=2),
                                                po_b[:, :, :], ALU.add))
                    layer_stats(lambda j: po_x[:, j, :], po_st, po_mv, 2, fstat)
                elif step == "norm":
                    dve.wait_ge(frstd, m + 1)
                    layer_norm(lambda j: po_x[:, j, :], po_mv, po_rs, lambda j: po_n[:, j, :], 2, fnorm)
                elif step == "out":
                    dve.wait_ge(ffn_ps, m + 1)
                    dve.wait_ge(diff_ready, m + 1)
                    chain.link(v_.tensor_tensor(po_d[:, :, :], psD[:, 1, 0:T].rearrange("p (j d) -> p j d", j=2),
                                                po_d[:, :, :], ALU.add))
                    xs = X[:, bass.ds(2 * m, 2), :]
                    v_.scalar_tensor_tensor(out=xs, in0=po_d[:, :, :], scalar=ang[:, bass.ds(16 + m, 1)], in1=xs,
                                            op0=ALU.mult, op1=ALU.add).then_inc(out_ready, 1)

            def attention(s, par, k, part_, first, last):
                if part_ != 0 or last:
                    return
                dve.wait_ge(s_ps, 8 * s + k + 1)
                chain.step(v_.tensor_reduce(rmax[:, 1, 2 * k:2 * k + 2], psA[:, :, 0:T], AX_X, ALU.max))
                v_.tensor_reduce(rmax[:, 0, 2 * k:2 * k + 2], psA[:, :, T:T + P], AX_X, ALU.max)\
                    .then_inc(max_ready, 1)
                if k % 2:
                    dve.wait_ge(max_ready, 8 * s + k + 1)
                    hs = slice(2 * k - 2, 2 * k + 2)
                    mhi = stack[par][:, :, 0, hs, 24]
                    chain.link(v_.tensor_copy(mhi, rmax[:, :, hs]))
                    v_.tensor_tensor(stack[par][:, :, 0, hs, 25], rmax[:, :, hs], mhi.bitcast(F32), ALU.subtract)\
                        .then_inc(m_ready, 1)

            PRE = [(0, "xcopy"), (7, "stats"), (8, "norm"), (9, "astats"), (10, "anorm"), (14, "qkv"), (15, "stack")]
            POST = [(11, "ctx"), (13, "x4"), (15, "norm"), (23, "out")]
            sequences(dve, chain, PRE, POST, pre, post, attention, True)


def kernel(**inputs):
    import numpy as np
    import concourse.bacc as bacc
    from concourse.bass_utils import run_bass_kernel_spmd

    def get(name):
        return np.asarray(inputs[name])

    l0, l2, l3 = ((lambda n, p=p: get(p + n)) for p in ("L0_cond_", "L2_cond_", "L3_cond_"))

    def experts(w1, w2):
        w2 = w2.reshape(E, FC, P, D).transpose(0, 2, 1, 3).reshape(E, P, FC * D)
        return np.concatenate([w1, w2], axis=2)

    arrays = {
        "x": get("x"),
        "ids": np.concatenate([get("itok_B_6_14"), get("itok_B_0_7")]).reshape(1, 16),
        "angles": np.concatenate([get("condB_theta"), get("condB_phi"), get("condB_gatescore")]).reshape(1, 24),
        "rows": np.concatenate([a.reshape(-1, P) for a in (
            l0("exp_b1"), l0("exp_b2"), l0("ln_g"), l0("ln_b"), l3("b1"), l0("hyp_b1"), l0("hyp_b2"), l0("sty_b2"),
            l3("gamma1"), l3("beta1"), l3("gamma2"), l3("beta2"))]),
        "sty_b1": l0("sty_b1").reshape(SE, 1),
        "subj": l0("subj_emb"),
        "hyp_w": np.concatenate([l0("hyp_w1"), l0("hyp_w2")]),
        "sty_w1": l0("sty_w1"),
        "sty_w2": l0("sty_w2"),
        "router": l0("router_w"),
        "moe_w": experts(l0("exp_w1"), l0("exp_w2")),
        "mlp_w": experts(l2("Wi"), l2("Wo")),
        "mlp_rows": np.concatenate([l2("bo"), l2("gamma"), l2("beta")], axis=1),
        "mlp_bi": l2("bi"),
        "att_w": np.concatenate([l3("Wq"), l3("Wk"), l3("Wv"), l3("Wo"), l3("W1"),
                                 l3("W2").reshape(FC, P, D).transpose(1, 0, 2).reshape(P, FC * D)], axis=1),
        "att_rows": np.concatenate([l3("bq"), l3("bk"), l3("bv"), l3("bo"), l3("b2")]).reshape(1, 640),
    }
    arrays = {f"in_{n}": np.ascontiguousarray(a) for n, a in arrays.items()}
    nc = bacc.Bacc("TRN2", target_bir_lowering=False, num_devices=1)
    aps = [nc.dram_tensor(n, a.shape, mybir.dt.from_np(a.dtype), kind="ExternalInput").ap() for n, a in arrays.items()]
    out = nc.dram_tensor("out", (SEQS, T, D), F32, kind="ExternalOutput").ap()
    conditioned_stack(nc, *aps, out)
    r = run_bass_kernel_spmd(nc, [arrays], core_ids=[0])
    return r.results[0]["out"]
```

```python
from contextlib import ExitStack

import concourse.bass as bass
from concourse import mybir

F32 = mybir.dt.float32
F32R = mybir.dt.float32r
BF16 = mybir.dt.bfloat16
I32 = mybir.dt.int32
ALU = mybir.AluOpType
ACT = mybir.ActivationFunctionType
AX_X = mybir.AxisListType.X

P = 128
D = 128
SEQS, T = 8, 256
TILES = SEQS * T // P
BLOCKS, BT = 4, 512
BTILES = BT // P
E, FF = 8, 512
FC = FF // P
CHUNKS = E * FC
HEADS, DH = 16, 8
SLOT = 32
GROUP = P // SLOT
PAIRS = HEADS // 2
LAG = 4
SUBJECTS, SE = 32, 64
MASKED = -1e30
PI = 3.141592653589793

ROWS = ["b1"] * (E * FC) + ["b2"] * E + ["ln_g", "ln_b"] + ["ffn_b1"] * FC + \
       ["hyp_b1", "hyp_b2", "sty_b2", "sty_b2", "gamma1", "beta1", "gamma2", "beta2"]
COL = {name: ROWS.index(name) for name in ROWS}
NROWS = len(ROWS)


COND_SHAPES = [(SUBJECTS, SE), (SE, P), (P, P), (P, SE), (SE, 2 * D), (D, E)]
COND_PLACES = [(r, sum(w_ for _, w_ in COND_SHAPES[:i]), w) for i, (r, w) in enumerate(COND_SHAPES)]
COND_COLS = sum(w for _, w in COND_SHAPES)


class Chain:

    def __init__(self, eng, sem, name, wait):
        self.wait = wait
        self.eng, self.sem, self.name, self.base, self.n = eng, sem, name, 0, 0

    def step(self, ins):
        ins.then_inc(self.sem, 1)
        self.n += 1

    def settle(self):
        self.wait(self.eng, self.sem, self.base + self.n)

    def link(self, ins):
        self.step(ins)
        self.settle()

    def enter(self, base):
        self.base, self.n = base, 0


DOWN_LAG = 3
GATE_AT, OUTPUT_AT = 5, 7
LAST_T, LAST_X1, LAST_ROTATE = 9, 8, 6
NORM = {"stats": 1, "rstd": 2, "normed": 5, "nT": 10, "hT": 10, "tstats": 11, "tscale": 12, "h2": 14,
        "logits": 17, "shift": 18, "exp": 19, "gates": 21, "gT_ps": 30, "gT": 30}
GATE_PARTS = 8
FIRST = {"xbo": 7, "xcopy": 8, "xT": 9, "mlp1a": 10, "mlp1b": 12, "gelu_a": 10, "gelu_b": 12, "mlp2": 15,
         "stats": 16, "mrstd": 16, "norm": 17, "affine": 17, "astats": 18, "arstd": 18, "anorm": 19, "aT": 20,
         "qkv_mm": 22, "qkv": 23, "stack": 24, "kT": 26, "qT": 28}
COND_DVE = 4
STEPS_OF_BLOCK = {"pool": 12, "dve": 40}
STEPS_OF_TWO = {"pool": 8, "dve": 78}
OUT_CREDIT = 1


def conditioned_stack(nc, x, ids, angles, rows, sty_b1, cond_w, moe_w, mlp_w,
                      mlp_rows, mlp_bi, att_w, att_rows, out):
    with ExitStack() as ctx:
        def sb(name, shape, dt=F32):
            return ctx.enter_context(nc.sbuf_tensor(name, shape, dt))

        def sem(name):
            return ctx.enter_context(nc.semaphore(name))

        psA = ctx.enter_context(nc.psum_tensor("psA", [P, 2, 512], F32))
        psB = ctx.enter_context(nc.psum_tensor("psB", [P, 2, 512], F32))
        psC = ctx.enter_context(nc.psum_tensor("psC", [P, 2, 512], F32))
        psD = ctx.enter_context(nc.psum_tensor("psD", [P, 2, 512], F32))

        ident = sb("ident", [P, P])
        ident16 = sb("ident16", [P, P], BF16)
        mask_qk = sb("mask_qk", [P, 2 * P], BF16)
        mask_kq = sb("mask_kq", [P, 2 * P], BF16)
        pick = sb("pick", [3 * E, E, P], BF16)
        before = sb("before", [P, E, E])
        neghalf = sb("neghalf", [P, 8])
        rowno = sb("rowno", [P, 1])
        rowno_i = sb("rowno_i", [P, 1], I32)

        X = sb("X", [P, TILES, D])
        idall = sb("idall", [SUBJECTS, 16], I32)
        idf = sb("idf", [SUBJECTS, 16])
        ang = sb("ang", [P, 24])
        prow = sb("prow", [NROWS, P])
        pcol = sb("pcol", [P, NROWS])
        styb1 = sb("styb1", [SE, 1])
        cond_sb = sb("cond_sb", [P, COND_COLS])
        subj_sb, hyp1_sb, hyp2_sb, sty1_sb, sty2_sb, router_sb = (
            cond_sb[0:r, c:c + w] for r, c, w in COND_PLACES)
        bi_rows = sb("bi_rows", [E, FF])
        arow = sb("arow", [P, 640])
        watt = sb("watt", [P, 512])
        raw = sb("raw", [P, E, 1024])

        onehot = sb("onehot", [SUBJECTS, 8])
        onehot_x = sb("onehot_x", [E, 8])
        cond_a = sb("cond_a", [P, 8])
        cond_b = sb("cond_b", [P, 8])
        cond_c = sb("cond_c", [P, 8])
        cond_d = sb("cond_d", [P, 8])
        gam = sb("gam", [P, 8])
        bet = sb("bet", [P, 8])
        sp_t = sb("sp_t", [P, 6, 8])
        trig = sb("trig", [P, 6, 16])
        rot_c = sb("rot_c", [P, SEQS, 4])
        rot_s = sb("rot_s", [P, SEQS, 4])
        bi_col = sb("bi_col", [P, FC, SEQS])

        wh = sb("wh", [P, E, 1024], F32R)
        wl = sb("wl", [P, E, 1024], F32R)
        stats = sb("stats", [P, BTILES, 6])
        mv = sb("mv", [P, BTILES, 2])
        rstd = sb("rstd", [P, BTILES])
        nwork = sb("nwork", [P, 3 * BT])
        normed = nwork[:, 0:BT].rearrange("p (t d) -> p t d", t=BTILES)
        hT, h2 = nwork[:, BT:2 * BT], nwork[:, 2 * BT:3 * BT]
        tstats = sb("tstats", [P, 2, 6])
        tmv = sb("tmv", [P, 2, 2])
        tscale = sb("tscale", [P, 2])
        tshift = sb("tshift", [P, 2])
        tvar = sb("tvar", [P, 2])
        hh = sb("hh", [P, BLOCKS, BT], F32R)
        hl = sb("hl", [P, BLOCKS, BT], F32R)
        lmax = sb("lmax", [P, BTILES])
        probs = sb("probs", [P, BTILES, E])
        psums = sb("psums", [P, BTILES])
        above = sb("above", [P, BTILES, E, E])
        equal = sb("equal", [P, BTILES, E, E])
        rank = sb("rank", [P, BTILES, E])
        gates = sb("gates", [P, BTILES, E])
        gparts = sb("gparts", [P, BTILES, 3 * E], BF16)
        gT = sb("gT", [3 * E, BLOCKS, BT], BF16)
        hidh = sb("hidh", [P, 4, BT], F32R)
        hidl = sb("hidl", [P, 4, BT], F32R)
        work = sb("work", [P, 4096])
        hid = work[:, 0:2048].rearrange("p (n t) -> p n t", n=4)
        gb = work[:, 2048:3072].rearrange("p (n t) -> p n t", n=2)
        part = work[:, 3072:4096].rearrange("p (n t) -> p n t", n=2)
        ysum = sb("ysum", [P, BT])
        rot_t = sb("rot_t", [P, 2, 2, D])

        rawf = raw[:, :, :].rearrange("p e c -> p (e c)")
        wmlp = [rawf[:, 1024 * i:1024 * (i + 1)] for i in range(2)]
        ghid = rawf[:, 2048:3072].rearrange("p (f t) -> p f t", f=FC)
        fhid = rawf[:, 3072:4096].rearrange("p (f t) -> p f t", f=FC)
        vm = [v.rearrange("p (j h c) -> p j h c", j=2, h=HEADS) for v in (rawf[:, 4096:8192], work[:, :])]
        whf = wh[:, :, :].rearrange("p e c -> p (e c)")
        stack = [whf[:, 4096 * i:4096 * i + 2048].rearrange("p (j q h c) -> p j q h c", j=2, q=2, h=HEADS)
                 for i in range(2)]
        qT = [whf[:, 4096 * i + 2048:4096 * i + 3072].rearrange("p (g t) -> p g t", g=GROUP) for i in range(2)]
        kT = [whf[:, 4096 * i + 3072:4096 * i + 4096].rearrange("p (g t) -> p g t", g=GROUP) for i in range(2)]
        wffn = sb("wffn", [P, 1024])
        mrow = [sb(f"mrow{i}", [P, 384]) for i in range(2)]
        pr_n = sb("pr_n", [P, 2, D])
        pr_t = sb("pr_t", [P, T])
        pr_b = sb("pr_b", [P, 2, D])
        pr_r = sb("pr_r", [P, 2, D])
        pr_st = sb("pr_st", [P, 2, 6])
        pr_mv = sb("pr_mv", [P, 2, 2])
        pr_rs = sb("pr_rs", [P, 2])
        qk = sb("qk", [P, 2, 2, HEADS, DH])
        qmT = sb("qmT", [P, 2, T], F32R)
        rmax = sb("rmax", [P, 2, HEADS])
        prob = nwork[:, :].rearrange("p (n i c) -> p n i c", n=2, i=2)
        ctx_sb = ysum
        rden = sb("rden", [64, 2 * T])
        ctxT = sb("ctxT", [P, T])
        po_b = sb("po_b", [P, 2, D])
        po_x = sb("po_x", [P, 2, D])
        po_n = sb("po_n", [P, 2, D])
        po_t = sb("po_t", [P, T])
        po_d = sb("po_d", [P, 2, D])
        po_st = sb("po_st", [P, 2, 6])
        po_mv = sb("po_mv", [P, 2, 2])
        po_rs = sb("po_rs", [P, 2])

        ids_in, params_in, cond_in, att_in, x_in0, x_in = map(sem, ["ids_in", "params_in", "cond_in", "att_in", "x_in0", "x_in"])
        ang_in, bi_in = sem("ang_in"), sem("bi_in")
        moe_in = [sem(f"moe_in{e}") for e in range(E)]
        mlp_in = [sem("mlp_in0"), sem("mlp_in1")]
        const_ready, dve_step, pool_step, act_step = map(sem, ["const_ready", "dve_step", "pool_step", "act_step"])
        cond_dve, cond_pe, cond_act = map(sem, ["cond_dve", "cond_pe", "cond_act"])
        whigh, wsplit, hid_high = sem("whigh"), sem("wsplit"), sem("hid_high")
        (stat_ready, rstd_ready, normed_ready, nT_ps, hT_ready, tstat_ready, tscale_ready, h2_ready, hsplit, logits_ps,
         shifted, exps, gparts_ready, gT_ps, gT_ready, gb_ps, gb_ready, hid_ps, hid_ready, hid_split, y_ps, part_ready,
         y_sum, yT_ps, x1_ready, rotated) = map(sem, [
             "stat_ready", "rstd_ready", "normed_ready", "nT_ps", "hT_ready", "tstat_ready", "tscale_ready", "h2_ready",
             "hsplit", "logits_ps", "shifted", "exps", "gparts_ready", "gT_ps", "gT_ready", "gb_ps", "gb_ready",
             "hid_ps", "hid_ready", "hid_split", "y_ps", "part_ready", "y_sum", "yT_ps", "x1_ready", "rotated"])
        (xT_ps, xT_ready, xbo_ready, ghid_ps, ghid_ready, mlp_ps, mstat, mrstd, mnorm, x3_ready, astat, arstd, anorm,
         aT_ps, aT_ready, qkv_ps, qkv_ready, stack_ready, kT_ps, kT_ready, qT_ps, qT_ready) = map(sem, [
             "xT_ps", "xT_ready", "xbo_ready", "ghid_ps", "ghid_ready", "mlp_ps", "mstat", "mrstd", "mnorm", "x3_ready",
             "astat", "arstd", "anorm", "aT_ps", "aT_ready", "qkv_ps", "qkv_ready", "stack_ready", "kT_ps", "kT_ready",
             "qT_ps", "qT_ready"])
        (s_ps, max_ready, m_ready, qmT_ps, qmT_ready, t_ps, prob_ready, pv_ps, ctx_ready, wo_ps, xb4_ready, fstat, frstd,
         fnorm, fT_ps, fT_ready, fhid_ps, fhid_ready, ffn_ps, diff_ready, out_ready, out_done) = map(sem, [
             "s_ps", "max_ready", "m_ready", "qmT_ps", "qmT_ready", "t_ps", "prob_ready", "pv_ps", "ctx_ready", "wo_ps",
             "xb4_ready", "fstat", "frstd", "fnorm", "fT_ps", "fT_ready", "fhid_ps", "fhid_ready", "ffn_ps",
             "diff_ready", "out_ready", "out_done"])

        values_clear, stack_clear, trig_ready, xcopy_ready = map(
            sem, ["values_clear", "stack_clear", "trig_ready", "xcopy_ready"])
        ctx_copied = sem("ctx_copied")
        started, trig_in = sem("started"), sem("trig_in")
        out_credit = sb("out_credit", [P, 1])

        scale = float(DH) ** -0.5
        x_tiles = x.rearrange("s (j p) d -> p (s j) d", p=P)
        out_tiles = out.rearrange("s (j p) d -> p (s j) d", p=P)

        def col(name, i=0):
            return pcol[:, COL[name] + i:COL[name] + i + 1]

        def mlp_count(n, par):
            return 16 * (n + 2 - par)

        def diagonal(cols):
            (step, count), (one, _) = cols.ap
            return bass.AP(cols.tensor, cols.offset, [(step, count), ((P + DH) * one, 8), (one, DH)])

        def sequences(eng, chain, pre_at, post_at, pre, post, attention=None, told=False):
            def body(s, par, first, last):
                for slot in range(3 * PAIRS):
                    if attention is not None:
                        attention(s, par, slot // 3, slot % 3, first, last)
                    if not last and not (isinstance(s, int) and s == SEQS - 1):
                        for at, step in pre_at:
                            if at == slot:
                                pre(s + 1, 1 - par, step)
                    if not first:
                        for at, step in post_at:
                            if at == slot:
                                if told:
                                    post(s - 1, not (isinstance(s, int) and s >= SEQS - 1), step)
                                else:
                                    post(s - 1, step)

            body(0, 0, True, False)
            start = chain.n + chain.base if chain else 0
            per = STEPS_OF_TWO[chain.name] if chain else 0
            with eng.Fori(0, 3) as i:
                if chain:
                    chain.enter(start + per * i)
                body(2 * i + 1, 1, False, False)
                body(2 * i + 2, 0, False, False)
                if chain:
                    assert chain.n == per, (chain.name, chain.n)
            if chain:
                chain.enter(start + 3 * per)
            body(SEQS - 1, 1, False, False)
            body(SEQS, 0, False, True)

        def need(eng, sem, value):
            if not isinstance(value, int) or value > 0:
                eng.wait_ge(sem, value)

        def high_on_act(n):
            return n % 4 != 1

        HIGHS = sum(map(high_on_act, range(CHUNKS)))

        def apart(eng, sem, value):
            if not isinstance(value, int):
                value = eng.to_reg(value)
                eng.wait_ge(started, 1)
            if not isinstance(value, int) or value > 0:
                eng.wait_ge(sem, value)

        block = ctx.enter_context(nc.Block())

        @block.sync
        def _(sp):
            sp.dma_start(ang[:, :], angles.partition_broadcast(P).rearrange("p a n -> p (a n)")).then_inc(ang_in, 16)
            sp.dma_start(idall[:, :], ids.partition_broadcast(SUBJECTS).rearrange("p a n -> p (a n)")).then_inc(ids_in, 16)
            sp.dma_start(X[:, 0:BTILES, :], x_tiles[:, 0:BTILES, :]).then_inc(x_in0, 16)
            sp.dma_start(cond_sb[:, :], cond_w).then_inc(cond_in, 16)
            sp.dma_start(prow[:, :], rows).then_inc(params_in, 16)
            sp.dma_start(styb1[:, :], sty_b1).then_inc(cond_in, 16)
            sp.dma_start(raw[:, 0, :], moe_w[0]).then_inc(moe_in[0], 16)
            sp.dma_start(bi_rows[:, :], mlp_bi).then_inc(bi_in, 16)
            for e in range(1, E):
                sp.dma_start(raw[:, e, :], moe_w[e]).then_inc(moe_in[e], 16)
            for g in range(1, BLOCKS):
                sp.dma_start(X[:, g * BTILES:(g + 1) * BTILES, :],
                             x_tiles[:, g * BTILES:(g + 1) * BTILES, :]).then_inc(x_in, 16)
            sp.dma_start(watt[:, :], att_w[:, 0:512]).then_inc(att_in, 16)
            sp.dma_start(wffn[:, :], att_w[:, 512:1536]).then_inc(att_in, 16)
            sp.dma_start(arow[:, :], att_rows.partition_broadcast(P).rearrange("p a n -> p (a n)")).then_inc(att_in, 16)
            sp.wait_ge(ids_in, 16)
            sp.wait_ge(wsplit, E)

            def load_mlp(s, par):
                need(sp, mlp_ps, s - 1)
                need(sp, x3_ready, s - 1)
                e = sp.value_load(idall[0:1, bass.ds(s + 8, 1)], min_val=0, max_val=E - 1)
                sp.dma_start(wmlp[par], mlp_w[bass.ds(e, 1)].rearrange("a p c -> p (a c)")).then_inc(mlp_in[par], 16)
                sp.dma_start(mrow[par][:, :], mlp_rows[bass.ds(e, 1), :].partition_broadcast(P)
                             .rearrange("p a n -> p (a n)")).then_inc(mlp_in[par], 16)

            def store(s):
                sp.wait_ge(out_ready, s + 1 + OUT_CREDIT)
                sp.dma_start(out_tiles[:, bass.ds(2 * s, 2), :], X[:, bass.ds(2 * s, 2), :]).then_inc(out_done, 16)

            for s in range(3):
                load_mlp(s, s % 2)
            with sp.Fori(0, 2) as i:
                store(2 * i)
                load_mlp(2 * i + 3, 1)
                store(2 * i + 1)
                load_mlp(2 * i + 4, 0)
            store(4)
            load_mlp(7, 1)
            for s in range(5, SEQS):
                store(s)
            sp.wait_ge(out_done, 16 * SEQS)

        @block.gpsimd
        def _(pool):
            g_ = nc.gpsimd
            chain = Chain(pool, pool_step, "pool", apart)
            g_.memset(ident[:, :], 0.0).then_inc(started, 1)
            chain.step(g_.memset(neghalf[:, :], -0.5))
            chain.link(g_.iota(rowno_i[:, :], pattern=[[0, 1]], base=0, channel_multiplier=1))
            chain.step(g_.tensor_copy(rowno[:, :], rowno_i[:, :]))

            def diagonal_ones(m):
                return g_.affine_select(out=m[:, :], in_=m[:, :], compare_op=ALU.not_equal, fill=1.0, base=0,
                                        pattern=[[-1, P]], channel_multiplier=1)

            diagonal_ones(ident).then_inc(const_ready, 1)
            chain.step(g_.memset(ident16[:, :], 0.0))
            chain.link(g_.memset(before[:, :, :], 1.0))
            chain.step(diagonal_ones(ident16))
            g_.affine_select(out=before[:, :, :], in_=before[:, :, :], compare_op=ALU.is_gt, fill=0.0, base=0,
                             pattern=[[1, E], [-1, E]], channel_multiplier=0).then_inc(const_ready, 1)

            def selectors():
                chain.link(g_.memset(pick[:, :, :], 0.0))
                for k in range(3):
                    ins = g_.affine_select(out=pick[:, :, :], in_=pick[:, :, :], compare_op=ALU.not_equal, fill=1.0,
                                           base=-E * k, pattern=[[-1, E], [0, P]], channel_multiplier=1)
                    if k < 2:
                        chain.link(ins)
                ins.then_inc(const_ready, 1)

            def masks():
                chain.step(g_.memset(mask_qk[:, :], 0.0))
                chain.link(g_.memset(mask_kq[:, :], 0.0))
                chain.step(g_.affine_select(out=mask_qk[:, :].rearrange("p (b k) -> p b k", b=2),
                                            in_=mask_qk[:, :].rearrange("p (b k) -> p b k", b=2), compare_op=ALU.is_ge,
                                            fill=MASKED, base=0, pattern=[[0, 2], [-1, P]], channel_multiplier=1))
                g_.affine_select(out=mask_kq[:, :].rearrange("p (b q) -> p b q", b=2),
                                 in_=mask_kq[:, :].rearrange("p (b q) -> p b q", b=2), compare_op=ALU.is_ge,
                                 fill=MASKED, base=0, pattern=[[0, 2], [1, P]], channel_multiplier=-1)\
                    .then_inc(const_ready, 1)

            def weights_rest(e):
                pool.wait_ge(whigh, e + 1)
                g_.tensor_tensor(wl[:, e, :], raw[:, e, :], wh[:, e, :].bitcast(F32), ALU.subtract).then_inc(wsplit, 1)

            def inverse_root(var, eps, out_ap, tmp, done):
                chain.link(g_.tensor_scalar(tmp, var, eps, None, ALU.add))
                ins = g_.tensor_tensor(out_ap, tmp, neghalf[:, 0:var.shape[1]], ALU.pow)
                return ins.then_inc(done, 1) if done is not None else chain.link(ins)

            def norm_rstd(a):
                apart(pool, stat_ready, a + 1)
                inverse_root(mv[:, :, 1], 1e-5, rstd[:, :], rstd[:, :], rstd_ready)

            def norm_tscale(a):
                apart(pool, tstat_ready, a + 1)
                inverse_root(tmv[:, :, 1], 1e-8, tvar[:, :], tvar[:, :], None)
                chain.link(g_.tensor_tensor(tscale[:, :], tvar[:, :], gam[:, bass.ds(2 * a, 2)], ALU.mult))
                chain.link(g_.tensor_tensor(tvar[:, :], tmv[:, :, 0], tscale[:, :], ALU.mult))
                g_.tensor_tensor(tshift[:, :], bet[:, bass.ds(2 * a, 2)], tvar[:, :], ALU.subtract)\
                    .then_inc(tscale_ready, 1)

            def expert_sum(g, e):
                apart(pool, part_ready, 8 * g + e + 1)
                if e == 1:
                    apart(pool, yT_ps, g)
                    g_.tensor_tensor(ysum[:, :], part[:, 0], part[:, 1], ALU.add).then_inc(y_sum, 1)
                elif e > 1:
                    apart(pool, y_sum, 7 * g + e - 1)
                    g_.tensor_tensor(ysum[:, :], ysum[:, :], part[:, e % 2], ALU.add).then_inc(y_sum, 1)

            def rotate(g):
                apart(pool, x1_ready, g + 1)
                for j in range(2):
                    s = 2 * g + j
                    xs = X[:, bass.ds(2 * s, 2), :].rearrange("p j (q c) -> p (j q) c", c=4)
                    t = rot_t[:, j].rearrange("p j (q c) -> p (j q) c", c=4)
                    cs = rot_c[:, bass.ds(s, 1), :].to_broadcast([P, 64, 4])
                    ss = rot_s[:, bass.ds(s, 1), :].to_broadcast([P, 64, 4])
                    chain.step(g_.tensor_tensor(t[:, :, 0:4:2], xs[:, :, 1:4:2], ss[:, :, 0:4:2], ALU.mult))
                    chain.link(g_.tensor_tensor(t[:, :, 1:4:2], xs[:, :, 0:4:2], ss[:, :, 1:4:2], ALU.mult))
                    chain.link(g_.tensor_tensor(xs, xs, cs, ALU.mult))
                    if j == 0:
                        chain.step(g_.tensor_tensor(xs, xs, t, ALU.add))
                    else:
                        g_.tensor_tensor(xs, xs, t, ALU.add).then_inc(rotated, 1)

            norm_rstd(0)
            selectors()
            weights_rest(0)
            pool.wait_ge(cond_dve, COND_DVE)
            norm_tscale(0)
            weights_rest(1)

            def clear_values(i):
                chain.link(g_.memset(vm[i], 0.0))
                for q in range(2):
                    v = vm[i].rearrange("p j (q h) c -> p j q h c", q=2)[:, :, q]
                    for h in range(8):
                        ins = g_.memset(v[:, :, h, 64 + DH * h:64 + DH * (h + 1)], 1.0)
                        if (q, h) != (1, 7):
                            chain.step(ins)
                        else:
                            ins.then_inc(values_clear, 1)

            def clear_stack(i):
                chain.link(g_.memset(stack[i][:, :, :, :, 24:32].bitcast(F32), 0.0))
                g_.memset(stack[i][:, :, 1, :, 24:26].bitcast(F32), -1.0).then_inc(stack_clear, 1)

            def pre(n, par, step):
                if step == "xbo":
                    pool.wait_ge(rotated, 1 if isinstance(n, int) and n < 2 else BLOCKS)
                    apart(pool, mlp_in[par], mlp_count(n, par))
                    g_.tensor_tensor(pr_b[:, :, :], X[:, bass.ds(2 * n, 2), :],
                                     mrow[par][:, 0:D].unsqueeze(1).to_broadcast([P, 2, D]), ALU.add)\
                        .then_inc(xbo_ready, 1)
                elif step == "mrstd":
                    apart(pool, mstat, n + 1)
                    inverse_root(pr_mv[:, :, 1], 1e-12, pr_rs[:, :], pr_rs[:, :], mrstd)
                elif step == "arstd":
                    apart(pool, astat, n + 1)
                    inverse_root(pr_mv[:, :, 1], 1e-5, pr_rs[:, :], pr_rs[:, :], arstd)

            def post(m, step):
                if step == "xb4":
                    g_.tensor_tensor(po_b[:, :, :], X[:, bass.ds(2 * m, 2), :],
                                     arow[:, 384:512].unsqueeze(1).to_broadcast([P, 2, D]), ALU.add)\
                        .then_inc(xb4_ready, 1)
                elif step == "frstd":
                    apart(pool, fstat, m + 1)
                    inverse_root(po_mv[:, :, 1], 1e-5, po_rs[:, :], po_rs[:, :], frstd)
                elif step == "diff":
                    chain.link(g_.tensor_tensor(po_d[:, :, :], po_x[:, :, :],
                                                arow[:, 512:640].unsqueeze(1).to_broadcast([P, 2, D]), ALU.add))
                    g_.tensor_tensor(po_d[:, :, :], po_d[:, :, :], X[:, bass.ds(2 * m, 2), :], ALU.subtract)\
                        .then_inc(diff_ready, 1)

            def moe(g, first, ahead):
                last = not ahead
                for n in range(CHUNKS):
                    if n % FC == OUTPUT_AT % FC:
                        e = (n - OUTPUT_AT) // FC
                        if e >= 0:
                            expert_sum(g, e)
                        elif not first:
                            expert_sum(g - 1, e + E)
                    if n == LAST_ROTATE and not first:
                        rotate(g - 1)
                    if ahead and n == NORM["rstd"]:
                        norm_rstd(g + 1)
                    if ahead and n == NORM["tscale"]:
                        norm_tscale(g + 1)
                    if first and n in (0, 2, 4, 5, 6, 7):
                        weights_rest(2 + (0, 2, 4, 5, 6, 7).index(n))
                    if first and n == 8:
                        masks()
                    if last:
                        if n == 4:
                            clear_values(0)
                        if n == 12:
                            pool.wait_ge(y_ps, CHUNKS * g + 2 * FC)
                            clear_stack(0)
                        for step in ("xbo", "mrstd", "arstd"):
                            if n == FIRST[step]:
                                pre(0, 0, step)

            moe(0, True, True)
            per, start = STEPS_OF_BLOCK["pool"], chain.base + chain.n
            with pool.Fori(1, BLOCKS - 1) as g:
                chain.enter(start + per * (g - 1))
                moe(g, False, True)
                assert chain.n == per, chain.n
            chain.enter(start + per * (BLOCKS - 2))
            moe(BLOCKS - 1, False, False)
            expert_sum(BLOCKS - 1, E - 1)

            def between(s, par, k, part_, first, last):
                if first and (k, part_) == (0, 2):
                    pool.wait_ge(y_sum, (E - 1) * BLOCKS)
                    clear_values(1)
                    clear_stack(1)
                if first and (k, part_) == (3, 0):
                    rotate(BLOCKS - 1)

            PRE = [(0, "xbo"), (6, "mrstd"), (8, "arstd")]
            POST = [(10, "xb4"), (13, "frstd"), (15, "diff")]
            sequences(pool, chain, PRE, POST, pre, post, between)

        @block.tensor
        def _(pe):
            mm, tr = nc.tensor.matmul, nc.tensor.transpose

            pe.wait_ge(const_ready, 1)
            pe.wait_ge(params_in, 16)
            tr(psD[:, 0, 0:NROWS], prow[:, :], ident[0:NROWS, 0:NROWS]).then_inc(cond_pe, 1)
            pe.wait_ge(cond_in, 32)
            pe.wait_ge(cond_dve, 1)
            mm(psD[0:SE, 1, 0:8], subj_sb, onehot[:, :], start=True, stop=True).then_inc(cond_pe, 1)
            pe.wait_ge(cond_dve, 2)
            mm(psD[:, 1, 128:136], hyp1_sb, cond_a[0:SE, :], start=True, stop=True).then_inc(cond_pe, 1)
            pe.wait_ge(cond_act, 1)
            mm(psD[:, 1, 136:144], hyp2_sb, cond_b[:, :], start=True, stop=True).then_inc(cond_pe, 1)
            pe.wait_ge(cond_act, 2)
            mm(psD[0:SE, 1, 144:152], sty1_sb, cond_c[:, :], start=True, stop=True).then_inc(cond_pe, 1)
            pe.wait_ge(cond_act, 3)
            mm(psD[:, 1, 152:160], sty2_sb[:, 0:D], cond_d[0:SE, :], start=True, stop=True)
            mm(psD[:, 1, 160:168], sty2_sb[:, D:2 * D], cond_d[0:SE, :], start=True, stop=True).then_inc(cond_pe, 1)

            def norm_nT(a):
                pe.wait_ge(normed_ready, a + 1)
                need(pe, hT_ready, a)
                need(pe, x1_ready, a - 1)
                for t in range(BTILES):
                    last = tr(psC[:, 1, t * P:(t + 1) * P], normed[:, t, :], ident[:, :])
                last.then_inc(nT_ps, 1)

            def norm_logits(a):
                pe.wait_ge(h2_ready, a + 1)
                for t in range(BTILES):
                    last = mm(psD[:, 0, t * E:(t + 1) * E], h2[:, t * P:(t + 1) * P], router_sb,
                              start=True, stop=True)
                last.then_inc(logits_ps, 1)

            def norm_gT(a):
                pe.wait_ge(gparts_ready, a + 1)
                for t in range(BTILES):
                    last = tr(psD[0:3 * E, 0, 64 * t:64 * (t + 1)].bitcast(BF16), gparts[:, t, :], ident16[:, :])
                last.then_inc(gT_ps, 1)

            norm_nT(0)
            pe.wait_ge(bi_in, 16)
            for f in range(FC):
                last = mm(psD[:, 1, 64 + 8 * f:72 + 8 * f], bi_rows[:, f * P:(f + 1) * P], onehot_x[:, :],
                          start=True, stop=True)
            last.then_inc(cond_pe, 1)
            norm_logits(0)

            def three(out_ap, wcols, h_hi, h_lo, start, stop):
                mm(out_ap, wh[:, wcols[0], wcols[1]:wcols[1] + P], h_hi, start=start, stop=False)
                mm(out_ap, wh[:, wcols[0], wcols[1]:wcols[1] + P], h_lo, start=False, stop=False)
                return mm(out_ap, wl[:, wcols[0], wcols[1]:wcols[1] + P], h_hi, start=False, stop=stop)

            def gate_rows(g, e):
                pe.wait_ge(const_ready, 3)
                if e == 0:
                    pe.wait_ge(gT_ready, g + 1)
                apart(pe, gb_ready, 8 * g + e)
                mm(psC[:, 0, :], pick[:, e, :], gT[:, g, :], start=True, stop=True).then_inc(gb_ps, 1)

            def up(g, n):
                e, f = divmod(n, FC)
                if f == 0:
                    pe.wait_ge(wsplit, e + 1)
                    if e == 0:
                        pe.wait_ge(hsplit, g + 1)
                need(pe, hid_ready, CHUNKS * g + n - 1)
                three(psA[:, n % 2, :], (e, f * P), hh[:, g, :], hl[:, g, :], True, True).then_inc(hid_ps, 1)

            def down(g, n):
                e, f = divmod(n, FC)
                pe.wait_ge(hid_split, CHUNKS * g + n + 1)
                if f == 0:
                    need(pe, part_ready, 8 * g + e - 1)
                three(psB[:, e % 2, :], (e, FF + f * P), hidh[:, n % 4, :], hidl[:, n % 4, :], f == 0, f == FC - 1)\
                    .then_inc(y_ps, 1)

            def sum_T(g):
                pe.wait_ge(y_sum, 7 * g + 7)
                for t in range(BTILES):
                    last = tr(psC[:, 1, t * P:(t + 1) * P], ysum[:, t * P:(t + 1) * P], ident[:, :])
                last.then_inc(yT_ps, 1)

            def pre(n, par, step):
                if step == "xT":
                    pe.wait_ge(xcopy_ready, n + 1)
                    need(pe, qT_ready, 2 * n)
                    for j in range(2):
                        last = tr(psD[:, 0, j * P:(j + 1) * P], pr_n[:, j, :], ident[:, :])
                    last.then_inc(xT_ps, 1)
                elif step in ("mlp1a", "mlp1b"):
                    b = 1 if step == "mlp1a" else 0
                    if b == 1:
                        pe.wait_ge(xT_ready, n + 1)
                        pe.wait_ge(mlp_in[par], mlp_count(n, par))
                        need(pe, out_ready, n - 2 + OUT_CREDIT)
                    for k in range(2):
                        f = 2 * (1 - b) + k
                        last = mm(psD[:, b, k * T:(k + 1) * T], wmlp[par][:, f * P:(f + 1) * P], pr_t[:, :],
                                  start=True, stop=True)
                    last.then_inc(ghid_ps, 1)
                elif step == "mlp2":
                    pe.wait_ge(ghid_ready, 2 * (n + 1))
                    for j in range(2):
                        for f in range(FC):
                            last = mm(psD[:, 1, j * P:(j + 1) * P], ghid[:, f, j * P:(j + 1) * P],
                                      wmlp[par][:, FF + f * P:FF + (f + 1) * P], start=f == 0, stop=f == FC - 1)
                    last.then_inc(mlp_ps, 1)
                elif step == "aT":
                    pe.wait_ge(anorm, n + 1)
                    for j in range(2):
                        last = tr(psD[:, 0, j * P:(j + 1) * P], pr_r[:, j, :], ident[:, :])
                    last.then_inc(aT_ps, 1)
                elif step == "qkv":
                    pe.wait_ge(aT_ready, n + 1)
                    if isinstance(n, int) and n == 0:
                        pe.wait_ge(att_in, 48)
                    need(pe, fstat, n - 1)
                    for j in range(2):
                        last = mm(psD[:, 1 - j, 0:3 * D], pr_t[:, j * P:(j + 1) * P], watt[:, 0:3 * D],
                                  start=True, stop=True)
                    last.then_inc(qkv_ps, 1)
                elif step in ("kT", "qT"):
                    pe.wait_ge(stack_ready, n + 1)
                    need(pe, fT_ready if step == "kT" else fhid_ready, n - 1 if step == "kT" else 2 * (n - 1))
                    if step == "qT":
                        pe.wait_ge(kT_ready, 2 * (n + 1))
                    qk_ = 1 if step == "kT" else 0
                    for b in (1, 0):
                        for k in range(2):
                            gr = 2 * (1 - b) + k
                            for j in range(2):
                                src = stack[par][:, j, qk_, GROUP * gr:GROUP * (gr + 1), :].bitcast(F32)
                                last = tr(psD[:, b, k * T + j * P:k * T + (j + 1) * P],
                                          src.rearrange("p h c -> p (h c)"), ident[:, :])
                        last.then_inc(kT_ps if step == "kT" else qT_ps, 1)

            def post(m, with_pre, step):
                if step == "wo":
                    pe.wait_ge(ctx_ready, 2 * (m + 1))
                    if with_pre:
                        pe.wait_ge(mstat, m + 3)
                    else:
                        pe.wait_ge(out_ready, m + OUT_CREDIT)
                    for j in range(2):
                        last = mm(psD[:, 1, j * P:(j + 1) * P], ctxT[:, j * P:(j + 1) * P], watt[:, 3 * D:4 * D],
                                  start=True, stop=True)
                    last.then_inc(wo_ps, 1)
                elif step == "fT":
                    pe.wait_ge(fnorm, m + 1)
                    if with_pre:
                        pe.wait_ge(qkv_ready, m + 3)
                    for j in range(2):
                        last = tr(psD[:, 1, j * P:(j + 1) * P], po_n[:, j, :], ident[:, :])
                    last.then_inc(fT_ps, 1)
                elif step == "ffn1":
                    pe.wait_ge(fT_ready, m + 1)
                    if with_pre:
                        pe.wait_ge(kT_ready, 2 * (m + 3))
                    for b in (1, 0):
                        for k in range(2):
                            f = 2 * (1 - b) + k
                            last = mm(psD[:, b, k * T:(k + 1) * T], wffn[:, f * P:(f + 1) * P], po_t[:, :],
                                      start=True, stop=True)
                        last.then_inc(fhid_ps, 1)
                elif step == "ffn2":
                    pe.wait_ge(fhid_ready, 2 * (m + 1))
                    if with_pre:
                        pe.wait_ge(qT_ready, 2 * (m + 3))
                    for j in range(2):
                        for f in range(FC):
                            last = mm(psD[:, 1, j * P:(j + 1) * P], fhid[:, f, j * P:(j + 1) * P],
                                      wffn[:, FF + f * P:FF + (f + 1) * P], start=f == 0, stop=f == FC - 1)
                    last.then_inc(ffn_ps, 1)

            def scores(s, par, k):
                if k == 0:
                    pe.wait_ge(qT_ready, 2 * (s + 1))
                need(pe, max_ready, 8 * s + k)
                for i in range(2):
                    gr, r = divmod(2 * k + i, GROUP)
                    rows_ = slice(SLOT * r, SLOT * r + 24)
                    mm(psA[:, i, P:3 * P], ident16[:, :], mask_qk[:, :], start=True, stop=False, skip_group_check=True)
                    mm(psA[:, i, 0:2 * P], qT[par][rows_, gr, P:2 * P], kT[par][rows_, gr, :],
                       start=False, stop=False, skip_group_check=True)
                    last = mm(psA[:, i, 2 * P:4 * P], qT[par][rows_, gr, 0:P], kT[par][rows_, gr, :],
                              start=False, stop=True, skip_group_check=True)
                last.then_inc(s_ps, 1)

            def queries_with_max(s, par, gr):
                pe.wait_ge(m_ready, 4 * s + gr + 1)
                need(pe, qmT_ready, 4 * s + gr)
                if isinstance(s, int) and s == 0:
                    pe.wait_ge(x1_ready, BLOCKS)
                for j in range(2):
                    src = stack[par][:, j, 0, GROUP * gr:GROUP * (gr + 1), :].bitcast(F32)
                    last = tr(psC[:, 1, j * P:(j + 1) * P], src.rearrange("p h c -> p (h c)"), ident[:, :])
                last.then_inc(qmT_ps, 1)

            def scores_t(s, par, k):
                pe.wait_ge(qmT_ready, 4 * s + k // 2 + 1)
                need(pe, prob_ready, 8 * s + k)
                if isinstance(s, int) and (s, k) == (0, 0):
                    pe.wait_ge(part_ready, E * BLOCKS)
                for i in range(2):
                    gr, r = divmod(2 * k + i, GROUP)
                    rows_ = slice(SLOT * r, SLOT * r + 26)
                    mm(psB[:, i, P:3 * P], ident16[:, :], mask_kq[:, :], start=True, stop=False, skip_group_check=True)
                    mm(psB[:, i, 0:2 * P], kT[par][rows_, gr, P:2 * P], qmT[rows_, gr % 2, :],
                       start=False, stop=False, skip_group_check=True)
                    last = mm(psB[:, i, 2 * P:4 * P], kT[par][rows_, gr, 0:P], qmT[rows_, gr % 2, :],
                              start=False, stop=True, skip_group_check=True)
                last.then_inc(t_ps, 1)

            def context(s, par, k):
                if k % 4 == 0:
                    need(pe, ctx_copied, 2 * s + k // 4)
                    if isinstance(s, int) and (s, k) == (0, 0):
                        pe.wait_ge(gb_ready, E * BLOCKS)
                pe.wait_ge(prob_ready, 8 * s + k + 1)
                for i in range(2):
                    h = 2 * k + i
                    c = T * (h // 8)
                    mm(psC[:, 0, c:c + T], vm[par][:, 0, h, :], prob[:, k % 2, i, P:3 * P],
                       start=h % 8 == 0, stop=False, skip_group_check=True)
                    last = mm(psC[:, 0, c + P:c + T], vm[par][:, 1, h, :], prob[:, k % 2, i, 0:P],
                              start=False, stop=h % 8 == 7, skip_group_check=True)
                last.then_inc(pv_ps, 1)

            def attention(s, par, k, part_, first, last):
                if first and (k, part_) == (1, 0):
                    sum_T(BLOCKS - 1)
                if part_ == 0:
                    if not last:
                        scores(s, par, k)
                    if k % 2 == 0:
                        if k >= 2 and not last:
                            queries_with_max(s, par, k // 2 - 1)
                        elif k == 0 and not first:
                            queries_with_max(s - 1, 1 - par, 3)
                elif part_ == 1:
                    if k >= 3 and not last:
                        scores_t(s, par, k - 3)
                    elif k < 3 and not first:
                        scores_t(s - 1, 1 - par, k + 5)
                else:
                    if k >= 4 and not last:
                        context(s, par, k - 4)
                    elif k < 4 and not first:
                        context(s - 1, 1 - par, k + 4)

            def moe(g, first, ahead):
                for n in range(CHUNKS):
                    up(g, n)
                    if n >= DOWN_LAG:
                        down(g, n - DOWN_LAG)
                    elif not first:
                        down(g - 1, n - DOWN_LAG + CHUNKS)
                    if n % FC == GATE_AT % FC:
                        e = (n - GATE_AT) // FC
                        if e >= 0:
                            gate_rows(g, e)
                        elif not first:
                            gate_rows(g - 1, e + E)
                    if n == LAST_T and not first:
                        sum_T(g - 1)
                    if first and n == 4:
                        norm_gT(0)
                    if ahead and n == NORM["nT"]:
                        norm_nT(g + 1)
                    if ahead and n == NORM["logits"]:
                        norm_logits(g + 1)
                    if ahead and n == NORM["gT_ps"]:
                        norm_gT(g + 1)
                    if not ahead:
                        for step in ("xT", "mlp1a", "mlp1b", "mlp2", "aT", "qkv", "kT", "qT"):
                            if n == FIRST["qkv_mm" if step == "qkv" else step]:
                                pre(0, 0, step)

            moe(0, True, True)
            with pe.Fori(1, BLOCKS - 1) as g:
                moe(g, False, True)
            moe(BLOCKS - 1, False, False)
            for n in range(CHUNKS - DOWN_LAG, CHUNKS):
                down(BLOCKS - 1, n)
            gate_rows(BLOCKS - 1, E - 1)
            pe.wait_ge(const_ready, 4)

            PRE = [(1, "xT"), (3, "mlp1a"), (4, "mlp1b"), (6, "mlp2"), (11, "aT"), (13, "qkv"), (17, "kT"),
                   (20, "qT")]
            POST = [(12, "wo"), (16, "fT"), (18, "ffn1"), (22, "ffn2")]
            sequences(pe, None, PRE, POST, pre, post, attention, True)

        @block.scalar
        def _(act):
            a_ = nc.scalar.activation
            chain = Chain(act, act_step, "act", need)
            act.wait_ge(trig_in, 1)
            chain.step(a_(trig[:, 4, :], trig[:, 2, :], ACT.Sin))
            a_(trig[:, 5, :], trig[:, 3, :], ACT.Sin).then_inc(trig_ready, 1)
            act.wait_ge(cond_pe, 3)
            a_(cond_b[:, :], psD[:, 1, 128:136], ACT.Relu, bias=col("hyp_b1")).then_inc(cond_act, 1)
            act.wait_ge(cond_pe, 4)
            a_(cond_c[:, :], psD[:, 1, 136:144], ACT.Identity, bias=col("hyp_b2")).then_inc(cond_act, 1)
            act.wait_ge(cond_pe, 5)
            a_(cond_d[0:SE, :], psD[0:SE, 1, 144:152], ACT.Relu, bias=styb1[:, :]).then_inc(cond_act, 1)
            def norm_hT(a):
                act.wait_ge(nT_ps, a + 1)
                a_(hT[:, :], psC[:, 1, :], ACT.Identity, bias=col("ln_b"), scale=col("ln_g")).then_inc(hT_ready, 1)

            def norm_exp(a):
                act.wait_ge(shifted, a + 1)
                a_(probs[:, :, :], probs[:, :, :], ACT.Exp).then_inc(exps, 1)

            def norm_gT(a):
                act.wait_ge(gT_ps, a + 1)
                a_(gT[:, a, :], psD[0:3 * E, 0, 0:256].bitcast(BF16), ACT.Copy).then_inc(gT_ready, 1)

            def weights_high(e):
                act.wait_ge(moe_in[e], 16)
                a_(wh[:, e, :], raw[:, e, :], ACT.Copy).then_inc(whigh, 1)

            act.wait_ge(cond_dve, 3)
            chain.link(a_(sp_t[:, 2, :], sp_t[:, 1, :], ACT.Exp, scale=-1.0))
            a_(sp_t[:, 3, :], sp_t[:, 2, :], ACT.Ln, bias=1.0).then_inc(cond_act, 1)

            weights_high(0)
            norm_hT(0)
            weights_high(1)
            weights_high(2)
            norm_exp(0)
            weights_high(3)

            def gate_rows(g, e):
                act.wait_ge(gb_ps, 8 * g + e + 1)
                need(act, part_ready, 8 * g + e - 1)
                a_(gb[:, e % 2, :], psC[:, 0, :], ACT.Copy).then_inc(gb_ready, 1)

            def pre(n, par, step):
                if step == "xT":
                    act.wait_ge(xT_ps, n + 1)
                    a_(pr_t[:, :], psD[:, 0, 0:T], ACT.Copy).then_inc(xT_ready, 1)
                elif step in ("gelu_a", "gelu_b"):
                    b = 1 if step == "gelu_a" else 0
                    act.wait_ge(ghid_ps, 2 * n + 2 - b)
                    for k in range(2):
                        f = 2 * (1 - b) + k
                        ins = a_(ghid[:, f, :], psD[:, b, k * T:(k + 1) * T], ACT.Gelu,
                                 bias=bi_col[:, f, bass.ds(n, 1)])
                    ins.then_inc(ghid_ready, 1)
                elif step == "aT":
                    act.wait_ge(aT_ps, n + 1)
                    a_(pr_t[:, :], psD[:, 0, 0:T], ACT.Identity, bias=col("beta1"), scale=col("gamma1"))\
                        .then_inc(aT_ready, 1)
                elif step in ("kT", "qT"):
                    for b in (1, 0):
                        act.wait_ge(kT_ps if step == "kT" else qT_ps, 2 * n + 2 - b)
                        dst = (kT if step == "kT" else qT)[par][:, 2 * (1 - b):2 * (2 - b), :]
                        a_(dst, psD[:, b, :].rearrange("p (g t) -> p g t", g=2), ACT.Copy)\
                            .then_inc(kT_ready if step == "kT" else qT_ready, 1)

            def post(m, with_pre, step):
                if step in ("ctx_a", "ctx_b"):
                    half = 0 if step == "ctx_a" else 1
                    act.wait_ge(pv_ps, 8 * m + 4 * (half + 1))
                    cols = slice(T * half, T * (half + 1))
                    a_(ctx_sb[:, cols], psC[:, 0, cols], ACT.Copy).then_inc(ctx_copied, 1)
                elif step == "fT":
                    act.wait_ge(fT_ps, m + 1)
                    a_(po_t[:, :], psD[:, 1, 0:T], ACT.Identity, bias=col("beta2"), scale=col("gamma2"))\
                        .then_inc(fT_ready, 1)
                elif step == "gelu":
                    for b in (1, 0):
                        act.wait_ge(fhid_ps, 2 * m + 2 - b)
                        for k in range(2):
                            f = 2 * (1 - b) + k
                            ins = a_(fhid[:, f, :], psD[:, b, k * T:(k + 1) * T], ACT.Gelu, bias=col("ffn_b1", f))
                        ins.then_inc(fhid_ready, 1)

            def exp_t(s, k):
                act.wait_ge(t_ps, 8 * s + k + 1)
                need(act, pv_ps, 8 * s + k - 1)
                a_(prob[:, k % 2], psB[:, :, P:4 * P], ACT.Exp, scale=scale).then_inc(prob_ready, 1)

            def queries(s, gr):
                act.wait_ge(qmT_ps, 4 * s + gr + 1)
                need(act, t_ps, 8 * s + 2 * gr - 2)
                a_(qmT[:, gr % 2, :], psC[:, 1, 0:T], ACT.Copy).then_inc(qmT_ready, 1)

            def attention(s, par, k, part_, first, last):
                if part_ == 0 and k % 2 == 0:
                    if k >= 2 and not last:
                        queries(s, k // 2 - 1)
                    elif k == 0 and not first:
                        queries(s - 1, 3)
                elif part_ == 1:
                    if k >= 3 and not last:
                        exp_t(s, k - 3)
                    elif k < 3 and not first:
                        exp_t(s - 1, k + 5)

            def moe(g, first, ahead):
                for n in range(CHUNKS):
                    act.wait_ge(hid_ps, CHUNKS * g + n + 1)
                    need(act, hid_split, CHUNKS * g + n - 3)
                    a_(hid[:, n % 4, :], psA[:, n % 2, :], ACT.Relu, bias=col("b1", n)).then_inc(hid_ready, 1)
                    if high_on_act(n):
                        act.wait_ge(hid_ready, CHUNKS * g + n + 1)
                        need(act, y_ps, CHUNKS * g + n - 3)
                        a_(hidh[:, n % 4, :], hid[:, n % 4, :], ACT.Copy).then_inc(hid_high, 1)
                    if first and n in (0, 1, 2, 3):
                        weights_high(n + 4)
                    if first and n == 4:
                        norm_gT(0)
                    if n % FC == GATE_AT % FC:
                        e = (n - GATE_AT) // FC
                        if e >= 0:
                            gate_rows(g, e)
                        elif not first:
                            gate_rows(g - 1, e + E)
                    if ahead and n == NORM["hT"]:
                        norm_hT(g + 1)
                    if ahead and n == NORM["exp"]:
                        norm_exp(g + 1)
                    if ahead and n == NORM["gT"]:
                        norm_gT(g + 1)
                    if not ahead:
                        for step in ("xT", "gelu_a", "gelu_b", "aT", "kT", "qT"):
                            if n == FIRST[step]:
                                pre(0, 0, step)

            moe(0, True, True)
            with act.Fori(1, BLOCKS - 1) as g:
                moe(g, False, True)
            moe(BLOCKS - 1, False, False)
            gate_rows(BLOCKS - 1, E - 1)

            PRE = [(2, "xT"), (4, "gelu_a"), (5, "gelu_b"), (12, "aT"), (18, "kT"), (21, "qT")]
            POST = [(0, "ctx_a"), (11, "ctx_b"), (17, "fT"), (19, "gelu")]
            sequences(act, None, PRE, POST, pre, post, attention, True)

        @block.vector
        def _(dve):
            v_ = nc.vector
            chain = Chain(dve, dve_step, "dve", need)

            def layer_stats(src, st, out_mv, count, done):
                for t in range(count):
                    chain.step(v_.bn_stats(st[:, t, :], src(t)))
                apart(dve, chain.sem, chain.base + chain.n)
                for t in range(count):
                    ins = v_.bn_aggr(out_mv[:, t, :], st[:, t, :])
                    if t < count - 1:
                        chain.step(ins)
                ins.then_inc(done, 1)

            def layer_norm(src, mv_, rs, dst, count, done):
                for t in range(count):
                    ins = v_.tensor_scalar(dst(t), src(t), mv_[:, t, 0:1], rs[:, t:t + 1], ALU.subtract, ALU.mult)
                    if t < count - 1:
                        chain.step(ins)
                ins.then_inc(done, 1)

            def norm_stats(a):
                if isinstance(a, int) and a == 0:
                    dve.wait_ge(x_in0, 16)
                else:
                    dve.wait_ge(x_in, 48)
                layer_stats(lambda t: X[:, BTILES * a + t, :], stats, mv, BTILES, stat_ready)

            def norm_normed(a):
                dve.wait_ge(rstd_ready, a + 1)
                need(dve, nT_ps, a)
                layer_norm(lambda t: X[:, BTILES * a + t, :], mv, rstd, lambda t: normed[:, t, :], BTILES, normed_ready)

            def norm_tstats(a):
                dve.wait_ge(hT_ready, a + 1)
                layer_stats(lambda j: hT[:, j * T:(j + 1) * T], tstats, tmv, 2, tstat_ready)

            def norm_h2(a):
                dve.wait_ge(tscale_ready, a + 1)
                need(dve, logits_ps, a)
                for j in range(2):
                    ins = v_.tensor_scalar(h2[:, j * T:(j + 1) * T], hT[:, j * T:(j + 1) * T], tscale[:, j:j + 1],
                                           tshift[:, j:j + 1], ALU.mult, ALU.add)
                    if j == 0:
                        chain.step(ins)
                ins.then_inc(h2_ready, 1)
                dve.wait_ge(h2_ready, a + 1)
                chain.link(v_.tensor_copy(hh[:, a, :], h2[:, :]))
                v_.tensor_tensor(hl[:, a, :], h2[:, :], hh[:, a, :].bitcast(F32), ALU.subtract).then_inc(hsplit, 1)

            def norm_shift(a):
                dve.wait_ge(logits_ps, a + 1)
                lg = psD[:, 0, 0:BTILES * E].rearrange("p (t e) -> p t e", t=BTILES)
                chain.link(v_.tensor_reduce(lmax[:, :], lg, AX_X, ALU.max))
                v_.tensor_tensor(probs[:, :, :], lg, lmax[:, :].unsqueeze(2).to_broadcast([P, BTILES, E]),
                                 ALU.subtract).then_inc(shifted, 1)

            def norm_gates(a, at):
                wide = [P, BTILES, E]
                pj = probs[:, :, :].unsqueeze(2).to_broadcast([P, BTILES, E, E])
                pe_ = probs[:, :, :].unsqueeze(3).to_broadcast([P, BTILES, E, E])
                if at == 0:
                    dve.wait_ge(exps, a + 1)
                    chain.link(v_.tensor_reduce(psums[:, :], probs[:, :, :], AX_X, ALU.add))
                    chain.link(v_.reciprocal(psums[:, :], psums[:, :]))
                    chain.link(v_.tensor_tensor(probs[:, :, :], probs[:, :, :],
                                                psums[:, :].unsqueeze(2).to_broadcast(wide), ALU.mult))
                elif at == 1:
                    if isinstance(a, int) and a == 0:
                        dve.wait_ge(const_ready, 2)
                    chain.step(v_.tensor_tensor(above[:, :, :, :], pj, pe_, ALU.is_gt))
                    chain.link(v_.tensor_tensor(equal[:, :, :, :], pj, pe_, ALU.is_equal))
                elif at == 2:
                    chain.link(v_.tensor_tensor(equal[:, :, :, :], equal[:, :, :, :],
                                                before[:, :, :].unsqueeze(1).to_broadcast([P, BTILES, E, E]), ALU.mult))
                    chain.link(v_.tensor_tensor(above[:, :, :, :], above[:, :, :, :], equal[:, :, :, :], ALU.add))
                elif at == 3:
                    chain.link(v_.tensor_reduce(rank[:, :, :], above[:, :, :, :], AX_X, ALU.add))
                    chain.link(v_.scalar_tensor_tensor(out=gates[:, :, :], in0=rank[:, :, :], scalar=2.0,
                                                       in1=probs[:, :, :], op0=ALU.is_lt, op1=ALU.mult))
                elif at == 4:
                    chain.link(v_.tensor_reduce(psums[:, :], gates[:, :, :], AX_X, ALU.add))
                    chain.link(v_.reciprocal(psums[:, :], psums[:, :]))
                    chain.link(v_.tensor_tensor(gates[:, :, :], gates[:, :, :],
                                                psums[:, :].unsqueeze(2).to_broadcast(wide), ALU.mult))
                else:
                    k = at - 5
                    ins = v_.tensor_copy(gparts[:, :, k * E:(k + 1) * E], gates[:, :, :])
                    if k < 2:
                        chain.link(ins)
                        chain.link(v_.tensor_tensor(gates[:, :, :], gates[:, :, :], gparts[:, :, k * E:(k + 1) * E],
                                                    ALU.subtract))
                    else:
                        ins.then_inc(gparts_ready, 1)

            dve.wait_ge(ang_in, 16)
            magic = 12582912.0
            chain.link(v_.tensor_scalar(trig[:, 0, :], ang[:, 0:16], 1.0 / (2 * PI), magic, ALU.mult, ALU.add))
            chain.link(v_.tensor_scalar(trig[:, 0, :], trig[:, 0, :], magic, None, ALU.subtract))
            chain.link(v_.scalar_tensor_tensor(out=trig[:, 1, :], in0=trig[:, 0, :], scalar=-6.28125, in1=ang[:, 0:16],
                                               op0=ALU.mult, op1=ALU.add))
            chain.link(v_.scalar_tensor_tensor(out=trig[:, 1, :], in0=trig[:, 0, :], scalar=-(2 * PI - 6.28125),
                                               in1=trig[:, 1, :], op0=ALU.mult, op1=ALU.add))
            chain.link(v_.tensor_scalar(trig[:, 2, :], trig[:, 1, :], 3.1415925, -3.1415925, ALU.min, ALU.max))
            chain.link(v_.tensor_scalar(trig[:, 0, :], trig[:, 1, :], PI / 2, -2 * PI, ALU.is_gt, ALU.mult))
            chain.link(v_.tensor_tensor(trig[:, 3, :], trig[:, 1, :], trig[:, 0, :], ALU.add))
            chain.link(v_.tensor_scalar(trig[:, 3, :], trig[:, 3, :], PI / 2, 3.1415925, ALU.add, ALU.min))
            v_.tensor_scalar(trig[:, 3, :], trig[:, 3, :], -3.1415925, None, ALU.max).then_inc(trig_in, 1)
            dve.wait_ge(const_ready, 1)
            dve.wait_ge(ids_in, 16)
            chain.link(v_.tensor_copy(idf[:, :], idall[:, :]))
            chain.step(v_.tensor_scalar(onehot[:, :], idf[:, 0:8], rowno[0:SUBJECTS, :], None, ALU.is_equal))
            v_.tensor_scalar(onehot_x[:, :], idf[0:E, 8:16], rowno[0:E, :], None, ALU.is_equal).then_inc(cond_dve, 1)
            v_.memset(out_credit[:, :], 0.0).then_inc(out_ready, OUT_CREDIT)
            dve.wait_ge(cond_pe, 1)
            chain.step(v_.tensor_copy(pcol[:, :], psD[:, 0, 0:NROWS]))
            dve.wait_ge(cond_pe, 2)
            v_.tensor_copy(cond_a[0:SE, :], psD[0:SE, 1, 0:8]).then_inc(cond_dve, 1)
            norm_stats(0)
            dve.wait_ge(trig_ready, 1)
            for k in range(2):
                sin_, cos_ = trig[:, 4, 8 * k:8 * k + 8], trig[:, 5, 8 * k:8 * k + 8]
                chain.step(v_.tensor_copy(rot_s[:, :, 2 * k], sin_))
                chain.step(v_.tensor_scalar(rot_s[:, :, 2 * k + 1], sin_, -1.0, None, ALU.mult))
                chain.step(v_.tensor_copy(rot_c[:, :, 2 * k], cos_))
                chain.step(v_.tensor_copy(rot_c[:, :, 2 * k + 1], cos_))
            dve.wait_ge(cond_pe, 6)
            chain.settle()
            chain.step(v_.tensor_scalar(bet[:, :], psD[:, 1, 160:168], col("sty_b2", 1), None, ALU.add))
            chain.link(v_.tensor_scalar(sp_t[:, 0, :], psD[:, 1, 152:160], col("sty_b2"), None, ALU.add))
            chain.link(v_.tensor_scalar(sp_t[:, 1, :], sp_t[:, 0, :], -1.0, None, ALU.mult))
            v_.tensor_tensor(sp_t[:, 1, :], sp_t[:, 0, :], sp_t[:, 1, :], ALU.max).then_inc(cond_dve, 1)
            norm_normed(0)
            dve.wait_ge(cond_act, 4)
            u, lw, w1, q = (sp_t[:, i, :] for i in (2, 3, 4, 5))
            chain.link(v_.tensor_scalar(w1, u, 1.0, -1.0, ALU.add, ALU.add))
            chain.link(v_.tensor_scalar(q, w1, 1e-30, None, ALU.max))
            chain.link(v_.reciprocal(q, q))
            chain.link(v_.tensor_tensor(q, q, u, ALU.mult))
            chain.link(v_.tensor_tensor(q, q, lw, ALU.mult))
            chain.link(v_.scalar_tensor_tensor(out=w1, in0=w1, scalar=0.0, in1=u, op0=ALU.is_equal, op1=ALU.mult))
            chain.link(v_.tensor_tensor(q, q, w1, ALU.add))
            chain.link(v_.scalar_tensor_tensor(out=q, in0=sp_t[:, 0, :], scalar=0.0, in1=q, op0=ALU.max, op1=ALU.add))
            v_.tensor_scalar(gam[:, :], q, 1e-8, None, ALU.add).then_inc(cond_dve, 1)
            norm_tstats(0)
            norm_h2(0)
            dve.wait_ge(cond_pe, 7)
            chain.step(v_.tensor_copy(bi_col[:, :, :], psD[:, 1, 64:96].rearrange("p (f s) -> p f s", f=FC)))
            norm_shift(0)

            def split_hidden(g, n):
                dve.wait_ge(hid_ready, CHUNKS * g + n + 1)
                if high_on_act(n):
                    dve.wait_ge(hid_high, HIGHS * g + sum(map(high_on_act, range(n + 1))))
                else:
                    need(dve, y_ps, CHUNKS * g + n - 3)
                    chain.link(v_.tensor_copy(hidh[:, n % 4, :], hid[:, n % 4, :]))
                v_.tensor_tensor(hidl[:, n % 4, :], hid[:, n % 4, :], hidh[:, n % 4, :].bitcast(F32), ALU.subtract)\
                    .then_inc(hid_split, 1)

            def gated(g, e):
                dve.wait_ge(y_ps, CHUNKS * g + FC * (e + 1))
                dve.wait_ge(gb_ready, 8 * g + e + 1)
                need(dve, y_sum, 7 * g + (max(e - 2, 1) if e >= 2 else e - 1))
                v_.scalar_tensor_tensor(out=part[:, e % 2, :], in0=psB[:, e % 2, :], scalar=col("b2", e),
                                        in1=gb[:, e % 2, :], op0=ALU.add, op1=ALU.mult).then_inc(part_ready, 1)

            def add_sum(g):
                dve.wait_ge(yT_ps, g + 1)
                xs = X[:, bass.ds(BTILES * g, BTILES), :]
                v_.tensor_tensor(xs, psC[:, 1, :].rearrange("p (t d) -> p t d", t=BTILES), xs, ALU.add)\
                    .then_inc(x1_ready, 1)

            def pre(n, par, step):
                if step == "xcopy":
                    dve.wait_ge(rotated, 1 if isinstance(n, int) and n < 2 else BLOCKS)
                    need(dve, x3_ready, n)
                    v_.tensor_copy(pr_n[:, :, :], X[:, bass.ds(2 * n, 2), :]).then_inc(xcopy_ready, 1)
                elif step == "stats":
                    dve.wait_ge(mlp_ps, n + 1)
                    dve.wait_ge(xbo_ready, n + 1)
                    chain.link(v_.tensor_tensor(pr_r[:, :, :], psD[:, 1, 0:T].rearrange("p (j d) -> p j d", j=2),
                                                pr_b[:, :, :], ALU.add))
                    layer_stats(lambda j: pr_r[:, j, :], pr_st, pr_mv, 2, mstat)
                elif step == "norm":
                    dve.wait_ge(mrstd, n + 1)
                    layer_norm(lambda j: pr_r[:, j, :], pr_mv, pr_rs, lambda j: pr_n[:, j, :], 2, mnorm)
                elif step == "affine":
                    dve.wait_ge(mnorm, n + 1)
                    dve.wait_ge(mlp_in[par], mlp_count(n, par))
                    chain.link(v_.tensor_tensor(pr_n[:, :, :], pr_n[:, :, :],
                                                mrow[par][:, D:2 * D].unsqueeze(1).to_broadcast([P, 2, D]), ALU.mult))
                    v_.tensor_tensor(X[:, bass.ds(2 * n, 2), :], pr_n[:, :, :],
                                     mrow[par][:, 2 * D:3 * D].unsqueeze(1).to_broadcast([P, 2, D]), ALU.add)\
                        .then_inc(x3_ready, 1)
                elif step == "astats":
                    apart(dve, x3_ready, n + 1)
                    layer_stats(lambda j: X[:, 2 * n + j, :], pr_st, pr_mv, 2, astat)
                elif step == "anorm":
                    dve.wait_ge(arstd, n + 1)
                    layer_norm(lambda j: X[:, 2 * n + j, :], pr_mv, pr_rs, lambda j: pr_r[:, j, :], 2, anorm)
                elif step == "qkv":
                    dve.wait_ge(qkv_ps, n + 1)
                    dve.wait_ge(values_clear, par + 1)
                    if isinstance(n, int) and n == 0:
                        dve.wait_ge(att_in, 48)
                    need(dve, pv_ps, 8 * (n - 1))
                    for j in range(2):
                        ps = psD[:, 1 - j, :]
                        chain.step(v_.tensor_tensor(qk[:, j].rearrange("p q h d -> p (q h d)"), ps[:, 0:2 * D],
                                                    arow[:, 0:2 * D], ALU.add))
                        for q in range(2):
                            c = 2 * D + 64 * q
                            base = vm[par][:, j, 8 * q:8 * (q + 1), :].rearrange("p h c -> p (h c)")
                            diag = diagonal(base)
                            ins = v_.tensor_tensor(diag, ps[:, c:c + 64].rearrange("p (h d) -> p h d", h=8),
                                                   arow[:, c:c + 64].rearrange("p (h d) -> p h d", h=8), ALU.add)
                            if (j, q) != (1, 1):
                                chain.step(ins)
                    ins.then_inc(qkv_ready, 1)
                elif step == "stack":
                    dve.wait_ge(qkv_ready, n + 1)
                    dve.wait_ge(stack_clear, par + 1)
                    need(dve, qmT_ps, 4 * (n - 1))
                    st = stack[par]
                    hi = st[:, :, :, :, 0:DH].rearrange("p j q h c -> p (j q h) c")
                    chain.link(v_.tensor_copy(hi, qk[:, :, :, :, :].rearrange("p j q h d -> p (j q h) d")))
                    for q, lo, dup in ((0, DH, 2 * DH), (1, 2 * DH, DH)):
                        h_ = st[:, :, q, :, 0:DH].bitcast(F32)
                        chain.step(v_.tensor_tensor(st[:, :, q, :, lo:lo + DH], qk[:, :, q], h_, ALU.subtract))
                        ins = v_.tensor_copy(st[:, :, q, :, dup:dup + DH], h_)
                        if q == 0:
                            chain.step(ins)
                    ins.then_inc(stack_ready, 1)

            def post(m, with_pre, step):
                if step in ("ctx_a", "ctx_b"):
                    half = 0 if step == "ctx_a" else 1
                    cols = slice(T * half, T * (half + 1))
                    dve.wait_ge(ctx_copied, 2 * m + half + 1)
                    chain.link(v_.reciprocal(rden[:, cols], ctx_sb[64:128, cols]))
                    v_.tensor_tensor(ctxT[64 * half:64 * (half + 1), :], ctx_sb[0:64, cols], rden[:, cols],
                                     ALU.mult).then_inc(ctx_ready, 1)
                elif step == "x4":
                    dve.wait_ge(wo_ps, m + 1)
                    dve.wait_ge(xb4_ready, m + 1)
                    chain.link(v_.tensor_tensor(po_x[:, :, :], psD[:, 1, 0:T].rearrange("p (j d) -> p j d", j=2),
                                                po_b[:, :, :], ALU.add))
                    layer_stats(lambda j: po_x[:, j, :], po_st, po_mv, 2, fstat)
                elif step == "norm":
                    dve.wait_ge(frstd, m + 1)
                    layer_norm(lambda j: po_x[:, j, :], po_mv, po_rs, lambda j: po_n[:, j, :], 2, fnorm)
                elif step == "out":
                    dve.wait_ge(ffn_ps, m + 1)
                    dve.wait_ge(diff_ready, m + 1)
                    chain.link(v_.tensor_tensor(po_d[:, :, :], psD[:, 1, 0:T].rearrange("p (j d) -> p j d", j=2),
                                                po_d[:, :, :], ALU.add))
                    xs = X[:, bass.ds(2 * m, 2), :]
                    v_.scalar_tensor_tensor(out=xs, in0=po_d[:, :, :], scalar=ang[:, bass.ds(16 + m, 1)], in1=xs,
                                            op0=ALU.mult, op1=ALU.add).then_inc(out_ready, 1)

            def attention(s, par, k, part_, first, last):
                if first and (k, part_) == (1, 2):
                    add_sum(BLOCKS - 1)
                if part_ != 0 or last:
                    return
                dve.wait_ge(s_ps, 8 * s + k + 1)
                chain.step(v_.tensor_reduce(rmax[:, 1, 2 * k:2 * k + 2], psA[:, :, 0:T], AX_X, ALU.max))
                v_.tensor_reduce(rmax[:, 0, 2 * k:2 * k + 2], psA[:, :, T:T + P], AX_X, ALU.max)\
                    .then_inc(max_ready, 1)
                if k % 2:
                    dve.wait_ge(max_ready, 8 * s + k + 1)
                    hs = slice(2 * k - 2, 2 * k + 2)
                    mhi = stack[par][:, :, 0, hs, 24]
                    chain.link(v_.tensor_copy(mhi, rmax[:, :, hs]))
                    v_.tensor_tensor(stack[par][:, :, 0, hs, 25], rmax[:, :, hs], mhi.bitcast(F32), ALU.subtract)\
                        .then_inc(m_ready, 1)

            def moe(g, first, ahead):
                for n in range(CHUNKS):
                    split_hidden(g, n)
                    if n % FC == OUTPUT_AT % FC:
                        e = (n - OUTPUT_AT) // FC
                        if e >= 0:
                            gated(g, e)
                        elif not first:
                            gated(g - 1, e + E)
                    if n == LAST_X1 and not first:
                        add_sum(g - 1)
                    if first and n < 4:
                        norm_gates(0, 2 * n)
                        norm_gates(0, 2 * n + 1)
                    if ahead:
                        for name, fn in (("stats", norm_stats), ("normed", norm_normed), ("tstats", norm_tstats),
                                         ("h2", norm_h2), ("shift", norm_shift)):
                            if n == NORM[name]:
                                fn(g + 1)
                        if 0 <= n - NORM["gates"] < GATE_PARTS:
                            norm_gates(g + 1, n - NORM["gates"])
                    else:
                        for step in ("xcopy", "stats", "norm", "affine", "astats", "anorm", "qkv", "stack"):
                            if n == FIRST[step]:
                                pre(0, 0, step)

            moe(0, True, True)
            per, start = STEPS_OF_BLOCK["dve"], chain.base + chain.n
            with dve.Fori(1, BLOCKS - 1) as g:
                chain.enter(start + per * (g - 1))
                moe(g, False, True)
                assert chain.n == per, chain.n
            chain.enter(start + per * (BLOCKS - 2))
            moe(BLOCKS - 1, False, False)
            gated(BLOCKS - 1, E - 1)

            PRE = [(0, "xcopy"), (6, "stats"), (7, "norm"), (7, "affine"), (8, "astats"), (10, "anorm"),
                   (14, "qkv"), (15, "stack")]
            POST = [(0, "ctx_a"), (11, "ctx_b"), (13, "x4"), (14, "norm"), (23, "out")]
            sequences(dve, chain, PRE, POST, pre, post, attention, True)


def kernel(**inputs):
    import numpy as np
    import concourse.bacc as bacc
    from concourse.bass_utils import run_bass_kernel_spmd

    def get(name):
        return np.asarray(inputs[name])

    l0, l2, l3 = ((lambda n, p=p: get(p + n)) for p in ("L0_cond_", "L2_cond_", "L3_cond_"))

    def experts(w1, w2):
        w2 = w2.reshape(E, FC, P, D).transpose(0, 2, 1, 3).reshape(E, P, FC * D)
        return np.concatenate([w1, w2], axis=2)

    def side_by_side(*matrices):
        place = np.zeros((P, COND_COLS), np.float32)
        for m, (r, c, w) in zip(matrices, COND_PLACES):
            place[0:r, c:c + w] = m
        return place

    arrays = {
        "x": get("x"),
        "ids": np.concatenate([get("itok_B_6_14"), get("itok_B_0_7")]).reshape(1, 16),
        "angles": np.concatenate([get("condB_theta"), get("condB_phi"), get("condB_gatescore")]).reshape(1, 24),
        "rows": np.concatenate([a.reshape(-1, P) for a in (
            l0("exp_b1"), l0("exp_b2"), l0("ln_g"), l0("ln_b"), l3("b1"), l0("hyp_b1"), l0("hyp_b2"), l0("sty_b2"),
            l3("gamma1"), l3("beta1"), l3("gamma2"), l3("beta2"))]),
        "sty_b1": l0("sty_b1").reshape(SE, 1),
        "cond_w": side_by_side(l0("subj_emb"), l0("hyp_w1"), l0("hyp_w2"), l0("sty_w1"), l0("sty_w2"), l0("router_w")),
        "moe_w": experts(l0("exp_w1"), l0("exp_w2")),
        "mlp_w": experts(l2("Wi"), l2("Wo")),
        "mlp_rows": np.concatenate([l2("bo"), l2("gamma"), l2("beta")], axis=1),
        "mlp_bi": l2("bi"),
        "att_w": np.concatenate([l3("Wq"), l3("Wk"), l3("Wv"), l3("Wo"), l3("W1"),
                                 l3("W2").reshape(FC, P, D).transpose(1, 0, 2).reshape(P, FC * D)], axis=1),
        "att_rows": np.concatenate([l3("bq"), l3("bk"), l3("bv"), l3("bo"), l3("b2")]).reshape(1, 640),
    }
    arrays = {f"in_{n}": np.ascontiguousarray(a) for n, a in arrays.items()}
    nc = bacc.Bacc("TRN2", target_bir_lowering=False, num_devices=1)
    aps = [nc.dram_tensor(n, a.shape, mybir.dt.from_np(a.dtype), kind="ExternalInput").ap() for n, a in arrays.items()]
    out = nc.dram_tensor("out", (SEQS, T, D), F32, kind="ExternalOutput").ap()
    conditioned_stack(nc, *aps, out)
    r = run_bass_kernel_spmd(nc, [arrays], core_ids=[0])
    return r.results[0]["out"]
```

```python
from contextlib import ExitStack

import concourse.bass as bass
from concourse import mybir

F32 = mybir.dt.float32
F32R = mybir.dt.float32r
BF16 = mybir.dt.bfloat16
I32 = mybir.dt.int32
ALU = mybir.AluOpType
ACT = mybir.ActivationFunctionType
AX_X = mybir.AxisListType.X

P = 128
D = 128
SEQS, T = 8, 256
TILES = SEQS * T // P
BLOCKS, BT = 4, 512
BTILES = BT // P
E, FF = 8, 512
FC = FF // P
CHUNKS = E * FC
HEADS, DH = 16, 8
SLOT = 32
GROUP = P // SLOT
PAIRS = HEADS // 2
SLOTS = 3 * PAIRS
T_LAG, PV_LAG = 3, 4
SUBJECTS, SE = 32, 64
MASKED = -1e30
PI = 3.141592653589793

ROWS = ["b1"] * (E * FC) + ["b2"] * E + ["ln_g", "ln_b"] + ["ffn_b1"] * FC + \
       ["hyp_b1", "hyp_b2", "sty_b2", "sty_b2", "gamma1", "beta1", "gamma2", "beta2"]
COL = {name: ROWS.index(name) for name in ROWS}
NROWS = len(ROWS)

COND_SHAPES = [(SUBJECTS, SE), (SE, P), (P, P), (P, SE), (SE, 2 * D), (D, E)]
COND_PLACES = [(r, sum(w_ for _, w_ in COND_SHAPES[:i]), w) for i, (r, w) in enumerate(COND_SHAPES)]
COND_COLS = sum(w for _, w in COND_SHAPES)


class Chain:

    def __init__(self, eng, sem, name, wait):
        self.wait = wait
        self.eng, self.sem, self.name, self.base, self.n = eng, sem, name, 0, 0

    def step(self, ins):
        ins.then_inc(self.sem, 1)
        self.n += 1

    def settle(self):
        self.wait(self.eng, self.sem, self.base + self.n)

    def link(self, ins):
        self.step(ins)
        self.settle()

    def enter(self, base):
        self.base, self.n = base, 0


DOWN_LAG = 3
GATE_AT, OUTPUT_AT = 6, 7
LAST_T, LAST_X1, LAST_ROTATE = 7, 7, 8
NORM = {"stats": 1, "rstd": 2, "normed": 5, "nT": 10, "hT": 10, "tstats": 10, "tscale": 11, "h2": 14,
        "logits": 16, "shift": 17, "exp": 18, "gates": 20, "gT_ps": 31, "gT": 31}
GATE_PARTS = 8
FIRST = {"xbo": 7, "xcopy": 8, "xT": 9, "mlp1a": 9, "mlp1b": 12, "gelu_a": 9, "gelu_b": 12, "mlp2": 16,
         "stats": 16, "mrstd": 16, "norm": 17, "affine": 17, "astats": 18, "arstd": 18, "anorm": 19, "aT": 20,
         "qkv_mm": 22, "qkv": 22, "stack": 24, "kT": 26, "qT": 29}
COND_DVE = 4
STEPS_OF_BLOCK = {"pool": 12, "dve": 40}
STEPS_OF_TWO = {"pool": 8, "dve": 76}


def conditioned_stack(nc, x, ids, angles, rows, sty_b1, cond_w, moe_w, mlp_w,
                      mlp_rows, mlp_bi, att_w, att_rows, out):
    with ExitStack() as ctx:
        def sb(name, shape, dt=F32):
            return ctx.enter_context(nc.sbuf_tensor(name, shape, dt))

        def sem(name):
            return ctx.enter_context(nc.semaphore(name))

        psA = ctx.enter_context(nc.psum_tensor("psA", [P, 2, 512], F32))
        psB = ctx.enter_context(nc.psum_tensor("psB", [P, 2, 512], F32))
        psC = ctx.enter_context(nc.psum_tensor("psC", [P, 2, 512], F32))
        psD = ctx.enter_context(nc.psum_tensor("psD", [P, 2, 512], F32))

        ident = sb("ident", [P, P])
        ident16 = sb("ident16", [P, P], BF16)
        mask_qk = sb("mask_qk", [P, 2 * P], BF16)
        pick = sb("pick", [3 * E, E, P], BF16)
        before = sb("before", [P, E, E])
        neghalf = sb("neghalf", [P, 8])
        rowno = sb("rowno", [P, 1])
        rowno_i = sb("rowno_i", [P, 1], I32)

        X = sb("X", [P, TILES, D])
        idall = sb("idall", [SUBJECTS, 16], I32)
        idf = sb("idf", [SUBJECTS, 16])
        ang = sb("ang", [P, 24])
        prow = sb("prow", [NROWS, P])
        pcol = sb("pcol", [P, NROWS])
        styb1 = sb("styb1", [SE, 1])
        cond_sb = sb("cond_sb", [P, COND_COLS])
        subj_sb, hyp1_sb, hyp2_sb, sty1_sb, sty2_sb, router_sb = (
            cond_sb[0:r, c:c + w] for r, c, w in COND_PLACES)
        bi_rows = sb("bi_rows", [E, FF])
        arow = sb("arow", [P, 640])
        watt = sb("watt", [P, 512])
        raw = sb("raw", [P, E, 1024])

        onehot = sb("onehot", [SUBJECTS, 8])
        onehot_x = sb("onehot_x", [E, 8])
        cond_a = sb("cond_a", [P, 8])
        cond_b = sb("cond_b", [P, 8])
        cond_c = sb("cond_c", [P, 8])
        cond_d = sb("cond_d", [P, 8])
        gam = sb("gam", [P, 8])
        bet = sb("bet", [P, 8])
        sp_t = sb("sp_t", [P, 6, 8])
        trig = sb("trig", [P, 6, 16])
        rot_c = sb("rot_c", [P, SEQS, 4])
        rot_s = sb("rot_s", [P, SEQS, 4])
        bi_col = sb("bi_col", [P, FC, SEQS])

        wh = sb("wh", [P, E, 1024], F32R)
        wl = sb("wl", [P, E, 1024], F32R)
        stats = sb("stats", [P, BTILES, 6])
        mv = sb("mv", [P, BTILES, 2])
        rstd = sb("rstd", [P, BTILES])
        nwork = sb("nwork", [P, 3 * BT])
        normed = nwork[:, 0:BT].rearrange("p (t d) -> p t d", t=BTILES)
        hT, h2 = nwork[:, BT:2 * BT], nwork[:, 2 * BT:3 * BT]
        tstats = sb("tstats", [P, 2, 6])
        tmv = sb("tmv", [P, 2, 2])
        tscale = sb("tscale", [P, 2])
        tshift = sb("tshift", [P, 2])
        tvar = sb("tvar", [P, 2])
        hh = sb("hh", [P, BLOCKS, BT], F32R)
        hl = sb("hl", [P, BLOCKS, BT], F32R)
        lmax = sb("lmax", [P, BTILES])
        probs = sb("probs", [P, BTILES, E])
        psums = sb("psums", [P, BTILES])
        above = sb("above", [P, BTILES, E, E])
        equal = sb("equal", [P, BTILES, E, E])
        rank = sb("rank", [P, BTILES, E])
        gates = sb("gates", [P, BTILES, E])
        gparts = sb("gparts", [P, BTILES, 3 * E], BF16)
        gT = sb("gT", [3 * E, BLOCKS, BT], BF16)
        hidh = sb("hidh", [P, 4, BT], F32R)
        hidl = sb("hidl", [P, 4, BT], F32R)
        work = sb("work", [P, 4096])
        hid = work[:, 0:2048].rearrange("p (n t) -> p n t", n=4)
        gb = work[:, 2048:3072].rearrange("p (n t) -> p n t", n=2)
        part = work[:, 3072:4096].rearrange("p (n t) -> p n t", n=2)
        ysum = sb("ysum", [P, BT])
        rot_t = sb("rot_t", [P, 2, 2, D])

        rawf = raw[:, :, :].rearrange("p e c -> p (e c)")
        wmlp = [rawf[:, 1024 * i:1024 * (i + 1)] for i in range(2)]
        ghid = rawf[:, 2048:3072].rearrange("p (f t) -> p f t", f=FC)
        fhid = rawf[:, 3072:4096].rearrange("p (f t) -> p f t", f=FC)
        vm = [v.rearrange("p (j h c) -> p j h c", j=2, h=HEADS) for v in (rawf[:, 4096:8192], work[:, :])]
        whf = wh[:, :, :].rearrange("p e c -> p (e c)")
        stack = [whf[:, 4096 * i:4096 * i + 2048].rearrange("p (j q h c) -> p j q h c", j=2, q=2, h=HEADS)
                 for i in range(2)]
        qT = [whf[:, 4096 * i + 2048:4096 * i + 3072].rearrange("p (g t) -> p g t", g=GROUP) for i in range(2)]
        kT = [whf[:, 4096 * i + 3072:4096 * i + 4096].rearrange("p (g t) -> p g t", g=GROUP) for i in range(2)]
        wffn = sb("wffn", [P, 1024])
        mrow = [sb(f"mrow{i}", [P, 384]) for i in range(2)]
        pr_n = sb("pr_n", [P, 2, D])
        pr_t = sb("pr_t", [P, T])
        pr_b = sb("pr_b", [P, 2, D])
        pr_r = sb("pr_r", [P, 2, D])
        pr_st = sb("pr_st", [P, 2, 6])
        pr_mv = sb("pr_mv", [P, 2, 2])
        pr_rs = sb("pr_rs", [P, 2])
        qk = sb("qk", [P, 2, 2, HEADS, DH])
        qmT = sb("qmT", [P, 2, T], F32R)
        rmax = sb("rmax", [P, 2, HEADS])
        prob = nwork[:, :].rearrange("p (n i c) -> p n i c", n=2, i=2)
        ctx_sb = ysum
        rden = sb("rden", [P, T])
        ctxT = sb("ctxT", [P, T])
        po_b = sb("po_b", [P, 2, D])
        po_x = sb("po_x", [P, 2, D])
        po_n = sb("po_n", [P, 2, D])
        po_t = sb("po_t", [P, T])
        po_d = sb("po_d", [P, 2, D])
        po_st = sb("po_st", [P, 2, 6])
        po_mv = sb("po_mv", [P, 2, 2])
        po_rs = sb("po_rs", [P, 2])

        ids_in, params_in, cond_in, att_in, x_in0, x_in = map(sem, ["ids_in", "params_in", "cond_in", "att_in", "x_in0", "x_in"])
        ang_in, bi_in = sem("ang_in"), sem("bi_in")
        moe_in = [sem(f"moe_in{e}") for e in range(E)]
        mlp_in = [sem("mlp_in0"), sem("mlp_in1")]
        const_ready, dve_step, pool_step, act_step = map(sem, ["const_ready", "dve_step", "pool_step", "act_step"])
        cond_dve, cond_pe, cond_act = map(sem, ["cond_dve", "cond_pe", "cond_act"])
        whigh, wsplit, hid_high = sem("whigh"), sem("wsplit"), sem("hid_high")
        (stat_ready, rstd_ready, normed_ready, nT_ps, hT_ready, tstat_ready, tscale_ready, h2_ready, hsplit, logits_ps,
         shifted, exps, gparts_ready, gT_ps, gT_ready, gb_ps, gb_ready, hid_ps, hid_ready, hid_split, y_ps, part_ready,
         y_sum, yT_ps, x1_ready, rotated) = map(sem, [
             "stat_ready", "rstd_ready", "normed_ready", "nT_ps", "hT_ready", "tstat_ready", "tscale_ready", "h2_ready",
             "hsplit", "logits_ps", "shifted", "exps", "gparts_ready", "gT_ps", "gT_ready", "gb_ps", "gb_ready",
             "hid_ps", "hid_ready", "hid_split", "y_ps", "part_ready", "y_sum", "yT_ps", "x1_ready", "rotated"])
        (xT_ps, xT_ready, xbo_ready, ghid_ps, ghid_ready, mlp_ps, mstat, mrstd, mnorm, x3_ready, astat, arstd, anorm,
         aT_ps, aT_ready, qkv_ps, qkv_ready, stack_ready, kT_ps, kT_ready, qT_ps, qT_ready) = map(sem, [
             "xT_ps", "xT_ready", "xbo_ready", "ghid_ps", "ghid_ready", "mlp_ps", "mstat", "mrstd", "mnorm", "x3_ready",
             "astat", "arstd", "anorm", "aT_ps", "aT_ready", "qkv_ps", "qkv_ready", "stack_ready", "kT_ps", "kT_ready",
             "qT_ps", "qT_ready"])
        (s_ps, max_ready, m_ready, qmT_ps, qmT_ready, t_ps, prob_ready, pv_ps, ctx_ready, wo_ps, xb4_ready, fstat, frstd,
         fnorm, fT_ps, fT_ready, fhid_ps, fhid_ready, ffn_ps, diff_ready, out_ready, out_done) = map(sem, [
             "s_ps", "max_ready", "m_ready", "qmT_ps", "qmT_ready", "t_ps", "prob_ready", "pv_ps", "ctx_ready", "wo_ps",
             "xb4_ready", "fstat", "frstd", "fnorm", "fT_ps", "fT_ready", "fhid_ps", "fhid_ready", "ffn_ps",
             "diff_ready", "out_ready", "out_done"])

        values_clear, stack_clear, trig_ready, xcopy_ready = map(
            sem, ["values_clear", "stack_clear", "trig_ready", "xcopy_ready"])
        ctx_copied, masked = sem("ctx_copied"), sem("masked")
        started, trig_in = sem("started"), sem("trig_in")

        scale = float(DH) ** -0.5
        x_tiles = x.rearrange("s (j p) d -> p (s j) d", p=P)
        out_tiles = out.rearrange("s (j p) d -> p (s j) d", p=P)

        def col(name, i=0):
            return pcol[:, COL[name] + i:COL[name] + i + 1]

        def mlp_count(n, par):
            return 16 * (n + 2 - par)

        def diagonal(cols):
            (step, count), (one, _) = cols.ap
            return bass.AP(cols.tensor, cols.offset, [(step, count), ((P + DH) * one, 8), (one, DH)])

        def sequences(eng, chain, pre_at, post_at, pre, post, attention):
            def body(s, par):
                known = isinstance(s, int)
                for slot in range(SLOTS):
                    attention(s, par, slot // 3, slot % 3, known and s == 0, known and s == SEQS)
                    for at, step in pre_at:
                        if at == slot and not (known and s >= SEQS - 1):
                            pre(s + 1, 1 - par, step)
                    for at, step in post_at:
                        if at == slot and not (known and s == 0):
                            post(s - 1, step)
                        if at == slot + SLOTS and not (known and s < 2):
                            post(s - 2, step)

            body(0, 0)
            body(1, 1)
            start = chain.n + chain.base if chain else 0
            per = STEPS_OF_TWO[chain.name] if chain else 0
            with eng.Fori(1, SEQS // 2 - 1) as i:
                if chain:
                    chain.enter(start + per * (i - 1))
                body(2 * i, 0)
                body(2 * i + 1, 1)
                if chain:
                    assert chain.n == per, (chain.name, chain.n)
            if chain:
                chain.enter(start + per * (SEQS // 2 - 2))
            body(SEQS - 2, 0)
            body(SEQS - 1, 1)
            body(SEQS, 0)
            for at, step in post_at:
                if at >= SLOTS:
                    post(SEQS - 1, step)

        def need(eng, sem, value):
            if not isinstance(value, int) or value > 0:
                eng.wait_ge(sem, value)

        def high_on_act(n):
            return n % 4 != 1

        HIGHS = sum(map(high_on_act, range(CHUNKS)))

        def apart(eng, sem, value):
            if not isinstance(value, int):
                value = eng.to_reg(value)
                eng.wait_ge(started, 1)
            if not isinstance(value, int) or value > 0:
                eng.wait_ge(sem, value)

        block = ctx.enter_context(nc.Block())

        @block.sync
        def _(sp):
            sp.dma_start(ang[:, :], angles.partition_broadcast(P).rearrange("p a n -> p (a n)")).then_inc(ang_in, 16)
            sp.dma_start(idall[:, :], ids.partition_broadcast(SUBJECTS).rearrange("p a n -> p (a n)")).then_inc(ids_in, 16)
            sp.dma_start(X[:, 0:BTILES, :], x_tiles[:, 0:BTILES, :]).then_inc(x_in0, 16)
            sp.dma_start(cond_sb[:, :], cond_w).then_inc(cond_in, 16)
            sp.dma_start(prow[:, :], rows).then_inc(params_in, 16)
            sp.dma_start(styb1[:, :], sty_b1).then_inc(cond_in, 16)
            sp.dma_start(raw[:, 0, :], moe_w[0]).then_inc(moe_in[0], 16)
            sp.dma_start(bi_rows[:, :], mlp_bi).then_inc(bi_in, 16)
            for e in range(1, E):
                sp.dma_start(raw[:, e, :], moe_w[e]).then_inc(moe_in[e], 16)
            for g in range(1, BLOCKS):
                sp.dma_start(X[:, g * BTILES:(g + 1) * BTILES, :],
                             x_tiles[:, g * BTILES:(g + 1) * BTILES, :]).then_inc(x_in, 16)
            sp.dma_start(watt[:, :], att_w[:, 0:512]).then_inc(att_in, 16)
            sp.dma_start(wffn[:, :], att_w[:, 512:1536]).then_inc(att_in, 16)
            sp.dma_start(arow[:, :], att_rows.partition_broadcast(P).rearrange("p a n -> p (a n)")).then_inc(att_in, 16)
            sp.wait_ge(ids_in, 16)
            sp.wait_ge(wsplit, E)

            def load_mlp(s, par):
                need(sp, mlp_ps, s - 1)
                need(sp, x3_ready, s - 1)
                e = sp.value_load(idall[0:1, bass.ds(s + 8, 1)], min_val=0, max_val=E - 1)
                sp.dma_start(wmlp[par], mlp_w[bass.ds(e, 1)].rearrange("a p c -> p (a c)")).then_inc(mlp_in[par], 16)
                sp.dma_start(mrow[par][:, :], mlp_rows[bass.ds(e, 1), :].partition_broadcast(P)
                             .rearrange("p a n -> p (a n)")).then_inc(mlp_in[par], 16)

            def store(s):
                sp.wait_ge(out_ready, s + 1)
                sp.dma_start(out_tiles[:, bass.ds(2 * s, 2), :], X[:, bass.ds(2 * s, 2), :]).then_inc(out_done, 16)

            for s in range(3):
                load_mlp(s, s % 2)
            with sp.Fori(0, 2) as i:
                store(2 * i)
                load_mlp(2 * i + 3, 1)
                store(2 * i + 1)
                load_mlp(2 * i + 4, 0)
            store(4)
            load_mlp(7, 1)
            for s in range(5, SEQS):
                store(s)
            sp.wait_ge(out_done, 16 * SEQS)

        @block.gpsimd
        def _(pool):
            g_ = nc.gpsimd
            chain = Chain(pool, pool_step, "pool", apart)
            g_.memset(ident[:, :], 0.0).then_inc(started, 1)
            chain.step(g_.memset(neghalf[:, :], -0.5))
            chain.link(g_.iota(rowno_i[:, :], pattern=[[0, 1]], base=0, channel_multiplier=1))
            chain.step(g_.tensor_copy(rowno[:, :], rowno_i[:, :]))

            def diagonal_ones(m):
                return g_.affine_select(out=m[:, :], in_=m[:, :], compare_op=ALU.not_equal, fill=1.0, base=0,
                                        pattern=[[-1, P]], channel_multiplier=1)

            diagonal_ones(ident).then_inc(const_ready, 1)
            chain.step(g_.memset(ident16[:, :], 0.0))
            chain.link(g_.memset(before[:, :, :], 1.0))
            chain.step(diagonal_ones(ident16))
            g_.affine_select(out=before[:, :, :], in_=before[:, :, :], compare_op=ALU.is_gt, fill=0.0, base=0,
                             pattern=[[1, E], [-1, E]], channel_multiplier=0).then_inc(const_ready, 1)

            def selectors():
                chain.link(g_.memset(pick[:, :, :], 0.0))
                for k in range(3):
                    ins = g_.affine_select(out=pick[:, :, :], in_=pick[:, :, :], compare_op=ALU.not_equal, fill=1.0,
                                           base=-E * k, pattern=[[-1, E], [0, P]], channel_multiplier=1)
                    if k < 2:
                        chain.link(ins)
                ins.then_inc(const_ready, 1)

            def masks():
                chain.link(g_.memset(mask_qk[:, :], 0.0))
                g_.affine_select(out=mask_qk[:, :].rearrange("p (b k) -> p b k", b=2),
                                 in_=mask_qk[:, :].rearrange("p (b k) -> p b k", b=2), compare_op=ALU.is_ge,
                                 fill=MASKED, base=0, pattern=[[0, 2], [-1, P]], channel_multiplier=1)\
                    .then_inc(const_ready, 1)

            def weights_rest(e):
                pool.wait_ge(whigh, e + 1)
                g_.tensor_tensor(wl[:, e, :], raw[:, e, :], wh[:, e, :].bitcast(F32), ALU.subtract).then_inc(wsplit, 1)

            def inverse_root(var, eps, out_ap, tmp, done):
                chain.link(g_.tensor_scalar(tmp, var, eps, None, ALU.add))
                ins = g_.tensor_tensor(out_ap, tmp, neghalf[:, 0:var.shape[1]], ALU.pow)
                return ins.then_inc(done, 1) if done is not None else chain.link(ins)

            def norm_rstd(a):
                apart(pool, stat_ready, a + 1)
                inverse_root(mv[:, :, 1], 1e-5, rstd[:, :], rstd[:, :], rstd_ready)

            def norm_tscale(a):
                apart(pool, tstat_ready, a + 1)
                inverse_root(tmv[:, :, 1], 1e-8, tvar[:, :], tvar[:, :], None)
                chain.link(g_.tensor_tensor(tscale[:, :], tvar[:, :], gam[:, bass.ds(2 * a, 2)], ALU.mult))
                chain.link(g_.tensor_tensor(tvar[:, :], tmv[:, :, 0], tscale[:, :], ALU.mult))
                g_.tensor_tensor(tshift[:, :], bet[:, bass.ds(2 * a, 2)], tvar[:, :], ALU.subtract)\
                    .then_inc(tscale_ready, 1)

            def expert_sum(g, e):
                apart(pool, part_ready, 8 * g + e + 1)
                if e == 1:
                    apart(pool, yT_ps, g)
                    g_.tensor_tensor(ysum[:, :], part[:, 0], part[:, 1], ALU.add).then_inc(y_sum, 1)
                elif e > 1:
                    apart(pool, y_sum, 7 * g + e - 1)
                    g_.tensor_tensor(ysum[:, :], ysum[:, :], part[:, e % 2], ALU.add).then_inc(y_sum, 1)

            def rotate(g):
                apart(pool, x1_ready, g + 1)
                for j in range(2):
                    s = 2 * g + j
                    xs = X[:, bass.ds(2 * s, 2), :].rearrange("p j (q c) -> p (j q) c", c=4)
                    t = rot_t[:, j].rearrange("p j (q c) -> p (j q) c", c=4)
                    cs = rot_c[:, bass.ds(s, 1), :].to_broadcast([P, 64, 4])
                    ss = rot_s[:, bass.ds(s, 1), :].to_broadcast([P, 64, 4])
                    chain.step(g_.tensor_tensor(t[:, :, 0:4:2], xs[:, :, 1:4:2], ss[:, :, 0:4:2], ALU.mult))
                    chain.link(g_.tensor_tensor(t[:, :, 1:4:2], xs[:, :, 0:4:2], ss[:, :, 1:4:2], ALU.mult))
                    chain.link(g_.tensor_tensor(xs, xs, cs, ALU.mult))
                    if j == 0:
                        chain.step(g_.tensor_tensor(xs, xs, t, ALU.add))
                    else:
                        g_.tensor_tensor(xs, xs, t, ALU.add).then_inc(rotated, 1)

            norm_rstd(0)
            weights_rest(0)
            pool.wait_ge(cond_dve, COND_DVE)
            norm_tscale(0)
            weights_rest(1)
            selectors()

            def clear_values(i):
                chain.link(g_.memset(vm[i], 0.0))
                for q in range(2):
                    v = vm[i].rearrange("p j (q h) c -> p j q h c", q=2)[:, :, q]
                    for h in range(8):
                        ins = g_.memset(v[:, :, h, 64 + DH * h:64 + DH * (h + 1)], 1.0)
                        if (q, h) != (1, 7):
                            chain.step(ins)
                        else:
                            ins.then_inc(values_clear, 1)

            def clear_stack(i):
                chain.link(g_.memset(stack[i][:, :, :, :, 24:32].bitcast(F32), 0.0))
                g_.memset(stack[i][:, :, 1, :, 24:26].bitcast(F32), -1.0).then_inc(stack_clear, 1)

            def pre(n, par, step):
                if step == "xbo":
                    pool.wait_ge(rotated, 1 if isinstance(n, int) and n < 2 else BLOCKS)
                    apart(pool, mlp_in[par], mlp_count(n, par))
                    g_.tensor_tensor(pr_b[:, :, :], X[:, bass.ds(2 * n, 2), :],
                                     mrow[par][:, 0:D].unsqueeze(1).to_broadcast([P, 2, D]), ALU.add)\
                        .then_inc(xbo_ready, 1)
                elif step == "mrstd":
                    apart(pool, mstat, n + 1)
                    inverse_root(pr_mv[:, :, 1], 1e-12, pr_rs[:, :], pr_rs[:, :], mrstd)
                elif step == "arstd":
                    apart(pool, astat, n + 1)
                    inverse_root(pr_mv[:, :, 1], 1e-5, pr_rs[:, :], pr_rs[:, :], arstd)

            def post(m, step):
                if step == "xb4":
                    g_.tensor_tensor(po_b[:, :, :], X[:, bass.ds(2 * m, 2), :],
                                     arow[:, 384:512].unsqueeze(1).to_broadcast([P, 2, D]), ALU.add)\
                        .then_inc(xb4_ready, 1)
                elif step == "frstd":
                    apart(pool, fstat, m + 1)
                    inverse_root(po_mv[:, :, 1], 1e-5, po_rs[:, :], po_rs[:, :], frstd)
                elif step == "diff":
                    apart(pool, fstat, m + 1)
                    chain.link(g_.tensor_tensor(po_d[:, :, :], po_x[:, :, :],
                                                arow[:, 512:640].unsqueeze(1).to_broadcast([P, 2, D]), ALU.add))
                    g_.tensor_tensor(po_d[:, :, :], po_d[:, :, :], X[:, bass.ds(2 * m, 2), :], ALU.subtract)\
                        .then_inc(diff_ready, 1)

            def moe(g, first, ahead):
                last = not ahead
                for n in range(CHUNKS):
                    if n % FC == OUTPUT_AT % FC:
                        e = (n - OUTPUT_AT) // FC
                        if e >= 0:
                            expert_sum(g, e)
                        elif not first:
                            expert_sum(g - 1, e + E)
                    if n == LAST_ROTATE and not first:
                        rotate(g - 1)
                    if ahead and n == NORM["rstd"]:
                        norm_rstd(g + 1)
                    if ahead and n == NORM["tscale"]:
                        norm_tscale(g + 1)
                    if first and n in (0, 2, 4, 5, 6, 7):
                        weights_rest(2 + (0, 2, 4, 5, 6, 7).index(n))
                    if first and n == 8:
                        masks()
                    if last:
                        if n == 4:
                            clear_values(0)
                        if n == 12:
                            pool.wait_ge(y_ps, CHUNKS * g + 2 * FC)
                            clear_stack(0)
                        for step in ("xbo", "mrstd", "arstd"):
                            if n == FIRST[step]:
                                pre(0, 0, step)

            moe(0, True, True)
            per, start = STEPS_OF_BLOCK["pool"], chain.base + chain.n
            with pool.Fori(1, BLOCKS - 1) as g:
                chain.enter(start + per * (g - 1))
                moe(g, False, True)
                assert chain.n == per, chain.n
            chain.enter(start + per * (BLOCKS - 2))
            moe(BLOCKS - 1, False, False)
            expert_sum(BLOCKS - 1, E - 1)

            def mask_probs(s, k):
                apart(pool, prob_ready, 8 * s + k + 1)
                diag = prob[:, k % 2, :, 0:2 * P].rearrange("p i (b q) -> p i b q", b=2)
                g_.affine_select(out=diag, in_=diag, compare_op=ALU.is_ge, fill=0.0, base=0,
                                 pattern=[[0, 2], [0, 2], [1, P]], channel_multiplier=-1).then_inc(masked, 1)

            def attention(s, par, k, part_, first, last):
                if part_ == 1:
                    if k >= T_LAG and not last:
                        mask_probs(s, k - T_LAG)
                    elif k < T_LAG and not first:
                        mask_probs(s - 1, k - T_LAG + PAIRS)
                if first and (k, part_) == (0, 2):
                    pool.wait_ge(y_sum, (E - 1) * BLOCKS)
                    clear_values(1)
                    clear_stack(1)
                if first and (k, part_) == (4, 2):
                    rotate(BLOCKS - 1)

            PRE = [(0, "xbo"), (5, "mrstd"), (9, "arstd")]
            POST = [(11, "xb4"), (13, "frstd"), (13, "diff")]
            sequences(pool, chain, PRE, POST, pre, post, attention)

        @block.tensor
        def _(pe):
            mm, tr = nc.tensor.matmul, nc.tensor.transpose

            pe.wait_ge(const_ready, 1)
            pe.wait_ge(params_in, 16)
            tr(psD[:, 0, 0:NROWS], prow[:, :], ident[0:NROWS, 0:NROWS]).then_inc(cond_pe, 1)
            pe.wait_ge(cond_in, 32)
            pe.wait_ge(cond_dve, 1)
            mm(psD[0:SE, 1, 0:8], subj_sb, onehot[:, :], start=True, stop=True).then_inc(cond_pe, 1)
            pe.wait_ge(cond_dve, 2)
            mm(psD[:, 1, 128:136], hyp1_sb, cond_a[0:SE, :], start=True, stop=True).then_inc(cond_pe, 1)
            pe.wait_ge(cond_act, 1)
            mm(psD[:, 1, 136:144], hyp2_sb, cond_b[:, :], start=True, stop=True).then_inc(cond_pe, 1)
            pe.wait_ge(cond_act, 2)
            mm(psD[0:SE, 1, 144:152], sty1_sb, cond_c[:, :], start=True, stop=True).then_inc(cond_pe, 1)
            pe.wait_ge(cond_act, 3)
            mm(psD[:, 1, 152:160], sty2_sb[:, 0:D], cond_d[0:SE, :], start=True, stop=True)
            mm(psD[:, 1, 160:168], sty2_sb[:, D:2 * D], cond_d[0:SE, :], start=True, stop=True).then_inc(cond_pe, 1)

            def norm_nT(a):
                pe.wait_ge(normed_ready, a + 1)
                need(pe, hT_ready, a)
                need(pe, x1_ready, a - 1)
                for t in range(BTILES):
                    last = tr(psC[:, 1, t * P:(t + 1) * P], normed[:, t, :], ident[:, :])
                last.then_inc(nT_ps, 1)

            def norm_logits(a):
                pe.wait_ge(h2_ready, a + 1)
                for t in range(BTILES):
                    last = mm(psD[:, 0, t * E:(t + 1) * E], h2[:, t * P:(t + 1) * P], router_sb,
                              start=True, stop=True)
                last.then_inc(logits_ps, 1)

            def norm_gT(a):
                pe.wait_ge(gparts_ready, a + 1)
                for t in range(BTILES):
                    last = tr(psD[0:3 * E, 0, 64 * t:64 * (t + 1)].bitcast(BF16), gparts[:, t, :], ident16[:, :])
                last.then_inc(gT_ps, 1)

            norm_nT(0)
            pe.wait_ge(bi_in, 16)
            for f in range(FC):
                last = mm(psC[:, 0, 8 * f:8 * (f + 1)], bi_rows[:, f * P:(f + 1) * P], onehot_x[:, :],
                          start=True, stop=True)
            last.then_inc(cond_pe, 1)
            norm_logits(0)

            def three(out_ap, wcols, h_hi, h_lo, start, stop):
                mm(out_ap, wh[:, wcols[0], wcols[1]:wcols[1] + P], h_hi, start=start, stop=False)
                mm(out_ap, wh[:, wcols[0], wcols[1]:wcols[1] + P], h_lo, start=False, stop=False)
                return mm(out_ap, wl[:, wcols[0], wcols[1]:wcols[1] + P], h_hi, start=False, stop=stop)

            def gate_rows(g, e):
                pe.wait_ge(const_ready, 3)
                if e == 0:
                    pe.wait_ge(gT_ready, g + 1)
                apart(pe, gb_ready, 8 * g + e)
                mm(psC[:, 0, :], pick[:, e, :], gT[:, g, :], start=True, stop=True).then_inc(gb_ps, 1)

            def up(g, n):
                e, f = divmod(n, FC)
                if f == 0:
                    pe.wait_ge(wsplit, e + 1)
                    if e == 0:
                        pe.wait_ge(hsplit, g + 1)
                need(pe, hid_ready, CHUNKS * g + n - 1)
                three(psA[:, n % 2, :], (e, f * P), hh[:, g, :], hl[:, g, :], True, True).then_inc(hid_ps, 1)

            def down(g, n):
                e, f = divmod(n, FC)
                pe.wait_ge(hid_split, CHUNKS * g + n + 1)
                if f == 0:
                    need(pe, part_ready, 8 * g + e - 1)
                three(psB[:, e % 2, :], (e, FF + f * P), hidh[:, n % 4, :], hidl[:, n % 4, :], f == 0, f == FC - 1)\
                    .then_inc(y_ps, 1)

            def sum_T(g):
                pe.wait_ge(y_sum, 7 * g + 7)
                for t in range(BTILES):
                    last = tr(psC[:, 1, t * P:(t + 1) * P], ysum[:, t * P:(t + 1) * P], ident[:, :])
                last.then_inc(yT_ps, 1)

            def pre(n, par, step):
                if step == "xT":
                    pe.wait_ge(xcopy_ready, n + 1)
                    need(pe, qT_ready, 2 * n)
                    for j in range(2):
                        last = tr(psD[:, 0, j * P:(j + 1) * P], pr_n[:, j, :], ident[:, :])
                    last.then_inc(xT_ps, 1)
                elif step in ("mlp1a", "mlp1b"):
                    b = 1 if step == "mlp1a" else 0
                    if b == 1:
                        pe.wait_ge(xT_ready, n + 1)
                        pe.wait_ge(mlp_in[par], mlp_count(n, par))
                    for k in range(2):
                        f = 2 * (1 - b) + k
                        last = mm(psD[:, b, k * T:(k + 1) * T], wmlp[par][:, f * P:(f + 1) * P], pr_t[:, :],
                                  start=True, stop=True)
                    last.then_inc(ghid_ps, 1)
                elif step == "mlp2":
                    pe.wait_ge(ghid_ready, 2 * (n + 1))
                    for j in range(2):
                        for f in range(FC):
                            last = mm(psD[:, 1, j * P:(j + 1) * P], ghid[:, f, j * P:(j + 1) * P],
                                      wmlp[par][:, FF + f * P:FF + (f + 1) * P], start=f == 0, stop=f == FC - 1)
                    last.then_inc(mlp_ps, 1)
                elif step == "aT":
                    pe.wait_ge(anorm, n + 1)
                    for j in range(2):
                        last = tr(psD[:, 0, j * P:(j + 1) * P], pr_r[:, j, :], ident[:, :])
                    last.then_inc(aT_ps, 1)
                elif step == "qkv":
                    pe.wait_ge(aT_ready, n + 1)
                    if isinstance(n, int) and n == 0:
                        pe.wait_ge(att_in, 48)
                    for j in range(2):
                        last = mm(psD[:, 1 - j, 0:3 * D], pr_t[:, j * P:(j + 1) * P], watt[:, 0:3 * D],
                                  start=True, stop=True)
                    last.then_inc(qkv_ps, 1)
                elif step in ("kT", "qT"):
                    pe.wait_ge(stack_ready, n + 1)
                    qk_ = 1 if step == "kT" else 0
                    for b in (1, 0):
                        if step == "qT":
                            pe.wait_ge(kT_ready, 2 * n + 2 - b)
                        for k in range(2):
                            gr = 2 * (1 - b) + k
                            for j in range(2):
                                src = stack[par][:, j, qk_, GROUP * gr:GROUP * (gr + 1), :].bitcast(F32)
                                last = tr(psD[:, b, k * T + j * P:k * T + (j + 1) * P],
                                          src.rearrange("p h c -> p (h c)"), ident[:, :])
                        last.then_inc(kT_ps if step == "kT" else qT_ps, 1)

            def post(m, step):
                if step == "wo":
                    pe.wait_ge(ctx_ready, m + 1)
                    need(pe, out_ready, m)
                    for j in range(2):
                        last = mm(psC[:, 1, j * P:(j + 1) * P], ctxT[:, j * P:(j + 1) * P], watt[:, 3 * D:4 * D],
                                  start=True, stop=True)
                    last.then_inc(wo_ps, 1)
                elif step == "fT":
                    pe.wait_ge(fnorm, m + 1)
                    for j in range(2):
                        last = tr(psC[:, 1, j * P:(j + 1) * P], po_n[:, j, :], ident[:, :])
                    last.then_inc(fT_ps, 1)
                elif step in ("ffn1a", "ffn1b"):
                    half = 0 if step == "ffn1a" else 1
                    if half == 0:
                        pe.wait_ge(fT_ready, m + 1)
                    else:
                        pe.wait_ge(fhid_ready, 2 * m + 1)
                    for k in range(2):
                        f = 2 * half + k
                        last = mm(psC[:, 1, k * T:(k + 1) * T], wffn[:, f * P:(f + 1) * P], po_t[:, :],
                                  start=True, stop=True)
                    last.then_inc(fhid_ps, 1)
                elif step == "ffn2":
                    pe.wait_ge(fhid_ready, 2 * (m + 1))
                    for j in range(2):
                        for f in range(FC):
                            last = mm(psC[:, 1, j * P:(j + 1) * P], fhid[:, f, j * P:(j + 1) * P],
                                      wffn[:, FF + f * P:FF + (f + 1) * P], start=f == 0, stop=f == FC - 1)
                    last.then_inc(ffn_ps, 1)

            def scores(s, par, k):
                if k == 0:
                    pe.wait_ge(qT_ready, 2 * (s + 1))
                need(pe, max_ready, 8 * s + k)
                for i in range(2):
                    gr, r = divmod(2 * k + i, GROUP)
                    rows_ = slice(SLOT * r, SLOT * r + 24)
                    mm(psA[:, i, P:3 * P], ident16[:, :], mask_qk[:, :], start=True, stop=False, skip_group_check=True)
                    mm(psA[:, i, 0:2 * P], qT[par][rows_, gr, P:2 * P], kT[par][rows_, gr, :],
                       start=False, stop=False, skip_group_check=True)
                    last = mm(psA[:, i, 2 * P:4 * P], qT[par][rows_, gr, 0:P], kT[par][rows_, gr, :],
                              start=False, stop=True, skip_group_check=True)
                last.then_inc(s_ps, 1)

            def queries_with_max(s, par, gr):
                pe.wait_ge(m_ready, 4 * s + gr + 1)
                if isinstance(s, int) and (s, gr) == (0, 0):
                    pe.wait_ge(part_ready, E * BLOCKS)
                need(pe, prob_ready, 8 * s + 2 * gr - 1)
                for j in range(2):
                    src = stack[par][:, j, 0, GROUP * gr:GROUP * (gr + 1), :].bitcast(F32)
                    last = tr(psB[:, j, 0:P], src.rearrange("p h c -> p (h c)"), ident[:, :])
                last.then_inc(qmT_ps, 1)

            def scores_t(s, par, k):
                following = (k + 1) // 2 + 1
                if isinstance(s, int) and s == SEQS - 1:
                    following = min(following, 4)
                pe.wait_ge(qmT_ready, 4 * s + following)
                need(pe, prob_ready, 8 * s + k)
                for i in range(2):
                    gr, r = divmod(2 * k + i, GROUP)
                    rows_ = slice(SLOT * r, SLOT * r + 26)
                    mm(psB[:, i, 0:2 * P], kT[par][rows_, gr, P:2 * P], qmT[rows_, gr % 2, :],
                       start=True, stop=False, skip_group_check=True)
                    last = mm(psB[:, i, 2 * P:4 * P], kT[par][rows_, gr, 0:P], qmT[rows_, gr % 2, :],
                              start=False, stop=True, skip_group_check=True)
                last.then_inc(t_ps, 1)

            def context(s, par, k):
                if k % 4 == 0:
                    need(pe, ctx_copied, 2 * s + k // 4)
                    if isinstance(s, int) and (s, k) == (0, 0):
                        pe.wait_ge(gb_ready, E * BLOCKS)
                pe.wait_ge(masked, 8 * s + k + 1)
                for i in range(2):
                    h = 2 * k + i
                    c = T * (h // 8)
                    mm(psC[:, 0, c:c + T], vm[par][:, 0, h, :], prob[:, k % 2, i, P:3 * P],
                       start=h % 8 == 0, stop=False, skip_group_check=True)
                    last = mm(psC[:, 0, c + P:c + T], vm[par][:, 1, h, :], prob[:, k % 2, i, 0:P],
                              start=False, stop=h % 8 == 7, skip_group_check=True)
                last.then_inc(pv_ps, 1)

            def attention(s, par, k, part_, first, last):
                if first and (k, part_) == (1, 0):
                    sum_T(BLOCKS - 1)
                if first and (k, part_) == (PAIRS - 1, 2):
                    pe.wait_ge(x1_ready, BLOCKS)
                if part_ == 0:
                    if not last:
                        scores(s, par, k)
                    if k % 2 == 0:
                        if k >= 2 and not last:
                            queries_with_max(s, par, k // 2 - 1)
                        elif k == 0 and not first:
                            queries_with_max(s - 1, 1 - par, 3)
                elif part_ == 1:
                    if k >= T_LAG and not last:
                        scores_t(s, par, k - T_LAG)
                    elif k < T_LAG and not first:
                        scores_t(s - 1, 1 - par, k - T_LAG + PAIRS)
                else:
                    if k >= PV_LAG and not last:
                        context(s, par, k - PV_LAG)
                    elif k < PV_LAG and not first:
                        context(s - 1, 1 - par, k - PV_LAG + PAIRS)

            def moe(g, first, ahead):
                for n in range(CHUNKS):
                    up(g, n)
                    if n >= DOWN_LAG:
                        down(g, n - DOWN_LAG)
                    elif not first:
                        down(g - 1, n - DOWN_LAG + CHUNKS)
                    if n % FC == GATE_AT % FC:
                        e = (n - GATE_AT) // FC
                        if e >= 0:
                            gate_rows(g, e)
                        elif not first:
                            gate_rows(g - 1, e + E)
                    if n == LAST_T and not first:
                        sum_T(g - 1)
                    if first and n == 5:
                        norm_gT(0)
                    if ahead and n == NORM["nT"]:
                        norm_nT(g + 1)
                    if ahead and n == NORM["logits"]:
                        norm_logits(g + 1)
                    if ahead and n == NORM["gT_ps"]:
                        norm_gT(g + 1)
                    if not ahead:
                        for step in ("xT", "mlp1a", "mlp1b", "mlp2", "aT", "qkv", "kT", "qT"):
                            if n == FIRST["qkv_mm" if step == "qkv" else step]:
                                pre(0, 0, step)

            moe(0, True, True)
            with pe.Fori(1, BLOCKS - 1) as g:
                moe(g, False, True)
            moe(BLOCKS - 1, False, False)
            for n in range(CHUNKS - DOWN_LAG, CHUNKS):
                down(BLOCKS - 1, n)
            gate_rows(BLOCKS - 1, E - 1)
            pe.wait_ge(const_ready, 4)

            PRE = [(2, "xT"), (4, "mlp1a"), (4, "mlp1b"), (5, "mlp2"), (12, "aT"), (16, "qkv"), (20, "kT"),
                   (22, "qT")]
            POST = [(13, "wo"), (16, "fT"), (17, "ffn1a"), (18, "ffn1b"), (20, "ffn2")]
            sequences(pe, None, PRE, POST, pre, post, attention)

        @block.scalar
        def _(act):
            a_ = nc.scalar.activation
            chain = Chain(act, act_step, "act", need)
            act.wait_ge(trig_in, 1)
            chain.step(a_(trig[:, 4, :], trig[:, 2, :], ACT.Sin))
            a_(trig[:, 5, :], trig[:, 3, :], ACT.Sin).then_inc(trig_ready, 1)
            act.wait_ge(cond_pe, 3)
            a_(cond_b[:, :], psD[:, 1, 128:136], ACT.Relu, bias=col("hyp_b1")).then_inc(cond_act, 1)
            act.wait_ge(cond_pe, 4)
            a_(cond_c[:, :], psD[:, 1, 136:144], ACT.Identity, bias=col("hyp_b2")).then_inc(cond_act, 1)
            act.wait_ge(cond_pe, 5)
            a_(cond_d[0:SE, :], psD[0:SE, 1, 144:152], ACT.Relu, bias=styb1[:, :]).then_inc(cond_act, 1)
            def norm_hT(a):
                act.wait_ge(nT_ps, a + 1)
                a_(hT[:, :], psC[:, 1, :], ACT.Identity, bias=col("ln_b"), scale=col("ln_g")).then_inc(hT_ready, 1)

            def norm_exp(a):
                act.wait_ge(shifted, a + 1)
                a_(probs[:, :, :], probs[:, :, :], ACT.Exp).then_inc(exps, 1)

            def norm_gT(a):
                act.wait_ge(gT_ps, a + 1)
                a_(gT[:, a, :], psD[0:3 * E, 0, 0:256].bitcast(BF16), ACT.Copy).then_inc(gT_ready, 1)

            def weights_high(e):
                act.wait_ge(moe_in[e], 16)
                a_(wh[:, e, :], raw[:, e, :], ACT.Copy).then_inc(whigh, 1)

            weights_high(0)
            act.wait_ge(cond_dve, 3)
            chain.step(a_(sp_t[:, 2, :], sp_t[:, 1, :], ACT.Exp, scale=-1.0))
            norm_hT(0)
            chain.settle()
            a_(sp_t[:, 3, :], sp_t[:, 2, :], ACT.Ln, bias=1.0).then_inc(cond_act, 1)

            weights_high(1)
            weights_high(2)
            norm_exp(0)
            weights_high(3)

            def gate_rows(g, e):
                act.wait_ge(gb_ps, 8 * g + e + 1)
                need(act, part_ready, 8 * g + e - 1)
                a_(gb[:, e % 2, :], psC[:, 0, :], ACT.Copy).then_inc(gb_ready, 1)

            def pre(n, par, step):
                if step == "xT":
                    act.wait_ge(xT_ps, n + 1)
                    a_(pr_t[:, :], psD[:, 0, 0:T], ACT.Copy).then_inc(xT_ready, 1)
                elif step in ("gelu_a", "gelu_b"):
                    b = 1 if step == "gelu_a" else 0
                    act.wait_ge(ghid_ps, 2 * n + 2 - b)
                    for k in range(2):
                        f = 2 * (1 - b) + k
                        ins = a_(ghid[:, f, :], psD[:, b, k * T:(k + 1) * T], ACT.Gelu,
                                 bias=bi_col[:, f, bass.ds(n, 1)])
                    ins.then_inc(ghid_ready, 1)
                elif step == "aT":
                    act.wait_ge(aT_ps, n + 1)
                    a_(pr_t[:, :], psD[:, 0, 0:T], ACT.Identity, bias=col("beta1"), scale=col("gamma1"))\
                        .then_inc(aT_ready, 1)
                elif step in ("kT", "qT"):
                    for b in (1, 0):
                        act.wait_ge(kT_ps if step == "kT" else qT_ps, 2 * n + 2 - b)
                        dst = (kT if step == "kT" else qT)[par][:, 2 * (1 - b):2 * (2 - b), :]
                        a_(dst, psD[:, b, :].rearrange("p (g t) -> p g t", g=2), ACT.Copy)\
                            .then_inc(kT_ready if step == "kT" else qT_ready, 1)

            def post(m, step):
                if step in ("ctx_a", "ctx_b"):
                    half = 0 if step == "ctx_a" else 1
                    act.wait_ge(pv_ps, 8 * m + 4 * (half + 1))
                    cols, rows_ = slice(T * half, T * (half + 1)), slice(64 * (1 - half), 64 * (2 - half))
                    if half == 0:
                        need(act, ctx_ready, m)
                    a_(ctx_sb[rows_, 0:T], psC[0:64, 0, cols], ACT.Copy)
                    a_(ctx_sb[rows_, T:2 * T], psC[64:128, 0, cols], ACT.Copy).then_inc(ctx_copied, 1)
                elif step == "fT":
                    act.wait_ge(fT_ps, m + 1)
                    a_(po_t[:, :], psC[:, 1, 0:T], ACT.Identity, bias=col("beta2"), scale=col("gamma2"))\
                        .then_inc(fT_ready, 1)
                elif step in ("gelu_a", "gelu_b"):
                    half = 0 if step == "gelu_a" else 1
                    act.wait_ge(fhid_ps, 2 * m + half + 1)
                    for k in range(2):
                        f = 2 * half + k
                        ins = a_(fhid[:, f, :], psC[:, 1, k * T:(k + 1) * T], ACT.Gelu, bias=col("ffn_b1", f))
                    ins.then_inc(fhid_ready, 1)

            def exp_t(s, k):
                act.wait_ge(t_ps, 8 * s + k + 1)
                need(act, pv_ps, 8 * s + k - 1)
                a_(prob[:, k % 2], psB[:, :, P:4 * P], ACT.Exp, scale=scale).then_inc(prob_ready, 1)

            def queries(s, gr):
                act.wait_ge(qmT_ps, 4 * s + gr + 1)
                need(act, t_ps, 8 * s + 2 * gr - 2)
                a_(qmT[:, gr % 2, :].rearrange("p (j q) -> p j q", j=2), psB[:, :, 0:P], ACT.Copy).then_inc(qmT_ready, 1)

            def attention(s, par, k, part_, first, last):
                if part_ == 0 and k % 2 == 0:
                    if k >= 2 and not last:
                        queries(s, k // 2 - 1)
                    elif k == 0 and not first:
                        queries(s - 1, 3)
                elif part_ == 1:
                    if k >= T_LAG and not last:
                        exp_t(s, k - T_LAG)
                    elif k < T_LAG and not first:
                        exp_t(s - 1, k - T_LAG + PAIRS)

            def moe(g, first, ahead):
                for n in range(CHUNKS):
                    act.wait_ge(hid_ps, CHUNKS * g + n + 1)
                    need(act, hid_split, CHUNKS * g + n - 3)
                    a_(hid[:, n % 4, :], psA[:, n % 2, :], ACT.Relu, bias=col("b1", n)).then_inc(hid_ready, 1)
                    if high_on_act(n):
                        act.wait_ge(hid_ready, CHUNKS * g + n + 1)
                        need(act, y_ps, CHUNKS * g + n - 3)
                        a_(hidh[:, n % 4, :], hid[:, n % 4, :], ACT.Copy).then_inc(hid_high, 1)
                    if first and n in (0, 1, 2, 3):
                        weights_high(n + 4)
                    if first and n == 5:
                        norm_gT(0)
                    if n % FC == GATE_AT % FC:
                        e = (n - GATE_AT) // FC
                        if e >= 0:
                            gate_rows(g, e)
                        elif not first:
                            gate_rows(g - 1, e + E)
                    if ahead and n == NORM["hT"]:
                        norm_hT(g + 1)
                    if ahead and n == NORM["exp"]:
                        norm_exp(g + 1)
                    if ahead and n == NORM["gT"]:
                        norm_gT(g + 1)
                    if not ahead:
                        for step in ("xT", "gelu_a", "gelu_b", "aT", "kT", "qT"):
                            if n == FIRST[step]:
                                pre(0, 0, step)

            moe(0, True, True)
            with act.Fori(1, BLOCKS - 1) as g:
                moe(g, False, True)
            moe(BLOCKS - 1, False, False)
            gate_rows(BLOCKS - 1, E - 1)

            PRE = [(3, "xT"), (4, "gelu_a"), (5, "gelu_b"), (14, "aT"), (20, "kT"), (23, "qT")]
            POST = [(0, "ctx_a"), (11, "ctx_b"), (17, "fT"), (17, "gelu_a"), (18, "gelu_b")]
            sequences(act, None, PRE, POST, pre, post, attention)

        @block.vector
        def _(dve):
            v_ = nc.vector
            chain = Chain(dve, dve_step, "dve", need)

            def layer_stats(src, st, out_mv, count, done):
                for t in range(count):
                    chain.step(v_.bn_stats(st[:, t, :], src(t)))
                apart(dve, chain.sem, chain.base + chain.n)
                for t in range(count):
                    ins = v_.bn_aggr(out_mv[:, t, :], st[:, t, :])
                    if t < count - 1:
                        chain.step(ins)
                ins.then_inc(done, 1)

            def layer_norm(src, mv_, rs, dst, count, done):
                for t in range(count):
                    ins = v_.tensor_scalar(dst(t), src(t), mv_[:, t, 0:1], rs[:, t:t + 1], ALU.subtract, ALU.mult)
                    if t < count - 1:
                        chain.step(ins)
                ins.then_inc(done, 1)

            def norm_stats(a):
                if isinstance(a, int) and a == 0:
                    dve.wait_ge(x_in0, 16)
                else:
                    dve.wait_ge(x_in, 48)
                layer_stats(lambda t: X[:, BTILES * a + t, :], stats, mv, BTILES, stat_ready)

            def norm_normed(a):
                dve.wait_ge(rstd_ready, a + 1)
                need(dve, nT_ps, a)
                layer_norm(lambda t: X[:, BTILES * a + t, :], mv, rstd, lambda t: normed[:, t, :], BTILES, normed_ready)

            def norm_tstats(a):
                dve.wait_ge(hT_ready, a + 1)
                layer_stats(lambda j: hT[:, j * T:(j + 1) * T], tstats, tmv, 2, tstat_ready)

            def norm_h2(a):
                dve.wait_ge(tscale_ready, a + 1)
                need(dve, logits_ps, a)
                for j in range(2):
                    ins = v_.tensor_scalar(h2[:, j * T:(j + 1) * T], hT[:, j * T:(j + 1) * T], tscale[:, j:j + 1],
                                           tshift[:, j:j + 1], ALU.mult, ALU.add)
                    if j == 0:
                        chain.step(ins)
                ins.then_inc(h2_ready, 1)
                dve.wait_ge(h2_ready, a + 1)
                chain.link(v_.tensor_copy(hh[:, a, :], h2[:, :]))
                v_.tensor_tensor(hl[:, a, :], h2[:, :], hh[:, a, :].bitcast(F32), ALU.subtract).then_inc(hsplit, 1)

            def norm_shift(a):
                dve.wait_ge(logits_ps, a + 1)
                lg = psD[:, 0, 0:BTILES * E].rearrange("p (t e) -> p t e", t=BTILES)
                chain.link(v_.tensor_reduce(lmax[:, :], lg, AX_X, ALU.max))
                v_.tensor_tensor(probs[:, :, :], lg, lmax[:, :].unsqueeze(2).to_broadcast([P, BTILES, E]),
                                 ALU.subtract).then_inc(shifted, 1)

            def norm_gates(a, at):
                wide = [P, BTILES, E]
                pj = probs[:, :, :].unsqueeze(2).to_broadcast([P, BTILES, E, E])
                pe_ = probs[:, :, :].unsqueeze(3).to_broadcast([P, BTILES, E, E])
                if at == 0:
                    dve.wait_ge(exps, a + 1)
                    chain.link(v_.tensor_reduce(psums[:, :], probs[:, :, :], AX_X, ALU.add))
                    chain.link(v_.reciprocal(psums[:, :], psums[:, :]))
                    chain.link(v_.tensor_tensor(probs[:, :, :], probs[:, :, :],
                                                psums[:, :].unsqueeze(2).to_broadcast(wide), ALU.mult))
                elif at == 1:
                    if isinstance(a, int) and a == 0:
                        dve.wait_ge(const_ready, 2)
                    chain.step(v_.tensor_tensor(above[:, :, :, :], pj, pe_, ALU.is_gt))
                    chain.link(v_.tensor_tensor(equal[:, :, :, :], pj, pe_, ALU.is_equal))
                elif at == 2:
                    chain.link(v_.tensor_tensor(equal[:, :, :, :], equal[:, :, :, :],
                                                before[:, :, :].unsqueeze(1).to_broadcast([P, BTILES, E, E]), ALU.mult))
                    chain.link(v_.tensor_tensor(above[:, :, :, :], above[:, :, :, :], equal[:, :, :, :], ALU.add))
                elif at == 3:
                    chain.link(v_.tensor_reduce(rank[:, :, :], above[:, :, :, :], AX_X, ALU.add))
                    chain.link(v_.scalar_tensor_tensor(out=gates[:, :, :], in0=rank[:, :, :], scalar=2.0,
                                                       in1=probs[:, :, :], op0=ALU.is_lt, op1=ALU.mult))
                elif at == 4:
                    chain.link(v_.tensor_reduce(psums[:, :], gates[:, :, :], AX_X, ALU.add))
                    chain.link(v_.reciprocal(psums[:, :], psums[:, :]))
                    chain.link(v_.tensor_tensor(gates[:, :, :], gates[:, :, :],
                                                psums[:, :].unsqueeze(2).to_broadcast(wide), ALU.mult))
                else:
                    k = at - 5
                    ins = v_.tensor_copy(gparts[:, :, k * E:(k + 1) * E], gates[:, :, :])
                    if k < 2:
                        chain.link(ins)
                        chain.link(v_.tensor_tensor(gates[:, :, :], gates[:, :, :], gparts[:, :, k * E:(k + 1) * E],
                                                    ALU.subtract))
                    else:
                        ins.then_inc(gparts_ready, 1)

            dve.wait_ge(ang_in, 16)
            magic = 12582912.0
            chain.link(v_.tensor_scalar(trig[:, 0, :], ang[:, 0:16], 1.0 / (2 * PI), magic, ALU.mult, ALU.add))
            chain.link(v_.tensor_scalar(trig[:, 0, :], trig[:, 0, :], magic, None, ALU.subtract))
            chain.link(v_.scalar_tensor_tensor(out=trig[:, 1, :], in0=trig[:, 0, :], scalar=-6.28125, in1=ang[:, 0:16],
                                               op0=ALU.mult, op1=ALU.add))
            chain.link(v_.scalar_tensor_tensor(out=trig[:, 1, :], in0=trig[:, 0, :], scalar=-(2 * PI - 6.28125),
                                               in1=trig[:, 1, :], op0=ALU.mult, op1=ALU.add))
            chain.link(v_.tensor_scalar(trig[:, 2, :], trig[:, 1, :], 3.1415925, -3.1415925, ALU.min, ALU.max))
            chain.link(v_.tensor_scalar(trig[:, 0, :], trig[:, 1, :], PI / 2, -2 * PI, ALU.is_gt, ALU.mult))
            chain.link(v_.tensor_tensor(trig[:, 3, :], trig[:, 1, :], trig[:, 0, :], ALU.add))
            chain.link(v_.tensor_scalar(trig[:, 3, :], trig[:, 3, :], PI / 2, 3.1415925, ALU.add, ALU.min))
            v_.tensor_scalar(trig[:, 3, :], trig[:, 3, :], -3.1415925, None, ALU.max).then_inc(trig_in, 1)
            dve.wait_ge(const_ready, 1)
            dve.wait_ge(ids_in, 16)
            chain.link(v_.tensor_copy(idf[:, :], idall[:, :]))
            chain.step(v_.tensor_scalar(onehot[:, :], idf[:, 0:8], rowno[0:SUBJECTS, :], None, ALU.is_equal))
            v_.tensor_scalar(onehot_x[:, :], idf[0:E, 8:16], rowno[0:E, :], None, ALU.is_equal).then_inc(cond_dve, 1)
            dve.wait_ge(cond_pe, 1)
            chain.step(v_.tensor_copy(pcol[:, :], psD[:, 0, 0:NROWS]))
            dve.wait_ge(cond_pe, 2)
            v_.tensor_copy(cond_a[0:SE, :], psD[0:SE, 1, 0:8]).then_inc(cond_dve, 1)
            norm_stats(0)
            dve.wait_ge(trig_ready, 1)
            for k in range(2):
                sin_, cos_ = trig[:, 4, 8 * k:8 * k + 8], trig[:, 5, 8 * k:8 * k + 8]
                chain.step(v_.tensor_copy(rot_s[:, :, 2 * k], sin_))
                chain.step(v_.tensor_scalar(rot_s[:, :, 2 * k + 1], sin_, -1.0, None, ALU.mult))
                chain.step(v_.tensor_copy(rot_c[:, :, 2 * k], cos_))
                chain.step(v_.tensor_copy(rot_c[:, :, 2 * k + 1], cos_))
            norm_normed(0)
            dve.wait_ge(cond_pe, 6)
            chain.settle()
            chain.step(v_.tensor_scalar(bet[:, :], psD[:, 1, 160:168], col("sty_b2", 1), None, ALU.add))
            chain.link(v_.tensor_scalar(sp_t[:, 0, :], psD[:, 1, 152:160], col("sty_b2"), None, ALU.add))
            chain.link(v_.tensor_scalar(sp_t[:, 1, :], sp_t[:, 0, :], -1.0, None, ALU.mult))
            v_.tensor_tensor(sp_t[:, 1, :], sp_t[:, 0, :], sp_t[:, 1, :], ALU.max).then_inc(cond_dve, 1)
            norm_tstats(0)
            dve.wait_ge(cond_act, 4)
            u, lw, w1, q = (sp_t[:, i, :] for i in (2, 3, 4, 5))
            chain.link(v_.tensor_scalar(w1, u, 1.0, -1.0, ALU.add, ALU.add))
            chain.link(v_.tensor_scalar(q, w1, 1e-30, None, ALU.max))
            chain.link(v_.reciprocal(q, q))
            chain.link(v_.tensor_tensor(q, q, u, ALU.mult))
            chain.link(v_.tensor_tensor(q, q, lw, ALU.mult))
            chain.link(v_.scalar_tensor_tensor(out=w1, in0=w1, scalar=0.0, in1=u, op0=ALU.is_equal, op1=ALU.mult))
            chain.link(v_.tensor_tensor(q, q, w1, ALU.add))
            chain.link(v_.scalar_tensor_tensor(out=q, in0=sp_t[:, 0, :], scalar=0.0, in1=q, op0=ALU.max, op1=ALU.add))
            v_.tensor_scalar(gam[:, :], q, 1e-8, None, ALU.add).then_inc(cond_dve, 1)
            norm_h2(0)
            dve.wait_ge(cond_pe, 7)
            chain.step(v_.tensor_copy(bi_col[:, :, :], psC[:, 0, 0:32].rearrange("p (f s) -> p f s", f=FC)))
            norm_shift(0)

            def split_hidden(g, n):
                dve.wait_ge(hid_ready, CHUNKS * g + n + 1)
                if high_on_act(n):
                    dve.wait_ge(hid_high, HIGHS * g + sum(map(high_on_act, range(n + 1))))
                else:
                    need(dve, y_ps, CHUNKS * g + n - 3)
                    chain.link(v_.tensor_copy(hidh[:, n % 4, :], hid[:, n % 4, :]))
                v_.tensor_tensor(hidl[:, n % 4, :], hid[:, n % 4, :], hidh[:, n % 4, :].bitcast(F32), ALU.subtract)\
                    .then_inc(hid_split, 1)

            def gated(g, e):
                dve.wait_ge(y_ps, CHUNKS * g + FC * (e + 1))
                dve.wait_ge(gb_ready, 8 * g + e + 1)
                need(dve, y_sum, 7 * g + (max(e - 2, 1) if e >= 2 else e - 1))
                v_.scalar_tensor_tensor(out=part[:, e % 2, :], in0=psB[:, e % 2, :], scalar=col("b2", e),
                                        in1=gb[:, e % 2, :], op0=ALU.add, op1=ALU.mult).then_inc(part_ready, 1)

            def add_sum(g):
                dve.wait_ge(yT_ps, g + 1)
                xs = X[:, bass.ds(BTILES * g, BTILES), :]
                v_.tensor_tensor(xs, psC[:, 1, :].rearrange("p (t d) -> p t d", t=BTILES), xs, ALU.add)\
                    .then_inc(x1_ready, 1)

            def pre(n, par, step):
                if step == "xcopy":
                    dve.wait_ge(rotated, 1 if isinstance(n, int) and n < 2 else BLOCKS)
                    need(dve, x3_ready, n)
                    v_.tensor_copy(pr_n[:, :, :], X[:, bass.ds(2 * n, 2), :]).then_inc(xcopy_ready, 1)
                elif step == "stats":
                    dve.wait_ge(mlp_ps, n + 1)
                    dve.wait_ge(xbo_ready, n + 1)
                    chain.link(v_.tensor_tensor(pr_r[:, :, :], psD[:, 1, 0:T].rearrange("p (j d) -> p j d", j=2),
                                                pr_b[:, :, :], ALU.add))
                    layer_stats(lambda j: pr_r[:, j, :], pr_st, pr_mv, 2, mstat)
                elif step == "norm":
                    dve.wait_ge(mrstd, n + 1)
                    layer_norm(lambda j: pr_r[:, j, :], pr_mv, pr_rs, lambda j: pr_n[:, j, :], 2, mnorm)
                elif step == "affine":
                    dve.wait_ge(mnorm, n + 1)
                    dve.wait_ge(mlp_in[par], mlp_count(n, par))
                    chain.link(v_.tensor_tensor(pr_n[:, :, :], pr_n[:, :, :],
                                                mrow[par][:, D:2 * D].unsqueeze(1).to_broadcast([P, 2, D]), ALU.mult))
                    v_.tensor_tensor(X[:, bass.ds(2 * n, 2), :], pr_n[:, :, :],
                                     mrow[par][:, 2 * D:3 * D].unsqueeze(1).to_broadcast([P, 2, D]), ALU.add)\
                        .then_inc(x3_ready, 1)
                elif step == "astats":
                    apart(dve, x3_ready, n + 1)
                    layer_stats(lambda j: X[:, 2 * n + j, :], pr_st, pr_mv, 2, astat)
                elif step == "anorm":
                    dve.wait_ge(arstd, n + 1)
                    layer_norm(lambda j: X[:, 2 * n + j, :], pr_mv, pr_rs, lambda j: pr_r[:, j, :], 2, anorm)
                elif step == "qkv":
                    dve.wait_ge(qkv_ps, n + 1)
                    dve.wait_ge(values_clear, par + 1)
                    if isinstance(n, int) and n == 0:
                        dve.wait_ge(att_in, 48)
                    need(dve, pv_ps, 8 * (n - 1))
                    for j in range(2):
                        ps = psD[:, 1 - j, :]
                        chain.step(v_.tensor_tensor(qk[:, j].rearrange("p q h d -> p (q h d)"), ps[:, 0:2 * D],
                                                    arow[:, 0:2 * D], ALU.add))
                        for q in range(2):
                            c = 2 * D + 64 * q
                            base = vm[par][:, j, 8 * q:8 * (q + 1), :].rearrange("p h c -> p (h c)")
                            diag = diagonal(base)
                            ins = v_.tensor_tensor(diag, ps[:, c:c + 64].rearrange("p (h d) -> p h d", h=8),
                                                   arow[:, c:c + 64].rearrange("p (h d) -> p h d", h=8), ALU.add)
                            if (j, q) != (1, 1):
                                chain.step(ins)
                    ins.then_inc(qkv_ready, 1)
                elif step == "stack":
                    dve.wait_ge(qkv_ready, n + 1)
                    dve.wait_ge(stack_clear, par + 1)
                    need(dve, qmT_ps, 4 * (n - 1))
                    st = stack[par]
                    hi = st[:, :, :, :, 0:DH].rearrange("p j q h c -> p (j q h) c")
                    chain.link(v_.tensor_copy(hi, qk[:, :, :, :, :].rearrange("p j q h d -> p (j q h) d")))
                    for q, lo, dup in ((0, DH, 2 * DH), (1, 2 * DH, DH)):
                        h_ = st[:, :, q, :, 0:DH].bitcast(F32)
                        chain.step(v_.tensor_tensor(st[:, :, q, :, lo:lo + DH], qk[:, :, q], h_, ALU.subtract))
                        ins = v_.tensor_copy(st[:, :, q, :, dup:dup + DH], h_)
                        if q == 0:
                            chain.step(ins)
                    ins.then_inc(stack_ready, 1)

            def post(m, step):
                if step == "ctx":
                    dve.wait_ge(ctx_copied, 2 * (m + 1))
                    chain.link(v_.reciprocal(rden[:, :], ctx_sb[:, T:2 * T]))
                    v_.tensor_tensor(ctxT[:, :], ctx_sb[:, 0:T], rden[:, :], ALU.mult).then_inc(ctx_ready, 1)
                elif step == "x4":
                    dve.wait_ge(wo_ps, m + 1)
                    dve.wait_ge(xb4_ready, m + 1)
                    chain.link(v_.tensor_tensor(po_x[:, :, :], psC[:, 1, 0:T].rearrange("p (j d) -> p j d", j=2),
                                                po_b[:, :, :], ALU.add))
                    layer_stats(lambda j: po_x[:, j, :], po_st, po_mv, 2, fstat)
                elif step == "norm":
                    dve.wait_ge(frstd, m + 1)
                    layer_norm(lambda j: po_x[:, j, :], po_mv, po_rs, lambda j: po_n[:, j, :], 2, fnorm)
                elif step == "out":
                    dve.wait_ge(ffn_ps, m + 1)
                    dve.wait_ge(diff_ready, m + 1)
                    chain.link(v_.tensor_tensor(po_d[:, :, :], psC[:, 1, 0:T].rearrange("p (j d) -> p j d", j=2),
                                                po_d[:, :, :], ALU.add))
                    xs = X[:, bass.ds(2 * m, 2), :]
                    v_.scalar_tensor_tensor(out=xs, in0=po_d[:, :, :], scalar=ang[:, bass.ds(16 + m, 1)], in1=xs,
                                            op0=ALU.mult, op1=ALU.add).then_inc(out_ready, 1)

            def attention(s, par, k, part_, first, last):
                if first and (k, part_) == (1, 2):
                    add_sum(BLOCKS - 1)
                if part_ != 0 or last:
                    return
                dve.wait_ge(s_ps, 8 * s + k + 1)
                chain.step(v_.tensor_reduce(rmax[:, 1, 2 * k:2 * k + 2], psA[:, :, 0:T], AX_X, ALU.max))
                v_.tensor_reduce(rmax[:, 0, 2 * k:2 * k + 2], psA[:, :, T:T + P], AX_X, ALU.max)\
                    .then_inc(max_ready, 1)
                if k % 2:
                    dve.wait_ge(max_ready, 8 * s + k + 1)
                    hs = slice(2 * k - 2, 2 * k + 2)
                    mhi = stack[par][:, :, 0, hs, 24]
                    chain.link(v_.tensor_copy(mhi, rmax[:, :, hs]))
                    v_.tensor_tensor(stack[par][:, :, 0, hs, 25], rmax[:, :, hs], mhi.bitcast(F32), ALU.subtract)\
                        .then_inc(m_ready, 1)

            def moe(g, first, ahead):
                for n in range(CHUNKS):
                    split_hidden(g, n)
                    if n % FC == OUTPUT_AT % FC:
                        e = (n - OUTPUT_AT) // FC
                        if e >= 0:
                            gated(g, e)
                        elif not first:
                            gated(g - 1, e + E)
                    if n == LAST_X1 and not first:
                        add_sum(g - 1)
                    if first and n < 4:
                        norm_gates(0, 2 * n)
                        norm_gates(0, 2 * n + 1)
                    if ahead:
                        for name, fn in (("stats", norm_stats), ("normed", norm_normed), ("tstats", norm_tstats),
                                         ("h2", norm_h2), ("shift", norm_shift)):
                            if n == NORM[name]:
                                fn(g + 1)
                        if 0 <= n - NORM["gates"] < GATE_PARTS:
                            norm_gates(g + 1, n - NORM["gates"])
                    else:
                        for step in ("xcopy", "stats", "norm", "affine", "astats", "anorm", "qkv", "stack"):
                            if n == FIRST[step]:
                                pre(0, 0, step)

            moe(0, True, True)
            per, start = STEPS_OF_BLOCK["dve"], chain.base + chain.n
            with dve.Fori(1, BLOCKS - 1) as g:
                chain.enter(start + per * (g - 1))
                moe(g, False, True)
                assert chain.n == per, chain.n
            chain.enter(start + per * (BLOCKS - 2))
            moe(BLOCKS - 1, False, False)
            gated(BLOCKS - 1, E - 1)

            PRE = [(0, "xcopy"), (5, "stats"), (8, "norm"), (8, "affine"), (8, "astats"), (11, "anorm"),
                   (17, "qkv"), (17, "stack")]
            POST = [(11, "ctx"), (13, "x4"), (14, "norm"), (21, "out")]
            sequences(dve, chain, PRE, POST, pre, post, attention)


def kernel(**inputs):
    import numpy as np
    import concourse.bacc as bacc
    from concourse.bass_utils import run_bass_kernel_spmd

    def get(name):
        return np.asarray(inputs[name])

    l0, l2, l3 = ((lambda n, p=p: get(p + n)) for p in ("L0_cond_", "L2_cond_", "L3_cond_"))

    def experts(w1, w2):
        w2 = w2.reshape(E, FC, P, D).transpose(0, 2, 1, 3).reshape(E, P, FC * D)
        return np.concatenate([w1, w2], axis=2)

    def side_by_side(*matrices):
        place = np.zeros((P, COND_COLS), np.float32)
        for m, (r, c, w) in zip(matrices, COND_PLACES):
            place[0:r, c:c + w] = m
        return place

    arrays = {
        "x": get("x"),
        "ids": np.concatenate([get("itok_B_6_14"), get("itok_B_0_7")]).reshape(1, 16),
        "angles": np.concatenate([get("condB_theta"), get("condB_phi"), get("condB_gatescore")]).reshape(1, 24),
        "rows": np.concatenate([a.reshape(-1, P) for a in (
            l0("exp_b1"), l0("exp_b2"), l0("ln_g"), l0("ln_b"), l3("b1"), l0("hyp_b1"), l0("hyp_b2"), l0("sty_b2"),
            l3("gamma1"), l3("beta1"), l3("gamma2"), l3("beta2"))]),
        "sty_b1": l0("sty_b1").reshape(SE, 1),
        "cond_w": side_by_side(l0("subj_emb"), l0("hyp_w1"), l0("hyp_w2"), l0("sty_w1"), l0("sty_w2"), l0("router_w")),
        "moe_w": experts(l0("exp_w1"), l0("exp_w2")),
        "mlp_w": experts(l2("Wi"), l2("Wo")),
        "mlp_rows": np.concatenate([l2("bo"), l2("gamma"), l2("beta")], axis=1),
        "mlp_bi": l2("bi"),
        "att_w": np.concatenate([l3("Wq"), l3("Wk"), l3("Wv"), np.roll(l3("Wo"), P // 2, axis=0), l3("W1"),
                                 l3("W2").reshape(FC, P, D).transpose(1, 0, 2).reshape(P, FC * D)], axis=1),
        "att_rows": np.concatenate([l3("bq"), l3("bk"), l3("bv"), l3("bo"), l3("b2")]).reshape(1, 640),
    }
    arrays = {f"in_{n}": np.ascontiguousarray(a) for n, a in arrays.items()}
    nc = bacc.Bacc("TRN2", target_bir_lowering=False, num_devices=1)
    aps = [nc.dram_tensor(n, a.shape, mybir.dt.from_np(a.dtype), kind="ExternalInput").ap() for n, a in arrays.items()]
    out = nc.dram_tensor("out", (SEQS, T, D), F32, kind="ExternalOutput").ap()
    conditioned_stack(nc, *aps, out)
    r = run_bass_kernel_spmd(nc, [arrays], core_ids=[0])
    return r.results[0]["out"]
```
